# Optimizing a Trainium2 kernel written in Bass

```python
import numpy as np
import jax
import jax.numpy as jnp

def _softmax(x, axis=-1):
    return jax.nn.softmax(x, axis=axis)

def _gelu(x):
    return jax.nn.gelu(x, approximate=True)

def _silu(x):
    return jax.nn.silu(x)

def _sigmoid(x):
    return jax.nn.sigmoid(x)

def _layernorm(x, axis=-1, eps=1e-05):
    m = jnp.mean(x, axis=axis, keepdims=True)
    v = jnp.var(x, axis=axis, keepdims=True)
    return (x - m) / jnp.sqrt(v + eps)

def _scatter_add(tgt, idx, src, axis=0):
    return tgt.at[idx].add(src)

def _segment_sum(src, seg, n):
    return jax.ops.segment_sum(src, seg, n)
kernel_name = 'mk_macaron_d2_jaxref_r8_a0a329'

def setup_inputs(seed: int=0):
    np.random.seed(seed)
    _w = jnp.asarray

    def _L0_attn_setup():
        import jax, jax.numpy as jnp
        import numpy as np
        B, T, DIM, H = (2, 256, 128, 16)
        HD = DIM // H

        def _custom_softmax(a):
            a = jnp.clip(a, -100.0, 100.0)
            m = jnp.max(a, axis=-1, keepdims=True)
            e = jnp.exp(a - m)
            p = e / (jnp.sum(e, axis=-1, keepdims=True) + 1e-06)
            p = p + 1e-08
            return p / jnp.sum(p, axis=-1, keepdims=True)
        key = jax.random.key(seed)
        k1, k2, k3 = jax.random.split(key, 3)
        x = jax.random.normal(k1, (B, T, DIM), dtype=jnp.float32)
        w_qkv = jax.random.normal(k2, (3 * DIM, DIM), dtype=jnp.float32) / np.sqrt(DIM)
        w_proj = jax.random.normal(k3, (DIM, DIM), dtype=jnp.float32) / np.sqrt(DIM)
        return {'x': x, 'w_qkv': w_qkv, 'w_proj': w_proj}
    _L0_attn_in = _L0_attn_setup()

    def _L0_ffn_setup():
        import jax, jax.numpy as jnp
        import numpy as np
        B, T, D = (4, 512, 128)
        E = 8
        TOP_K = 2
        FFN = 384
        HALF = FFN // 2

        def _kaiming_uniform(key, shape, fan_in):
            bound = 1.0 / np.sqrt(fan_in)
            return jax.random.uniform(key, shape, jnp.float32, -bound, bound)
        key = jax.random.key(seed)
        ks = jax.random.split(key, 7)
        x = jax.random.normal(ks[0], (B, T, D), jnp.float32)
        gate_w = _kaiming_uniform(ks[1], (E, D), D) * 0.01
        w_up = _kaiming_uniform(ks[2], (E, FFN, D), D)
        w_down = _kaiming_uniform(ks[3], (E, D, HALF), HALF)
        sg_gate = _kaiming_uniform(ks[4], (HALF, D), D)
        sg_up = _kaiming_uniform(ks[5], (HALF, D), D)
        sg_down = _kaiming_uniform(ks[6], (D, HALF), HALF)
        return {'x': x, 'gate_w': gate_w, 'w_up': w_up, 'w_down': w_down, 'sg_gate': sg_gate, 'sg_up': sg_up, 'sg_down': sg_down}
    _L0_ffn_in = _L0_ffn_setup()

    def _L1_attn_setup():
        import jax, jax.numpy as jnp
        import numpy as np
        NUM_HEADS = 16
        ROPE_BASE = 10000.0
        ROPE_SCALE = 3.0

        def _rope_tables(L, head_dim, dtype):
            theta = 1.0 / ROPE_BASE ** (jnp.arange(0, head_dim, 2, dtype=jnp.float32) / head_dim) * ROPE_SCALE
            ang = jnp.arange(L, dtype=jnp.float32)[:, None] * theta[None, :]
            return (jnp.cos(ang).astype(dtype), jnp.sin(ang).astype(dtype))

        def _apply_rope(t, cos, sin):
            B, H, L, D = t.shape
            tr = t.reshape(B, H, L, D // 2, 2)
            real, imag = (tr[..., 0], tr[..., 1])
            c = cos[None, None, :, :]
            s = sin[None, None, :, :]
            out_real = real * c - imag * s
            out_imag = real * s + imag * c
            return jnp.stack([out_real, out_imag], axis=-1).reshape(B, H, L, D)
        key = jax.random.key(seed)
        k1, k2, k3 = jax.random.split(key, 3)
        B, L, C = (4, 256, 128)
        std = 1.0 / np.sqrt(C)
        x = jax.random.normal(k1, (B, L, C), dtype=jnp.float32)
        w_qkv = jax.random.normal(k2, (C, 3 * C), dtype=jnp.float32) * std
        w_proj = jax.random.normal(k3, (C, C), dtype=jnp.float32) * std
        b_proj = jnp.zeros((C,), dtype=jnp.float32)
        return {'x': x, 'w_qkv': w_qkv, 'w_proj': w_proj, 'b_proj': b_proj}
    _L1_attn_in = _L1_attn_setup()

    def _L1_ffn_setup():
        import jax, jax.numpy as jnp
        import numpy as np
        DIM = 128
        DEPTH = 2
        HEADS = 8
        DIM_HEAD = 64
        WINDOW = 64
        INNER = HEADS * DIM_HEAD
        HID = int(DIM * 4 * 2 / 3)
        B, N = (2, 1024)
        QK_SCALE = 8.0

        def shift_token(t):
            t1, t2 = jnp.split(t, 2, axis=-1)
            t2 = jnp.pad(t2, ((0, 0), (1, 0), (0, 0)))[:, :-1]
            return jnp.concatenate([t1, t2], axis=-1)

        def l2norm(t):
            return t / jnp.clip(jnp.linalg.norm(t, axis=-1, keepdims=True), 1e-12)

        def rotate_half(x):
            x1, x2 = jnp.split(x, 2, axis=-1)
            return jnp.concatenate([-x2, x1], axis=-1)

        def rotary_xpos(q, k):
            n = q.shape[-2]
            half_idx = jnp.arange(0, DIM_HEAD, 2, dtype=jnp.float32)
            inv_freq = 1.0 / 10000.0 ** (half_idx / DIM_HEAD)
            t = jnp.arange(n, dtype=jnp.float32)
            freqs = t[:, None] * inv_freq[None, :]
            freqs = jnp.concatenate([freqs, freqs], axis=-1)
            base = (half_idx + 0.4 * DIM_HEAD) / (1.4 * DIM_HEAD)
            power = (t - n // 2) / float(WINDOW // 2)
            scale = base[None, :] ** power[:, None]
            scale = jnp.concatenate([scale, scale], axis=-1)
            cos, sin = (jnp.cos(freqs), jnp.sin(freqs))
            q = q * cos * scale + rotate_half(q) * sin * scale
            k = k * cos / scale + rotate_half(k) * sin / scale
            return (q, k)

        def local_attention(q, k, v):
            b, h, n, d = q.shape
            w = n // WINDOW
            bq = q.reshape(b, h, w, WINDOW, d) * QK_SCALE
            bk = k.reshape(b, h, w, WINDOW, d)
            bv = v.reshape(b, h, w, WINDOW, d)

            def look_around(t):
                p = jnp.pad(t, ((0, 0), (0, 0), (1, 0), (0, 0), (0, 0)))
                return jnp.concatenate([p[:, :, :w], p[:, :, 1:]], axis=3)
            bk, bv = (look_around(bk), look_around(bv))
            bt = jnp.arange(n).reshape(w, WINDOW)
            btp = jnp.pad(bt, ((1, 0), (0, 0)), constant_values=-1)
            btk = jnp.concatenate([btp[:w], btp[1:]], axis=1)
            sim = jnp.einsum('bhwid,bhwjd->bhwij', bq, bk)
            i = bt[:, :, None]
            j = btk[:, None, :]
            mask = (i < j) | (i > j + WINDOW) | (j == -1)
            sim = jnp.where(mask, -jnp.finfo(sim.dtype).max, sim)
            attn = jax.nn.softmax(sim, axis=-1)
            out = jnp.einsum('bhwij,bhwjd->bhwid', attn, bv)
            return out.reshape(b, h, n, d)

        def _layer(x, wqkv, qs, ksc, wo, lg, lb, w1, b1, w2, b2):
            b, n, _ = x.shape
            h = shift_token(x)
            qkv = h @ wqkv
            q, k, v = jnp.split(qkv, 3, axis=-1)
            to_heads = lambda t: t.reshape(b, n, HEADS, DIM_HEAD).transpose(0, 2, 1, 3)
            q, k, v = (to_heads(q), to_heads(k), to_heads(v))
            q = l2norm(q) * qs
            k = l2norm(k) * ksc
            q, k = rotary_xpos(q, k)
            o = local_attention(q, k, v)
            o = o.transpose(0, 2, 1, 3).reshape(b, n, INNER)
            x = x + o @ wo
            h = shift_token(x)
            mu = h.mean(-1, keepdims=True)
            var = h.var(-1, keepdims=True)
            h = (h - mu) / jnp.sqrt(var + 1e-05) * lg + lb
            h = h @ w1 + b1
            a, g = jnp.split(h, 2, axis=-1)
            h = a * jax.nn.gelu(g, approximate=False)
            x = x + h @ w2 + b2
            return x
        key = jax.random.key(seed)
        ks = jax.random.split(key, 6)
        return {'x': jax.random.normal(ks[0], (B, N, DIM), jnp.float32), 'wqkv': jax.random.normal(ks[1], (DEPTH, DIM, 3 * INNER), jnp.float32) * 0.02, 'q_scale': jnp.ones((DEPTH, DIM_HEAD), jnp.float32), 'k_scale': jnp.ones((DEPTH, DIM_HEAD), jnp.float32), 'wo': jax.random.normal(ks[2], (DEPTH, INNER, DIM), jnp.float32) * 0.02, 'ln_g': jnp.ones((DEPTH, DIM), jnp.float32), 'ln_b': jnp.zeros((DEPTH, DIM), jnp.float32), 'w1': jax.random.normal(ks[3], (DEPTH, DIM, 2 * HID), jnp.float32) * 0.02, 'b1': jnp.zeros((DEPTH, 2 * HID), jnp.float32), 'w2': jax.random.normal(ks[4], (DEPTH, HID, DIM), jnp.float32) * 0.02, 'b2': jnp.zeros((DEPTH, DIM), jnp.float32)}
    _L1_ffn_in = _L1_ffn_setup()
    _d = {'L0_attn_x': _L0_attn_in['x'], 'L0_attn_w_qkv': _L0_attn_in['w_qkv'], 'L0_attn_w_proj': _L0_attn_in['w_proj'], 'L0_ffn_gate_w': _L0_ffn_in['gate_w'], 'L0_ffn_w_up': _L0_ffn_in['w_up'], 'L0_ffn_w_down': _L0_ffn_in['w_down'], 'L0_ffn_sg_gate': _L0_ffn_in['sg_gate'], 'L0_ffn_sg_up': _L0_ffn_in['sg_up'], 'L0_ffn_sg_down': _L0_ffn_in['sg_down'], 'L1_attn_w_qkv': _L1_attn_in['w_qkv'], 'L1_attn_w_proj': _L1_attn_in['w_proj'], 'L1_attn_b_proj': _L1_attn_in['b_proj'], 'L1_ffn_wqkv': _L1_ffn_in['wqkv'], 'L1_ffn_q_scale': _L1_ffn_in['q_scale'], 'L1_ffn_k_scale': _L1_ffn_in['k_scale'], 'L1_ffn_wo': _L1_ffn_in['wo'], 'L1_ffn_ln_g': _L1_ffn_in['ln_g'], 'L1_ffn_ln_b': _L1_ffn_in['ln_b'], 'L1_ffn_w1': _L1_ffn_in['w1'], 'L1_ffn_b1': _L1_ffn_in['b1'], 'L1_ffn_w2': _L1_ffn_in['w2'], 'L1_ffn_b2': _L1_ffn_in['b2']}
    _x0 = _d['L0_attn_x']
    _d['L0_attn_x'] = jax.random.normal(jax.random.fold_in(jax.random.key(seed), 1), (16, 512, 128), dtype=_x0.dtype)
    del _x0
    return _d

def reference(L0_attn_x, L0_attn_w_qkv, L0_attn_w_proj, L0_ffn_gate_w, L0_ffn_w_up, L0_ffn_w_down, L0_ffn_sg_gate, L0_ffn_sg_up, L0_ffn_sg_down, L1_attn_w_qkv, L1_attn_w_proj, L1_attn_b_proj, L1_ffn_wqkv, L1_ffn_q_scale, L1_ffn_k_scale, L1_ffn_wo, L1_ffn_ln_g, L1_ffn_ln_b, L1_ffn_w1, L1_ffn_b1, L1_ffn_w2, L1_ffn_b2):

    def _L0_attn_ref(x, w_qkv, w_proj):
        import jax, jax.numpy as jnp
        import numpy as np
        B, T, DIM, H = (2, 256, 128, 16)
        HD = DIM // H

        def _custom_softmax(a):
            a = jnp.clip(a, -100.0, 100.0)
            m = jnp.max(a, axis=-1, keepdims=True)
            e = jnp.exp(a - m)
            p = e / (jnp.sum(e, axis=-1, keepdims=True) + 1e-06)
            p = p + 1e-08
            return p / jnp.sum(p, axis=-1, keepdims=True)
        b, t, c = x.shape
        scale = HD ** (-0.5)
        qkv = jnp.einsum('btc,oc->bto', x, w_qkv)
        qkv = qkv.reshape(b, t, 3, H, HD)
        q = jnp.transpose(qkv[:, :, 0], (0, 2, 1, 3))
        k = jnp.transpose(qkv[:, :, 1], (0, 2, 1, 3))
        v = jnp.transpose(qkv[:, :, 2], (0, 2, 1, 3))
        attn = jnp.einsum('bhqd,bhkd->bhqk', q, k) * scale
        causal = jnp.tril(jnp.ones((t, t), dtype=bool))
        attn = jnp.where(causal, attn, -jnp.inf)
        attn = _custom_softmax(attn)
        out = jnp.einsum('bhqk,bhkd->bhqd', attn, v)
        out = jnp.transpose(out, (0, 2, 1, 3)).reshape(b, t, c)
        return jnp.einsum('btc,oc->bto', out, w_proj)

    def _L0_ffn_ref(x, gate_w, w_up, w_down, sg_gate, sg_up, sg_down):
        import jax, jax.numpy as jnp
        import numpy as np
        B, T, D = (4, 512, 128)
        E = 8
        TOP_K = 2
        FFN = 384
        HALF = FFN // 2

        def _kaiming_uniform(key, shape, fan_in):
            bound = 1.0 / np.sqrt(fan_in)
            return jax.random.uniform(key, shape, jnp.float32, -bound, bound)
        b, t, d = x.shape
        xf = x.reshape(b * t, d)
        N = xf.shape[0]
        logits = xf @ gate_w.T
        topk_logits, topk_idx = jax.lax.top_k(logits, TOP_K)
        topk_w = jax.nn.softmax(topk_logits.astype(jnp.float32), axis=-1).astype(x.dtype)
        comb = jnp.zeros((N, E), x.dtype).at[jnp.arange(N)[:, None], topk_idx].add(topk_w)
        wg = w_up[:, :HALF, :]
        wu = w_up[:, HALF:, :]
        out = jnp.zeros_like(xf)
        for e in range(E):
            g = xf @ wg[e].T
            u = xf @ wu[e].T
            y = jax.nn.silu(g) * u @ w_down[e].T
            out = out + comb[:, e:e + 1] * y
        shared = jax.nn.silu(xf @ sg_gate.T) * (xf @ sg_up.T) @ sg_down.T
        return (shared + out).reshape(b, t, d)

    def _L1_attn_ref(x, w_qkv, w_proj, b_proj):
        import jax, jax.numpy as jnp
        import numpy as np
        NUM_HEADS = 16
        ROPE_BASE = 10000.0
        ROPE_SCALE = 3.0

        def _rope_tables(L, head_dim, dtype):
            theta = 1.0 / ROPE_BASE ** (jnp.arange(0, head_dim, 2, dtype=jnp.float32) / head_dim) * ROPE_SCALE
            ang = jnp.arange(L, dtype=jnp.float32)[:, None] * theta[None, :]
            return (jnp.cos(ang).astype(dtype), jnp.sin(ang).astype(dtype))

        def _apply_rope(t, cos, sin):
            B, H, L, D = t.shape
            tr = t.reshape(B, H, L, D // 2, 2)
            real, imag = (tr[..., 0], tr[..., 1])
            c = cos[None, None, :, :]
            s = sin[None, None, :, :]
            out_real = real * c - imag * s
            out_imag = real * s + imag * c
            return jnp.stack([out_real, out_imag], axis=-1).reshape(B, H, L, D)
        B, L, C = x.shape
        H = NUM_HEADS
        D = C // H
        scale = D ** (-0.5)
        qkv = (x @ w_qkv).reshape(B, L, 3, H, D).transpose(2, 0, 3, 1, 4)
        q, k, v = (qkv[0], qkv[1], qkv[2])
        cos, sin = _rope_tables(L, D, x.dtype)
        q = _apply_rope(q, cos, sin)
        k = _apply_rope(k, cos, sin)
        attn = jnp.einsum('bhqd,bhkd->bhqk', q, k) * scale
        attn = jax.nn.softmax(attn, axis=-1)
        out = jnp.einsum('bhqk,bhkd->bhqd', attn, v)
        out = out.transpose(0, 2, 1, 3).reshape(B, L, C)
        return out @ w_proj + b_proj

    def _L1_ffn_ref(x, wqkv, q_scale, k_scale, wo, ln_g, ln_b, w1, b1, w2, b2):
        import jax, jax.numpy as jnp
        import numpy as np
        DIM = 128
        DEPTH = 2
        HEADS = 8
        DIM_HEAD = 64
        WINDOW = 64
        INNER = HEADS * DIM_HEAD
        HID = int(DIM * 4 * 2 / 3)
        B, N = (2, 1024)
        QK_SCALE = 8.0

        def shift_token(t):
            t1, t2 = jnp.split(t, 2, axis=-1)
            t2 = jnp.pad(t2, ((0, 0), (1, 0), (0, 0)))[:, :-1]
            return jnp.concatenate([t1, t2], axis=-1)

        def l2norm(t):
            return t / jnp.clip(jnp.linalg.norm(t, axis=-1, keepdims=True), 1e-12)

        def rotate_half(x):
            x1, x2 = jnp.split(x, 2, axis=-1)
            return jnp.concatenate([-x2, x1], axis=-1)

        def rotary_xpos(q, k):
            n = q.shape[-2]
            half_idx = jnp.arange(0, DIM_HEAD, 2, dtype=jnp.float32)
            inv_freq = 1.0 / 10000.0 ** (half_idx / DIM_HEAD)
            t = jnp.arange(n, dtype=jnp.float32)
            freqs = t[:, None] * inv_freq[None, :]
            freqs = jnp.concatenate([freqs, freqs], axis=-1)
            base = (half_idx + 0.4 * DIM_HEAD) / (1.4 * DIM_HEAD)
            power = (t - n // 2) / float(WINDOW // 2)
            scale = base[None, :] ** power[:, None]
            scale = jnp.concatenate([scale, scale], axis=-1)
            cos, sin = (jnp.cos(freqs), jnp.sin(freqs))
            q = q * cos * scale + rotate_half(q) * sin * scale
            k = k * cos / scale + rotate_half(k) * sin / scale
            return (q, k)

        def local_attention(q, k, v):
            b, h, n, d = q.shape
            w = n // WINDOW
            bq = q.reshape(b, h, w, WINDOW, d) * QK_SCALE
            bk = k.reshape(b, h, w, WINDOW, d)
            bv = v.reshape(b, h, w, WINDOW, d)

            def look_around(t):
                p = jnp.pad(t, ((0, 0), (0, 0), (1, 0), (0, 0), (0, 0)))
                return jnp.concatenate([p[:, :, :w], p[:, :, 1:]], axis=3)
            bk, bv = (look_around(bk), look_around(bv))
            bt = jnp.arange(n).reshape(w, WINDOW)
            btp = jnp.pad(bt, ((1, 0), (0, 0)), constant_values=-1)
            btk = jnp.concatenate([btp[:w], btp[1:]], axis=1)
            sim = jnp.einsum('bhwid,bhwjd->bhwij', bq, bk)
            i = bt[:, :, None]
            j = btk[:, None, :]
            mask = (i < j) | (i > j + WINDOW) | (j == -1)
            sim = jnp.where(mask, -jnp.finfo(sim.dtype).max, sim)
            attn = jax.nn.softmax(sim, axis=-1)
            out = jnp.einsum('bhwij,bhwjd->bhwid', attn, bv)
            return out.reshape(b, h, n, d)

        def _layer(x, wqkv, qs, ksc, wo, lg, lb, w1, b1, w2, b2):
            b, n, _ = x.shape
            h = shift_token(x)
            qkv = h @ wqkv
            q, k, v = jnp.split(qkv, 3, axis=-1)
            to_heads = lambda t: t.reshape(b, n, HEADS, DIM_HEAD).transpose(0, 2, 1, 3)
            q, k, v = (to_heads(q), to_heads(k), to_heads(v))
            q = l2norm(q) * qs
            k = l2norm(k) * ksc
            q, k = rotary_xpos(q, k)
            o = local_attention(q, k, v)
            o = o.transpose(0, 2, 1, 3).reshape(b, n, INNER)
            x = x + o @ wo
            h = shift_token(x)
            mu = h.mean(-1, keepdims=True)
            var = h.var(-1, keepdims=True)
            h = (h - mu) / jnp.sqrt(var + 1e-05) * lg + lb
            h = h @ w1 + b1
            a, g = jnp.split(h, 2, axis=-1)
            h = a * jax.nn.gelu(g, approximate=False)
            x = x + h @ w2 + b2
            return x
        for l in range(DEPTH):
            x = _layer(x, wqkv[l], q_scale[l], k_scale[l], wo[l], ln_g[l], ln_b[l], w1[l], b1[l], w2[l], b2[l])
        return x
    x = L0_attn_x
    x = x + 0.5 * _L0_ffn_ref(_layernorm(x, axis=-1), L0_ffn_gate_w, L0_ffn_w_up, L0_ffn_w_down, L0_ffn_sg_gate, L0_ffn_sg_up, L0_ffn_sg_down)
    x = x + _L0_attn_ref(_layernorm(x, axis=-1), L0_attn_w_qkv, L0_attn_w_proj)
    x = x + 0.5 * _L0_ffn_ref(_layernorm(x, axis=-1), L0_ffn_gate_w, L0_ffn_w_up, L0_ffn_w_down, L0_ffn_sg_gate, L0_ffn_sg_up, L0_ffn_sg_down)
    x = x + 0.5 * _L1_ffn_ref(_layernorm(x, axis=-1), L1_ffn_wqkv, L1_ffn_q_scale, L1_ffn_k_scale, L1_ffn_wo, L1_ffn_ln_g, L1_ffn_ln_b, L1_ffn_w1, L1_ffn_b1, L1_ffn_w2, L1_ffn_b2)
    x = x + _L1_attn_ref(_layernorm(x, axis=-1), L1_attn_w_qkv, L1_attn_w_proj, L1_attn_b_proj)
    x = x + 0.5 * _L1_ffn_ref(_layernorm(x, axis=-1), L1_ffn_wqkv, L1_ffn_q_scale, L1_ffn_k_scale, L1_ffn_wo, L1_ffn_ln_g, L1_ffn_ln_b, L1_ffn_w1, L1_ffn_b1, L1_ffn_w2, L1_ffn_b2)
    return x

_drawn_inputs = setup_inputs


def setup_inputs(seed=0):
    import zlib

    import numpy as np

    out = dict(_drawn_inputs(seed))
    spreads = {'L1_attn_b_proj': (0.0, 0.412),
     'L1_ffn_q_scale': (1.0, 0.6),
     'L1_ffn_k_scale': (1.0, 0.6),
     'L1_ffn_ln_g': (1.0, 0.6),
     'L1_ffn_ln_b': (0.0, 0.8),
     'L1_ffn_b1': (0.0, 0.8),
     'L1_ffn_b2': (0.0, 0.272)}
    factors = {'L1_ffn_wqkv': 2.769, 'L1_ffn_wo': 2.821, 'L1_ffn_w1': 5.759, 'L1_ffn_w2': 5.617}
    for name, (base, spread) in spreads.items():
        noise = np.random.default_rng([zlib.crc32(name.encode()), seed]).standard_normal(out[name].shape)
        drawn = base * np.exp(spread * noise) if base else spread * noise
        out[name] = jnp.asarray(drawn.astype(out[name].dtype))
    for name, factor in factors.items():
        out[name] = (out[name] * factor).astype(out[name].dtype)
    return out
```

```python
from contextlib import ExitStack

import numpy as np

import concourse.bass as bass
from concourse import mybir

F32 = mybir.dt.float32
BF16 = mybir.dt.bfloat16
ALU = mybir.AluOpType
ACT = mybir.ActivationFunctionType
AX = mybir.AxisListType

P = 128
NSEQ, SEQ, DIM = 16, 512, 128
NB = SEQ // P
EXPERTS, HALF = 8, 192
TAIL = HALF - P
HEADS, HD = 16, 8
LH, LD = 8, 64
INNER = LH * LD
WINDOW = 64
HID = 341
DEPTH = 2
LN_EPS = 1e-5


class Signal:

    def __init__(self, ctx, nc, name, per, unit=1):
        self.sem = ctx.enter_context(nc.semaphore(name))
        self.per, self.unit = per, unit

    def at(self, g, n):
        return g * (self.per * self.unit) + n * self.unit

    def credit(self):
        return 2 * self.per * self.unit


class Norm:

    behind = 0

    def __init__(self, ctx, nc, name):
        sig = lambda n, per: Signal(ctx, nc, f"{name}_{n}", per)
        self.name = name
        self.stats_ready = sig("stats_ready", NB)
        self.moment = sig("moment", 6)
        self.veps_ready = sig("veps_ready", 1)
        self.rstd_ready = sig("rstd_ready", 1)
        self.out_ready = sig("out_ready", NB)
        self.of_vector = [self.stats_ready, self.moment, self.veps_ready, self.out_ready]

    def buffers(self, ctx, nc, stage):
        sb = lambda n, s: ctx.enter_context(nc.sbuf_tensor(f"{self.name}{stage}_{n}", s, F32))
        self.stats = sb("stats", [P, NB, 6])
        self.mean = sb("mean", [P, NB])
        self.diff = sb("diff", [P, NB])
        self.veps = sb("veps", [P, NB])
        self.rstd = sb("rstd", [P, NB])
        self.out = sb("out", [P, 2, NB, DIM])

    def vector(self, v, g, par, src, out_free):
        stage_g, g = g, g - self.behind
        for b in range(NB):
            v.bn_stats(self.stats[:, b, :], src[:, b, :]).then_inc(self.stats_ready.sem, 1)
        me, mo = self.stats[:, :, 1], self.stats[:, :, 4]
        v.wait_ge(self.stats_ready.sem, self.stats_ready.at(g, NB))
        v.wait_ge(self.rstd_ready.sem, self.rstd_ready.at(g, 0))
        v.wait_ge(self.out_ready.sem, self.out_ready.at(stage_g, 0))
        v.tensor_tensor(self.veps[:, :], self.stats[:, :, 2], self.stats[:, :, 5], ALU.add)\
            .then_inc(self.moment.sem, 1)
        v.tensor_tensor(self.diff[:, :], me, mo, ALU.subtract).then_inc(self.moment.sem, 1)
        v.tensor_tensor(self.mean[:, :], me, mo, ALU.add).then_inc(self.moment.sem, 1)
        v.wait_ge(self.moment.sem, self.moment.at(g, 1))
        v.tensor_scalar(self.veps[:, :], self.veps[:, :], 1.0 / DIM, LN_EPS, ALU.mult, ALU.add)\
            .then_inc(self.moment.sem, 1)
        v.wait_ge(self.moment.sem, self.moment.at(g, 2))
        v.scalar_tensor_tensor(out=self.diff[:, :], in0=self.diff[:, :], scalar=0.25, in1=self.diff[:, :],
                                    op0=ALU.mult, op1=ALU.mult).then_inc(self.moment.sem, 1)
        v.wait_ge(self.moment.sem, self.moment.at(g, 3))
        v.tensor_scalar(self.mean[:, :], self.mean[:, :], 0.5, None, ALU.mult).then_inc(self.moment.sem, 1)
        v.wait_ge(self.moment.sem, self.moment.at(g, 5))
        v.tensor_tensor(self.veps[:, :], self.veps[:, :], self.diff[:, :], ALU.add).then_inc(self.veps_ready.sem, 1)
        out_free()
        v.wait_ge(self.moment.sem, self.moment.at(g, 6))
        v.wait_ge(self.rstd_ready.sem, self.rstd_ready.at(g, 1))
        for b in range(NB):
            v.tensor_scalar(self.out[:, par, b, :], src[:, b, :], self.mean[:, b:b + 1],
                                                     self.rstd[:, b:b + 1], ALU.subtract, ALU.mult)\
                                                         .then_inc(self.out_ready.sem, 1)

    def pool(self, pl, g, minus_half):
        pl.wait_ge(self.out_ready.sem, self.out_ready.at(g, 0))
        g = g - self.behind
        pl.wait_ge(self.veps_ready.sem, self.veps_ready.at(g, 1))
        pl.tensor_tensor(self.rstd[:, :], self.veps[:, :], minus_half[:, 0:NB], ALU.pow)\
            .then_inc(self.rstd_ready.sem, 1)


def pipeline(eng, first, head, body):
    head(first + 2, 0)
    with eng.Fori(first + 2, first + NSEQ, 2) as g:
        body(g, 0, True)
        body(g + 1, 1, True)
    body(first + NSEQ, 0, True)
    body(first + NSEQ + 1, 1, False)


def slot(T, g, first, b=0, n=NB):
    return T[:, bass.ds((g - (first + 2)) * NB + b, n), :]


MOE_UNITS = [(0, P), (0, TAIL)] + [(1 + p, P) for p in range(EXPERTS // 2) for _ in range(3)]
MOE_PASSES = 1 + EXPERTS // 2
MOE_PASS_UNITS = [[u for u, (q, _) in enumerate(MOE_UNITS) if q == p] for p in range(MOE_PASSES)]
MOE_UP_COLS = sum(2 * m for _, m in MOE_UNITS)


class Moe:

    def __init__(self, ctx, nc):
        sig = lambda n, per: Signal(ctx, nc, f"moe_{n}", per)
        self.norm = Norm(ctx, nc, "moe_norm")
        self.xs_ready = sig("xs_ready", 1)
        self.hT_ps = sig("hT_in_psum", 1)
        self.hT_ready = sig("hT_ready", 1)
        self.logits = sig("logits", 1)
        self.gate_step = sig("gate_step", 13)
        self.ex_ready = sig("ex_ready", 1)
        self.up = sig("up_ready", len(MOE_UNITS))
        self.silu = sig("silu_ready", len(MOE_UNITS))
        self.hid = sig("hidden_ready", len(MOE_UNITS))
        self.down = sig("down_ready", 1 + EXPERTS)
        self.accd = sig("accumulated", NB * (1 + EXPERTS))

    def emit(self, nc, run, X, W):
        n, first = self.norm, run * NSEQ
        with ExitStack() as ctx:
            pb = lambda name: ctx.enter_context(nc.psum_tensor(f"moe{run}_{name}", [P, SEQ], F32))
            sb = lambda name, s, dt=F32: ctx.enter_context(nc.sbuf_tensor(f"moe{run}_{name}", s, dt))
            n.buffers(ctx, nc, run)
            gate_bank, up_bank = [pb("g0"), pb("g1")], [pb("u0"), pb("u1")]
            down_bank = [pb("d0"), pb("d1")]
            hT_bank, lg_bank = pb("hT"), pb("lg")
            xs = sb("xs", [P, 2, NB, DIM])
            hT = sb("hTs", [P, 2, SEQ])
            self.lg = sb("lgs", [P, NB, EXPERTS])
            self.gt = sb("gt", [P, NB * EXPERTS, EXPERTS])
            self.ge = sb("ge", [P, NB * EXPERTS, EXPERTS])
            self.rank = sb("rank", [P, NB, EXPERTS])
            self.top = sb("top", [P, NB])
            self.ex = sb("ex", [P, NB, EXPERTS])
            self.den = sb("den", [P, NB])
            self.comb = sb("comb", [P, 2, NB, EXPERTS])
            sg = sb("sg", [P, 2, SEQ])
            h = sb("h", [P, 2, 3, SEQ])
            acc = sb("acc", [P, NB, DIM])
            block = ctx.enter_context(nc.Block())

            @block.gpsimd
            def _(pl):
                if run == 0:
                    pl.sem_inc(n.rstd_ready.sem, n.rstd_ready.credit())

                def head(g, par):
                    n.pool(pl, g, W["minus_half"])

                def body(g, par, more):
                    if more:
                        head(g + 1, 1 - par)

                pipeline(pl, first, head, body)

            @block.vector
            def _(v):
                if run == 0:
                    for s in (*n.of_vector, self.xs_ready, self.gate_step, self.hid, self.accd):
                        v.sem_inc(s.sem, s.credit())

                def normed(g, par):
                    v.wait_ge(self.accd.sem, self.accd.at(g, -self.accd.per))
                    v.tensor_scalar(xs[:, par, :, :], slot(X, g, first), 1.0, None, ALU.mult)\
                        .then_inc(self.xs_ready.sem, 1)
                    v.wait_ge(self.xs_ready.sem, self.xs_ready.at(g, 1))
                    n.vector(v, g, par, xs[:, par, :, :], lambda: v.wait_ge(self.hT_ps.sem, self.hT_ps.at(g, -1)))

                def head(g, par):
                    normed(g, par)
                    self.gate(v, g, par, lg_bank, W)

                def body(g, par, more):
                    def hidden(q):
                        v.wait_ge(self.down.sem, self.down.at(g, 1 + 2 * (q - 2) if q >= 2 else (0, -2)[q]))
                        for u in MOE_PASS_UNITS[q]:
                            m, part = MOE_UNITS[u][1], u - MOE_PASS_UNITS[q][0]
                            v.wait_ge(self.silu.sem, self.silu.at(g, u + 1))
                            v.tensor_tensor(h[0:m, q % 2, part, :], sg[0:m, u % 2, :],
                                                               up_bank[u % 2][0:m, :], ALU.mult)\
                                                                   .then_inc(self.hid.sem, 1)

                    def add(e):
                        v.wait_ge(self.down.sem, self.down.at(g, e + 1))
                        for b in range(NB):
                            v.wait_ge(self.accd.sem, self.accd.at(g, NB * (e - 1) + b + 1 if e else 0))
                            scalar, other = (self.comb[:, par, b, e - 1:e], acc[:, b, :]) if e else (0.5, xs[:, par, b, :])
                            o = acc[:, b, :] if e < EXPERTS else slot(X, g, first, b, 1)
                            v.scalar_tensor_tensor(
                                out=o, in0=down_bank[e % 2][:, b * DIM:(b + 1) * DIM], scalar=scalar, in1=other,
                                op0=ALU.mult, op1=ALU.add).then_inc(self.accd.sem, 1)

                    hidden(0)
                    hidden(1)
                    add(0)
                    hidden(2)
                    add(1)
                    add(2)
                    if more:
                        normed(g + 1, 1 - par)
                    hidden(3)
                    add(3)
                    add(4)
                    hidden(4)
                    add(5)
                    add(6)
                    if more:
                        self.gate(v, g + 1, 1 - par, lg_bank, W)
                    add(7)
                    add(8)

                pipeline(v, first, head, body)

            @block.scalar
            def _(act):
                if run == 0:
                    for s in (self.hT_ready, self.ex_ready, self.silu):
                        act.sem_inc(s.sem, s.credit())

                def move_hT(g, par):
                    act.wait_ge(self.hT_ps.sem, self.hT_ps.at(g, 1))
                    act.wait_ge(self.up.sem, self.up.at(g, -self.up.per))
                    act.activation(hT[:, par, :], hT_bank[:, :], ACT.Copy).then_inc(self.hT_ready.sem, 1)

                def exp_logits(g):
                    act.wait_ge(self.gate_step.sem, self.gate_step.at(g, 8))
                    act.activation(self.ex[:, :, :], self.ex[:, :, :], ACT.Exp).then_inc(self.ex_ready.sem, 1)

                def silus(g, units):
                    for u in units:
                        m = MOE_UNITS[u][1]
                        act.wait_ge(self.up.sem, self.up.at(g, u + 1))
                        act.wait_ge(self.hid.sem, self.hid.at(g, u - 1))
                        act.activation(sg[0:m, u % 2, :], gate_bank[u % 2][0:m, :], ACT.Silu)\
                            .then_inc(self.silu.sem, 1)

                def head(g, par):
                    move_hT(g, par)
                    exp_logits(g)

                def body(g, par, more):
                    last = MOE_PASS_UNITS[MOE_PASSES - 1]
                    silus(g, range(last[0]))
                    if more:
                        move_hT(g + 1, 1 - par)
                    silus(g, last)
                    if more:
                        exp_logits(g + 1)

                pipeline(act, first, head, body)

            @block.tensor
            def _(pe):
                if run == 0:
                    for s in (self.hT_ps, self.logits, self.up, self.down):
                        pe.sem_inc(s.sem, s.credit())

                def head(g, par):
                    pe.wait_ge(self.hT_ready.sem, self.hT_ready.at(g, 0))
                    for b in range(NB):
                        pe.wait_ge(n.out_ready.sem, n.out_ready.at(g, b + 1))
                        ins = pe.transpose(hT_bank[:, b * P:(b + 1) * P], n.out[:, par, b, :], W["ident"])
                    ins.then_inc(self.hT_ps.sem, 1)
                    pe.wait_ge(self.hT_ready.sem, self.hT_ready.at(g, 1))
                    pe.wait_ge(self.gate_step.sem, self.gate_step.at(g, 1 - self.gate_step.per))
                    for b in range(NB):
                        ins = pe.matmul(lg_bank[:, b * EXPERTS:(b + 1) * EXPERTS], hT[:, par, b * P:(b + 1) * P],
                                        W["wg"], start=True, stop=True)
                    ins.then_inc(self.logits.sem, 1)

                def body(g, par, more):
                    def up(q):
                        for u in MOE_PASS_UNITS[q]:
                            m, col = MOE_UNITS[u][1], 2 * sum(m for _, m in MOE_UNITS[:u])
                            pe.wait_ge(self.hid.sem, self.hid.at(g, u - 1))
                            pe.matmul(gate_bank[u % 2][0:m, :], W["wup"][:, col:col + m], hT[:, par, :],
                                      start=True, stop=True)
                            pe.matmul(up_bank[u % 2][0:m, :], W["wup"][:, col + m:col + 2 * m],
                                                        hT[:, par, :], start=True, stop=True).then_inc(self.up.sem, 1)

                    def down(q):
                        pe.wait_ge(self.hid.sem, self.hid.at(g, MOE_PASS_UNITS[q][-1] + 1))
                        tail = len(MOE_PASS_UNITS[q]) - 1
                        for j in range(tail):
                            e = 2 * q - 1 + j if q else 0
                            pe.wait_ge(self.accd.sem, self.accd.at(g, NB * (e - 1) if e >= 2 else (0, -NB)[e]))
                            r = TAIL * j
                            for b in range(NB):
                                o = down_bank[e % 2][:, b * DIM:(b + 1) * DIM]
                                pe.matmul(o, h[:, q % 2, j, b * P:(b + 1) * P], W["wdm"][:, e, :],
                                          start=True, stop=False)
                                ins = pe.matmul(o, h[r:r + TAIL, q % 2, tail, b * P:(b + 1) * P],
                                                W["wdt"][r:r + TAIL, q, :], start=False, stop=True)
                            ins.then_inc(self.down.sem, 1)

                    up(0)
                    for q in range(MOE_PASSES):
                        if q == 3 and more:
                            head(g + 1, 1 - par)
                        if q + 1 < MOE_PASSES:
                            up(q + 1)
                        down(q)

                pipeline(pe, first, head, body)

    def gate(self, v, g, par, lg_bank, W):
        v.wait_ge(self.accd.sem, self.accd.at(g, -self.accd.per))
        v.wait_ge(self.logits.sem, self.logits.at(g, 1))
        lg, gt, ge, ex = self.lg, self.gt, self.ge, self.ex
        v.tensor_scalar(lg[:, :, :], lg_bank[:, 0:NB * EXPERTS].rearrange("p (b e) -> p b e", b=NB), 1.0,
                             None, ALU.mult).then_inc(self.gate_step.sem, 1)
        v.wait_ge(self.gate_step.sem, self.gate_step.at(g, 1))
        shape = [P, NB, EXPERTS, EXPERTS]
        other = lg[:, :, :].unsqueeze(2).broadcast_to(shape)
        own = lg[:, :, :].unsqueeze(3).broadcast_to(shape)
        v4 = lambda t: t[:, :, :].rearrange("p (b e) j -> p b e j", b=NB)
        v.tensor_tensor(v4(gt), other, own, ALU.is_gt).then_inc(self.gate_step.sem, 1)
        v.wait_ge(self.gate_step.sem, self.gate_step.at(g, 2))
        v.tensor_tensor(v4(ge), other, own, ALU.is_ge).then_inc(self.gate_step.sem, 1)
        v.wait_ge(self.gate_step.sem, self.gate_step.at(g, 3))
        v.tensor_tensor(ge[:, :, :], ge[:, :, :], W["lower"], ALU.mult).then_inc(self.gate_step.sem, 1)
        v.wait_ge(self.gate_step.sem, self.gate_step.at(g, 4))
        v.tensor_tensor(gt[:, :, :], gt[:, :, :], ge[:, :, :], ALU.max).then_inc(self.gate_step.sem, 1)
        v.wait_ge(self.gate_step.sem, self.gate_step.at(g, 5))
        v.tensor_reduce(self.rank[:, :, :].rearrange("p b e -> p (b e)"), gt[:, :, :], AX.X, ALU.add)\
            .then_inc(self.gate_step.sem, 1)
        v.wait_ge(self.gate_step.sem, self.gate_step.at(g, 6))
        v.tensor_reduce(self.top[:, :], lg[:, :, :], AX.X, ALU.max).then_inc(self.gate_step.sem, 1)
        v.wait_ge(self.gate_step.sem, self.gate_step.at(g, 7))
        bc = lambda t: t[:, :].unsqueeze(2).broadcast_to([P, NB, EXPERTS])
        v.tensor_tensor(ex[:, :, :], lg[:, :, :], bc(self.top), ALU.subtract).then_inc(self.gate_step.sem, 1)
        v.wait_ge(self.gate_step.sem, self.gate_step.at(g, 8))
        v.wait_ge(self.ex_ready.sem, self.ex_ready.at(g, 1))
        v.scalar_tensor_tensor(out=ex[:, :, :], in0=self.rank[:, :, :], scalar=1.5, in1=ex[:, :, :],
                                    op0=ALU.is_lt, op1=ALU.mult).then_inc(self.gate_step.sem, 1)
        v.wait_ge(self.gate_step.sem, self.gate_step.at(g, 9))
        v.tensor_reduce(self.den[:, :], ex[:, :, :], AX.X, ALU.add).then_inc(self.gate_step.sem, 1)
        v.wait_ge(self.gate_step.sem, self.gate_step.at(g, 10))
        v.reciprocal(self.den[:, :], self.den[:, :]).then_inc(self.gate_step.sem, 1)
        v.wait_ge(self.gate_step.sem, self.gate_step.at(g, 11))
        v.tensor_scalar(self.den[:, :], self.den[:, :], 0.5, None, ALU.mult).then_inc(self.gate_step.sem, 1)
        v.wait_ge(self.gate_step.sem, self.gate_step.at(g, 12))
        v.tensor_tensor(self.comb[:, par, :, :], ex[:, :, :], bc(self.den), ALU.mult).then_inc(self.gate_step.sem, 1)
        v.wait_ge(self.gate_step.sem, self.gate_step.at(g, 13))


HID_BLOCKS = [(0, P), (P, P), (2 * P, HID - 2 * P)]


class Geglu:

    def __init__(self, ctx, nc):
        sig = lambda n, per, unit=1: Signal(ctx, nc, f"ffn_{n}", per, unit)
        self.norm = Norm(ctx, nc, "ffn_norm")
        self.shifted = sig("shifted", 3, 16)
        self.hT_ps = sig("hT_in_psum", 1)
        self.hT_ready = sig("hT_ready", 1)
        self.up = sig("up_ready", 3)
        self.gelu = sig("gelu_ready", 3)
        self.hid = sig("hidden_ready", 3)
        self.down = sig("down_ready", 1)
        self.sum = sig("sum_ready", 1)
        self.summed = sig("summed", 1)
        self.moved = sig("result_stored", 1)
        self.first_token = ctx.enter_context(nc.semaphore("ffn_first_token"))

    def emit(self, nc, run, X, Y, W, layer, last):
        n, first = self.norm, run * NSEQ
        others = (run - run // DEPTH) * NSEQ
        w1, w2 = W["w1"][:, layer, :], W["w2"][:, layer, :, :]
        b1, b2, lg, lb = W["b1"][:, layer, :], W["b2"][:, layer, :], W["ln_g"], W["ln_b"]
        with ExitStack() as ctx:
            pb = lambda name: ctx.enter_context(nc.psum_tensor(f"ffn{run}_{name}", [P, SEQ], F32))
            sb = lambda name, s, dt=F32: ctx.enter_context(nc.sbuf_tensor(f"ffn{run}_{name}", s, dt))
            n.buffers(ctx, nc, run)
            a_bank, g_bank = [pb(f"a{j}") for j in range(3)], [pb(f"g{j}") for j in range(3)]
            hT_bank, out_bank = pb("hT"), pb("out")
            hs = sb("shifted", [P, 2, NB, DIM])
            hT = sb("hTs", [P, 2, SEQ])
            gl = sb("gelu", [P, 3, SEQ])
            hid = sb("hidden", [P, 2, 3, SEQ])
            total = sb("total", [P, NB, DIM])
            H = DIM // 2
            block = ctx.enter_context(nc.Block())

            @block.sync
            def _(sp):
                if run == 0:
                    sp.sem_inc(self.shifted.sem, self.shifted.credit())
                sp.wait_ge(self.first_token, run + 1)

                def head(g, par):
                    sp.wait_ge(self.shifted.sem, self.shifted.at(g, 0))
                    sp.wait_ge(n.out_ready.sem, n.out_ready.at(g, -NB))
                    y = lambda b, c: slot(Y, g, first, b, c)
                    sp.dma_start(hs[:, par, :, 0:H], y(0, NB)[:, :, 0:H]).then_inc(self.shifted.sem, 16)
                    sp.dma_start(hs[1:P, par, :, H:DIM], y(0, NB)[0:P - 1, :, H:DIM]).then_inc(self.shifted.sem, 16)
                    sp.dma_start(hs[0:1, par, 1:NB, H:DIM], y(0, NB - 1)[P - 1:P, :, H:DIM]).then_inc(self.shifted.sem, 16)

                def body(g, par, more):
                    if more:
                        head(g + 1, 1 - par)

                pipeline(sp, first, head, body)

            @block.gpsimd
            def _(pl):
                if run == 0:
                    pl.sem_inc(n.rstd_ready.sem, n.rstd_ready.credit())

                def head(g, par):
                    n.pool(pl, g, W["minus_half"])

                def body(g, par, more):
                    if more:
                        head(g + 1, 1 - par)

                pipeline(pl, first, head, body)

            @block.vector
            def _(v):
                if run == 0:
                    for s in (*n.of_vector, self.hid, self.sum, self.summed, self.moved):
                        v.sem_inc(s.sem, s.credit())
                v.memset(hs[0:1, :, 0:1, H:DIM], 0.0).then_inc(self.first_token, 1)

                def head(g, par):
                    v.wait_ge(self.shifted.sem, self.shifted.at(g, 3))
                    n.vector(v, g, par, hs[:, par, :, :], lambda: v.wait_ge(self.hT_ps.sem, self.hT_ps.at(g, -1)))

                def body(g, par, more):
                    for j, (_, m) in enumerate(HID_BLOCKS):
                        v.wait_ge(self.gelu.sem, self.gelu.at(g, j + 1))
                        v.wait_ge(self.down.sem, self.down.at(g, -1))
                        v.scalar_tensor_tensor(
                            out=hid[0:m, par, j, :], in0=a_bank[j][0:m, :], scalar=b1[0:m, j:j + 1],
                            in1=gl[0:m, j, :], op0=ALU.add, op1=ALU.mult).then_inc(self.hid.sem, 1)
                    if more:
                        head(g + 1, 1 - par)
                    v.wait_ge(self.down.sem, self.down.at(g, 1))
                    v.wait_ge(self.moved.sem, self.moved.at(g, 0))
                    out3 = out_bank[:, :].rearrange("p (b d) -> p b d", b=NB)
                    v.tensor_tensor(total[:, :, :], out3,
                                                       b2.unsqueeze(1).broadcast_to([P, NB, DIM]), ALU.add)\
                                                           .then_inc(self.sum.sem, 1)
                    v.wait_ge(self.sum.sem, self.sum.at(g, 1))
                    y = slot(Y, g, first)
                    if last:
                        v.tensor_tensor(total[:, :, :], total[:, :, :], y, ALU.add).then_inc(self.summed.sem, 1)
                        v.wait_ge(self.summed.sem, self.summed.at(g - others, 1))
                        x = slot(X, g, first)
                        v.scalar_tensor_tensor(out=x, in0=total[:, :, :], scalar=0.5, in1=x,
                                                                    op0=ALU.mult, op1=ALU.add)\
                                                                        .then_inc(self.moved.sem, 1)
                    else:
                        v.tensor_tensor(y, total[:, :, :], y, ALU.add).then_inc(self.moved.sem, 1)

                pipeline(v, first, head, body)

            @block.scalar
            def _(act):
                if run == 0:
                    for s in (self.hT_ready, self.gelu):
                        act.sem_inc(s.sem, s.credit())

                def head(g, par):
                    act.wait_ge(self.hT_ps.sem, self.hT_ps.at(g, 1))
                    act.wait_ge(self.up.sem, self.up.at(g, -3))
                    act.activation(hT[:, par, :], hT_bank[:, :], ACT.Identity,
                                                           bias=lb[:, layer:layer + 1], scale=lg[:, layer:layer + 1])\
                                                               .then_inc(self.hT_ready.sem, 1)

                def body(g, par, more):
                    for j, (_, m) in enumerate(HID_BLOCKS):
                        act.wait_ge(self.up.sem, self.up.at(g, j + 1))
                        act.wait_ge(self.hid.sem, self.hid.at(g, j - 2))
                        act.activation(gl[0:m, j, :], g_bank[j][0:m, :], ACT.Gelu,
                                                           bias=b1[0:m, 3 + j:4 + j]).then_inc(self.gelu.sem, 1)
                    if more:
                        head(g + 1, 1 - par)

                pipeline(act, first, head, body)

            @block.tensor
            def _(pe):
                if run == 0:
                    for s in (self.hT_ps, self.up, self.down):
                        pe.sem_inc(s.sem, s.credit())

                def head(g, par):
                    pe.wait_ge(self.hT_ready.sem, self.hT_ready.at(g, 0))
                    for b in range(NB):
                        pe.wait_ge(n.out_ready.sem, n.out_ready.at(g, b + 1))
                        ins = pe.transpose(hT_bank[:, b * P:(b + 1) * P], n.out[:, par, b, :], W["ident"])
                    ins.then_inc(self.hT_ps.sem, 1)

                def body(g, par, more):
                    pe.wait_ge(self.hT_ready.sem, self.hT_ready.at(g, 1))
                    for j, (r, m) in enumerate(HID_BLOCKS):
                        pe.wait_ge(self.hid.sem, self.hid.at(g, j - 2))
                        pe.matmul(g_bank[j][0:m, :], w1[:, HID + r:HID + r + m], hT[:, par, :], start=True, stop=True)
                        pe.matmul(a_bank[j][0:m, :], w1[:, r:r + m], hT[:, par, :],
                                                    start=True, stop=True).then_inc(self.up.sem, 1)
                    if more:
                        head(g + 1, 1 - par)
                    pe.wait_ge(self.hid.sem, self.hid.at(g, 3))
                    pe.wait_ge(self.sum.sem, self.sum.at(g, 0))
                    for b in range(NB):
                        for j, (_, m) in enumerate(HID_BLOCKS):
                            ins = pe.matmul(out_bank[:, b * DIM:(b + 1) * DIM], hid[0:m, par, j, b * P:(b + 1) * P],
                                            w2[0:m, j, :], start=(j == 0), stop=(j == 2))
                    ins.then_inc(self.down.sem, 1)

                pipeline(pe, first, head, body)


PAIRS = LH // 2
UNITS = NB * PAIRS
BAND = P + WINDOW


def unit_heads(k):
    a = k % PAIRS
    return [4 * (a // 2) + a % 2 + 2 * j for j in range(2)]


class LocalAttention:

    def __init__(self, ctx, nc):
        sig = lambda n, per, unit=1: Signal(ctx, nc, f"loc_{n}", per, unit)
        self.norm = Norm(ctx, nc, "loc_norm")
        self.xs_ready = sig("xs_ready", 1)
        self.yT_ps = sig("yT_in_psum", 1)
        self.hT_ready = sig("hT_ready", 2)
        self.qkv = sig("qkv_ready", NB)
        self.squares = sig("squares", NB)
        self.v_ready = sig("v_ready", NB)
        self.ss_ready = sig("ss_ready", 2 * NB)
        self.terms = sig("turn_terms", 3 * NB)
        self.rn_ready = sig("rn_ready", NB)
        self.turned = sig("turned", 2 * NB)
        self.k_normed = sig("k_normed", NB)
        self.qT_ps = sig("qT_in_psum", NB)
        self.kT_ps = sig("kT_in_psum", NB)
        self.qT_ready = sig("qT_ready", NB)
        self.kT_ready = sig("kT_ready", NB)
        self.scores = sig("scores", UNITS)
        self.top = sig("top", UNITS)
        self.bias = sig("bias", UNITS)
        self.probs = sig("probs", 2 * UNITS)
        self.rsum = sig("rsum", UNITS)
        self.divided = sig("divided", UNITS)
        self.pT_ps = sig("pT_in_psum", UNITS)
        self.pT_ready = [sig(f"pT_ready{j}", UNITS // 2) for j in range(2)]
        self.pv = sig("pv", UNITS // 2)
        self.oT_ready = sig("oT_ready", NB)
        self.wo = sig("wo_ready", NB)
        self.moved = sig("result_stored", NB)
        self.cleared = ctx.enter_context(nc.semaphore("loc_cleared"))

    def emit(self, nc, run, X, Y, W, layer):
        n, first = self.norm, run * NSEQ
        n.behind = (run - run // DEPTH) * NSEQ
        wqkv, wo = W["wqkv"][:, layer, :], W["wo"][:, layer, :, :]
        turn_cos, turn_sin = W["turn_cos"][:, layer, :, :, :], W["turn_sin"][:, layer, :, :, :]
        H = DIM // 2
        with ExitStack() as ctx:
            pb = lambda name, banks=1: ctx.enter_context(nc.psum_tensor(f"loc{run}_{name}", [P, banks * SEQ], F32))
            sb = lambda name, s, dt=F32: ctx.enter_context(nc.sbuf_tensor(f"loc{run}_{name}", s, dt))
            n.buffers(ctx, nc, run)
            qk_bank = pb("qk", 2)
            v_bank = pb("v")
            t_bank = pb("t")
            s_bank = [pb("s0"), pb("s1")]
            p_bank = pb("p")
            o_bank = pb("o")
            xs = sb("xs", [P, NB, DIM])
            hT = sb("hTs", [P, 2, SEQ])
            sq = sb("sq", [P, 2 * INNER])
            ss = sb("ss", [P, 2 * LH])
            rn = sb("rn", [P, NB, 2 * LH])
            t1 = sb("t1", [P, 2 * INNER])
            t2 = sb("t2", [P, 2 * INNER])
            qk = sb("qk_turned", [P, 2 * INNER])
            vs = sb("vs", [P, NB, INNER])
            qT = sb("qT", [P, 2, PAIRS, P])
            kT = sb("kT", [P, PAIRS, SEQ])
            top = sb("tops", [P, UNITS, 2])
            bias = sb("biases", [P, UNITS, 2])
            sums = sb("sums", [P, UNITS, 2])
            rs = sb("rs", [P, UNITS, 2])
            probs = sb("probs_s", [P, 2, 2, 2 * P])
            pT = sb("pT", [P, 2, 2, BAND])
            oT = sb("oT", [P, PAIRS, P])
            block = ctx.enter_context(nc.Block())
            by_head = lambda t: t.rearrange("p (h d) -> p h d", d=LD)

            @block.gpsimd
            def _(pl):
                if run == 0:
                    for s in (n.rstd_ready, self.rn_ready, self.turned, self.k_normed, self.divided):
                        pl.sem_inc(s.sem, s.credit())

                def turn(g, t):
                    pl.wait_ge(self.terms.sem, self.terms.at(g, 3 * t + 3))
                    pl.wait_ge(self.kT_ps.sem, self.kT_ps.at(g, t))
                    for j in range(2):
                        part = slice(j * INNER, (j + 1) * INNER)
                        pl.tensor_tensor(qk[:, part], t1[:, part], t2[:, part], ALU.add).then_inc(self.turned.sem, 1)
                    pl.wait_ge(self.ss_ready.sem, self.ss_ready.at(g, 2 * t + 2))
                    pl.wait_ge(self.probs.sem, self.probs.at(g, 2 * PAIRS * (t + 1) - 2 * UNITS))
                    pl.tensor_tensor(rn[:, t, :], ss[:, :], W["minus_half"][:, 0:2 * LH],
                                                             ALU.pow).then_inc(self.rn_ready.sem, 1)
                    pl.wait_ge(self.rn_ready.sem, self.rn_ready.at(g, t + 1))
                    pl.wait_ge(self.turned.sem, self.turned.at(g, 2 * t + 2))
                    k3 = by_head(qk[:, INNER:2 * INNER])
                    pl.tensor_tensor(
                        k3, k3, rn[:, t, LH:2 * LH].unsqueeze(2).broadcast_to([P, LH, LD]), ALU.mult)\
                            .then_inc(self.k_normed.sem, 1)

                def divide(g, k):
                    pl.wait_ge(self.rsum.sem, self.rsum.at(g, k + 1))
                    p_ = probs[:, k % 2, :, H:2 * P]
                    pl.tensor_tensor(
                        p_, p_, rs[:, k, :].unsqueeze(2).broadcast_to([P, 2, BAND]), ALU.mult)\
                            .then_inc(self.divided.sem, 1)

                def head(g, par):
                    if layer == 0:
                        n.pool(pl, g, W["minus_half"])
                    turn(g, 0)

                def body(g, par, more):
                    for k in range(UNITS):
                        t = k // PAIRS
                        if k % PAIRS == 1 and t + 1 < NB:
                            turn(g, t + 1)
                        if k == 1 and more and layer == 0:
                            n.pool(pl, g + 1, W["minus_half"])
                        if k == 13 and more:
                            turn(g + 1, 0)
                        divide(g, k)

                pipeline(pl, first, head, body)

            @block.vector
            def _(v):
                if run == 0:
                    for s in (*n.of_vector, self.xs_ready, self.ss_ready, self.terms, self.top, self.bias,
                              self.rsum, self.pT_ready[0], self.moved):
                        v.sem_inc(s.sem, s.credit())
                v.memset(hT[H:P, :, 0:1], 0.0).then_inc(self.cleared, 1)
                v.memset(probs[:, :, :, 0:H], 0.0).then_inc(self.cleared, 1)

                def tokens(g, par):
                    if layer == 0:
                        v.wait_ge(n.out_ready.sem, n.out_ready.at(g, 0))
                        v.tensor_scalar(xs[:, :, :], slot(X, g, first), 1.0, None, ALU.mult)\
                            .then_inc(self.xs_ready.sem, 1)
                        v.wait_ge(self.xs_ready.sem, self.xs_ready.at(g - n.behind, 1))
                        v.wait_ge(self.moved.sem, self.moved.at(g, -NB))
                        n.vector(v, g, par, xs, lambda: v.wait_ge(self.yT_ps.sem, self.yT_ps.at(g, -1)))
                    else:
                        v.wait_ge(self.moved.sem, self.moved.at(g, -NB))
                        v.wait_ge(self.yT_ps.sem, self.yT_ps.at(g, -1))
                        for b in range(NB):
                            v.tensor_scalar(n.out[:, par, b:b + 1, :], slot(Y, g, first, b, 1),
                                                                  1.0, None, ALU.mult).then_inc(n.out_ready.sem, 1)

                def squares(g, t):
                    v.wait_ge(self.squares.sem, self.squares.at(g, t + 1))
                    v.wait_ge(self.rn_ready.sem, self.rn_ready.at(g, t))
                    v.tensor_reduce(ss[:, :], by_head(sq[:, :]), AX.X, ALU.add).then_inc(self.ss_ready.sem, 1)
                    v.wait_ge(self.ss_ready.sem, self.ss_ready.at(g, 2 * t + 1))
                    v.tensor_scalar(ss[:, :], ss[:, :], 1e-24, None, ALU.max).then_inc(self.ss_ready.sem, 1)

                def turn_terms(g, t):
                    v.wait_ge(self.qkv.sem, self.qkv.at(g, t + 1))
                    v.wait_ge(self.turned.sem, self.turned.at(g, 2 * t))
                    tables = lambda tab, j: tab[:, t, j, :].unsqueeze(1).broadcast_to([P, LH, LD])
                    q4 = qk_bank[:, :].rearrange("p (j h d) -> p j h d", j=2, d=LD)
                    cos = turn_cos[:, t, :, :].unsqueeze(2).broadcast_to([P, 2, LH, LD])
                    v.tensor_tensor(t1[:, :].rearrange("p (j h d) -> p j h d", j=2, d=LD),
                                                         q4, cos, ALU.mult).then_inc(self.terms.sem, 1)
                    for j in range(2):
                        halves = lambda ap: ap.rearrange("p h (s d) -> p h s d", s=2)
                        src = halves(q4[:, j, :, :])[:, :, ::-1, :]
                        v.tensor_tensor(halves(by_head(t2[:, j * INNER:(j + 1) * INNER])), src,
                                                             halves(tables(turn_sin, j)), ALU.mult)\
                                                                 .then_inc(self.terms.sem, 1)

                def top_of(g, k):
                    v.wait_ge(self.scores.sem, self.scores.at(g, k + 1))
                    s3 = s_bank[k % 2][:, 0:2 * BAND].rearrange("p (j c) -> p j c", j=2)
                    v.tensor_reduce(top[:, k, :], s3, AX.X, ALU.max, negate=True).then_inc(self.top.sem, 1)
                    v.wait_ge(self.top.sem, self.top.at(g, k + 1))
                    v.wait_ge(self.rn_ready.sem, self.rn_ready.at(g, k // PAIRS + 1))
                    h = unit_heads(k)
                    v.tensor_tensor(bias[:, k, :], top[:, k, :],
                                                        rn[:, k // PAIRS, h[0]:h[1] + 1:2], ALU.mult)\
                                                            .then_inc(self.bias.sem, 1)

                def inverse(g, k):
                    v.wait_ge(self.probs.sem, self.probs.at(g, 2 * k + 2))
                    v.reciprocal(rs[:, k, :], sums[:, k, :]).then_inc(self.rsum.sem, 1)

                def move_pT(g, k):
                    v.wait_ge(self.pT_ps.sem, self.pT_ps.at(g, k + 1))
                    v.wait_ge(self.pv.sem, self.pv.at(g, k // 2))
                    c = BAND if k >= PAIRS else P
                    src = p_bank[:, 0:2 * BAND].rearrange("p (j c) -> p j c", j=2)[:, :, 0:c]
                    v.tensor_copy(pT[:, k % 2, :, 0:c], src).then_inc(self.pT_ready[0].sem, 1)

                def add(g, par, t):
                    v.wait_ge(self.wo.sem, self.wo.at(g, t + 1))
                    v.tensor_tensor(slot(Y, g, first, t, 1), t_bank[:, 0:DIM].unsqueeze(1),
                                                         n.out[:, par, t:t + 1, :], ALU.add)\
                                                             .then_inc(self.moved.sem, 1)

                def head(g, par):
                    tokens(g, par)
                    squares(g, 0)
                    turn_terms(g, 0)

                def body(g, par, more):
                    for k in range(UNITS + 5):
                        if k < UNITS:
                            top_of(g, k)
                        if k % PAIRS == 0 and k // PAIRS + 1 < NB:
                            squares(g, k // PAIRS + 1)
                            turn_terms(g, k // PAIRS + 1)
                        if k == 2 and more:
                            tokens(g + 1, 1 - par)
                        if k == 12 and more:
                            squares(g + 1, 0)
                            turn_terms(g + 1, 0)
                        if 1 <= k <= UNITS:
                            inverse(g, k - 1)
                        if 2 <= k < UNITS + 2 and k % 2 == 0:
                            move_pT(g, k - 2)
                        if k >= 8 and k % PAIRS == 0:
                            add(g, par, (k - 8) // PAIRS)

                pipeline(v, first, head, body)

            @block.scalar
            def _(act):
                if run == 0:
                    for s in (self.hT_ready, self.squares, self.v_ready, self.qT_ready, self.kT_ready, self.probs,
                              self.pT_ready[1], self.oT_ready):
                        act.sem_inc(s.sem, s.credit())
                act.wait_ge(self.cleared, 2 * run + 2)
                copy = lambda o, i: act.activation(o, i, ACT.Copy)

                def move_hT(g, par):
                    act.wait_ge(self.yT_ps.sem, self.yT_ps.at(g, 1))
                    act.wait_ge(self.qkv.sem, self.qkv.at(g, -NB))
                    copy(hT[0:H, par, :], t_bank[0:H, :]).then_inc(self.hT_ready.sem, 1)
                    copy(hT[H:P, par, 1:SEQ], t_bank[H:P, 0:SEQ - 1]).then_inc(self.hT_ready.sem, 1)

                def take_qkv(g, t):
                    act.wait_ge(self.qkv.sem, self.qkv.at(g, t + 1))
                    act.wait_ge(self.ss_ready.sem, self.ss_ready.at(g, 2 * t))
                    act.activation(sq[:, :], qk_bank[:, :], ACT.Square).then_inc(self.squares.sem, 1)
                    act.wait_ge(self.pv.sem, self.pv.at(g, (PAIRS * min(t + 2, NB) - UNITS) // 2))
                    copy(vs[:, t, :], v_bank[:, :]).then_inc(self.v_ready.sem, 1)

                def take_T(g, t):
                    act.wait_ge(self.qT_ps.sem, self.qT_ps.at(g, t + 1))
                    act.wait_ge(self.scores.sem, self.scores.at(g, PAIRS * (t - 1)))
                    copy(qT[:, t % 2, :, :], t_bank[:, :].rearrange("p (a c) -> p a c", c=P))\
                        .then_inc(self.qT_ready.sem, 1)
                    act.wait_ge(self.kT_ps.sem, self.kT_ps.at(g, t + 1))
                    act.wait_ge(self.scores.sem, self.scores.at(g, PAIRS * min(t + 2, NB) - UNITS))
                    copy(kT[:, :, t * P:(t + 1) * P],
                                                 v_bank[:, :].rearrange("p (a c) -> p a c", c=P))\
                                                     .then_inc(self.kT_ready.sem, 1)

                def exp(g, k):
                    act.wait_ge(self.bias.sem, self.bias.at(g, k + 1))
                    act.wait_ge(self.pT_ps.sem, self.pT_ps.at(g, k - 1))
                    act.wait_ge(self.rsum.sem, self.rsum.at(g, k + 1 - UNITS))
                    for j, h in enumerate(unit_heads(k)):
                        act.activation(
                            probs[:, k % 2, j, H:2 * P], s_bank[k % 2][:, j * BAND:(j + 1) * BAND], ACT.Exp,
                            bias=bias[:, k, j:j + 1], scale=rn[:, k // PAIRS, h:h + 1], accum_out=sums[:, k, j:j + 1])\
                                .then_inc(self.probs.sem, 1)

                def move_pT(g, k):
                    act.wait_ge(self.pT_ps.sem, self.pT_ps.at(g, k + 1))
                    act.wait_ge(self.pv.sem, self.pv.at(g, (k - 1) // 2))
                    c = BAND if k >= PAIRS else P
                    src = p_bank[:, 0:2 * BAND].rearrange("p (j c) -> p j c", j=2)[:, :, 0:c]
                    copy(pT[:, k % 2, :, 0:c], src).then_inc(self.pT_ready[1].sem, 1)

                def move_oT(g, t):
                    act.wait_ge(self.pv.sem, self.pv.at(g, PAIRS // 2 * (t + 1)))
                    act.wait_ge(self.wo.sem, self.wo.at(g, t))
                    copy(oT[:, :, :], o_bank[:, :].rearrange("p (a c) -> p a c", c=P)).then_inc(self.oT_ready.sem, 1)

                def head(g, par):
                    move_hT(g, par)
                    take_qkv(g, 0)
                    take_T(g, 0)

                def body(g, par, more):
                    for k in range(UNITS + 3):
                        if k < UNITS:
                            exp(g, k)
                        if k % PAIRS == 0 and k // PAIRS + 1 < NB:
                            take_qkv(g, k // PAIRS + 1)
                        if k == 12 and more:
                            take_qkv(g + 1, 0)
                        if 2 <= k < UNITS + 2 and k % 2 == 1:
                            move_pT(g, k - 2)
                        if k >= 6 and k % PAIRS == 2:
                            move_oT(g, (k - 6) // PAIRS)
                        if k % PAIRS == 3 and k // PAIRS + 1 < NB:
                            take_T(g, k // PAIRS + 1)
                        if k == 15 and more:
                            take_T(g + 1, 0)
                        if k == 6 and more:
                            move_hT(g + 1, 1 - par)

                pipeline(act, first, head, body)

            @block.tensor
            def _(pe):
                if run == 0:
                    for s in (self.yT_ps, self.qkv, self.qT_ps, self.kT_ps, self.scores, self.pT_ps, self.pv, self.wo):
                        pe.sem_inc(s.sem, s.credit())
                pe.wait_ge(self.cleared, 2 * run + 2)

                def transpose_y(g, par):
                    for b in range(NB):
                        pe.wait_ge(n.out_ready.sem, n.out_ready.at(g, b + 1))
                        ins = pe.transpose(t_bank[:, b * P:(b + 1) * P], n.out[:, par, b, :], W["ident"])
                    ins.then_inc(self.yT_ps.sem, 1)

                def make_qkv(g, par, t):
                    pe.wait_ge(self.hT_ready.sem, self.hT_ready.at(g, 2))
                    pe.wait_ge(self.squares.sem, self.squares.at(g, t))
                    pe.wait_ge(self.terms.sem, self.terms.at(g, 3 * t))
                    pe.wait_ge(self.kT_ready.sem, self.kT_ready.at(g, t))
                    for j, o in enumerate((qk_bank[:, 0:INNER], qk_bank[:, INNER:2 * INNER], v_bank[:, :])):
                        ins = pe.matmul(o, hT[:, par, t * P:(t + 1) * P], wqkv[:, j * INNER:(j + 1) * INNER],
                                        start=True, stop=True)
                    ins.then_inc(self.qkv.sem, 1)

                def transpose_qk(g, t):
                    pe.wait_ge(self.turned.sem, self.turned.at(g, 2 * t + 1))
                    for a in range(PAIRS):
                        ins = pe.transpose(t_bank[:, a * P:(a + 1) * P], qk[:, a * P:(a + 1) * P], W["ident"])
                    ins.then_inc(self.qT_ps.sem, 1)
                    pe.wait_ge(self.k_normed.sem, self.k_normed.at(g, t + 1))
                    pe.wait_ge(self.v_ready.sem, self.v_ready.at(g, t + 1))
                    for a in range(PAIRS):
                        ins = pe.transpose(v_bank[:, a * P:(a + 1) * P], qk[:, INNER + a * P:INNER + (a + 1) * P],
                                           W["ident"])
                    ins.then_inc(self.kT_ps.sem, 1)

                def score(g, k):
                    t = k // PAIRS
                    pe.wait_ge(self.qT_ready.sem, self.qT_ready.at(g, t + 1))
                    pe.wait_ge(self.kT_ready.sem, self.kT_ready.at(g, t + 1))
                    pe.wait_ge(self.probs.sem, self.probs.at(g, 2 * (k - 1)))
                    skip = WINDOW if t == 0 else 0
                    bank = s_bank[k % 2]
                    pe.matmul(bank[:, 0:2 * BAND], W["ident16"], W["band"][:, min(t, 1), :], start=True, stop=False)
                    for j, h in enumerate(unit_heads(k)):
                        rows = slice(LD * (h % 2), LD * (h % 2) + LD)
                        ins = pe.matmul(bank[:, j * BAND + skip:(j + 1) * BAND], qT[rows, t % 2, h // 2, :],
                                        kT[rows, h // 2, t * P - WINDOW + skip:(t + 1) * P], start=False, stop=(j == 1))
                    ins.then_inc(self.scores.sem, 1)

                def transpose_p(g, k):
                    pe.wait_ge(self.divided.sem, self.divided.at(g, k + 1))
                    pe.wait_ge(self.pT_ready[(k - 1) % 2].sem, self.pT_ready[(k - 1) % 2].at(g, (k + 1) // 2 if k % 2 else k // 2))
                    for j in range(2):
                        o = p_bank[:, j * BAND:(j + 1) * BAND]
                        ins = pe.transpose(o[:, 0:P], probs[:, k % 2, j, P:2 * P], W["ident"])
                        if k >= PAIRS:
                            ins = pe.transpose(o[:, P:BAND], probs[0:WINDOW, k % 2, j, 0:P],
                                               W["ident"][0:WINDOW, 0:WINDOW])
                    ins.then_inc(self.pT_ps.sem, 1)

                def times_v(g, k):
                    t = k // PAIRS
                    pe.wait_ge(self.pT_ready[0].sem, self.pT_ready[0].at(g, k // 2 + 1))
                    pe.wait_ge(self.pT_ready[1].sem, self.pT_ready[1].at(g, k // 2 + 1))
                    if k % PAIRS == 0:
                        pe.wait_ge(self.oT_ready.sem, self.oT_ready.at(g, t))
                    for j in range(2):
                        for own in (True, False)[0:2 if t else 1]:
                            for u in (k, k + 1):
                                h = unit_heads(u)[j]
                                o = o_bank[LD * (h % 2):LD * (h % 2) + LD, h // 2 * P:(h // 2 + 1) * P]
                                v_ = vs[:, t if own else t - 1, h * LD:(h + 1) * LD]
                                if own:
                                    ins = pe.matmul(o, v_, pT[:, u % 2, j, 0:P], start=True, stop=(t == 0))
                                else:
                                    ins = pe.matmul(o[:, 0:WINDOW], v_, pT[:, u % 2, j, P:BAND],
                                                    start=False, stop=True)
                    ins.then_inc(self.pv.sem, 1)

                def project(g, t):
                    pe.wait_ge(self.oT_ready.sem, self.oT_ready.at(g, t + 1))
                    for a in range(PAIRS):
                        ins = pe.matmul(t_bank[:, 0:DIM], oT[:, a, :], wo[:, a, :], start=(a == 0), stop=(a == PAIRS - 1))
                    ins.then_inc(self.wo.sem, 1)

                def head(g, par):
                    transpose_y(g, par)
                    make_qkv(g, par, 0)
                    transpose_qk(g, 0)

                def body(g, par, more):
                    for k in range(UNITS + 5):
                        t = k // PAIRS
                        if k < UNITS:
                            score(g, k)
                        if k % PAIRS == 0 and t + 1 < NB:
                            make_qkv(g, par, t + 1)
                        if k == 12 and more:
                            make_qkv(g + 1, 1 - par, 0)
                        if 2 <= k < UNITS + 2:
                            transpose_p(g, k - 2)
                        if 4 <= k < UNITS + 4 and k % 2 == 0:
                            times_v(g, k - 4)
                        if k == 3:
                            pe.wait_ge(self.moved.sem, self.moved.at(g, 0))
                            transpose_qk(g, 1)
                        if k == 6 and more:
                            pe.wait_ge(self.qT_ready.sem, self.qT_ready.at(g, 2))
                            transpose_y(g + 1, 1 - par)
                        if k == 7:
                            if more:
                                pe.wait_ge(self.hT_ready.sem, self.hT_ready.at(g + 1, 2))
                            pe.wait_ge(self.qT_ready.sem, self.qT_ready.at(g, 2))
                            transpose_qk(g, 2)
                        if k == 8:
                            pe.wait_ge(self.qT_ready.sem, self.qT_ready.at(g, 3))
                            project(g, 0)
                        if k == 11:
                            pe.wait_ge(self.moved.sem, self.moved.at(g, 1))
                            transpose_qk(g, 3)
                        if k == 12:
                            pe.wait_ge(self.qT_ready.sem, self.qT_ready.at(g, 4))
                            project(g, 1)
                        if k == 15 and more:
                            pe.wait_ge(self.moved.sem, self.moved.at(g, 2))
                            transpose_qk(g + 1, 0)
                        if k == 16:
                            if more:
                                pe.wait_ge(self.qT_ready.sem, self.qT_ready.at(g + 1, 1))
                            pe.wait_ge(self.moved.sem, self.moved.at(g, 2))
                            project(g, 2)
                        if k == 20:
                            pe.wait_ge(self.moved.sem, self.moved.at(g, 3))
                            project(g, 3)

                pipeline(pe, first, head, body)

SPLIT = 3
PAIR_ROWS = SPLIT * SPLIT * HD
ROWS = PAIR_ROWS + SPLIT
GROUPS = HEADS // 4
PANE = 32
STEPS = 8
SLOTS = GROUPS * STEPS
ATOPS = NB * 4


class GlobalAttention:

    def __init__(self, ctx, nc, kind):
        sig = lambda n, per, unit=1: Signal(ctx, nc, f"{kind}_{n}", per, unit)
        self.kind, self.causal = kind, kind == "causal"
        self.norm = Norm(ctx, nc, kind + "_norm")
        self.xs_ready = sig("xs_ready", 1)
        self.hT_ps = sig("hT_in_psum", 1)
        self.hT_ready = sig("hT_ready", 1)
        self.made = sig("qkv_in_psum", 3 if self.causal else 5)
        self.turn = sig("turn_step", 4)
        self.qk_ready = sig("qk_ready", 2)
        self.v_ready = sig("v_ready", 1)
        self.part = sig("part_ready", 6)
        self.rest = sig("rest_ready", 4)
        self.spread_q = sig("spread_q", 9, 16)
        self.spread_k = sig("spread_k", 9, 16)
        self.a_scores = sig("a_scores", GROUPS * ATOPS)
        self.top = sig("top", GROUPS * ATOPS)
        self.top_step = sig("top_step", GROUPS * (6 if self.causal else 5))
        self.mT_ps = sig("mT_in_psum", GROUPS)
        self.mT_ready = sig("mT_ready", GROUPS)
        self.m_spread = sig("m_spread", GROUPS, 16)
        self.floor_ps = sig("floor_in_psum", HEADS)
        self.floor = sig("floor_ready", HEADS)
        self.b_scores = sig("b_scores", SLOTS)
        self.clipped = sig("clipped", 2 * SLOTS)
        self.probs = sig("probs", SLOTS)
        self.pv = sig("pv", 2 * GROUPS)
        self.oT_ready = sig("oT_ready", GROUPS)
        self.o_ps = sig("o_in_psum", NB)
        self.out_step = sig("out_step", NB * 8 - 2 if self.causal else NB)
        self.on_ready = sig("on_ready", NB)
        self.vsum_ps = sig("vsum_in_psum", 1)
        self.vsum_ready = sig("vsum_ready", 1)
        self.vsum_step = sig("vsum_step", 3)
        self.away_ready = sig("away_ready", 1)
        self.onT_ps = sig("onT_in_psum", 1)
        self.onT_ready = sig("onT_ready", 1)
        self.proj = sig("proj_ready", 1)
        self.biased = sig("biased", 1)
        self.moved = sig("result_stored", 1)
        self.setup = ctx.enter_context(nc.semaphore(kind + "_setup"))
        self.tables_made = ctx.enter_context(nc.semaphore(kind + "_tables_made"))

    def emit(self, nc, run, X, W):
        assert run == 0
        n, first, causal, kind = self.norm, 0, self.causal, self.kind
        wq, wproj = W[kind + "_wqkv"], W[kind + "_wproj"]
        with ExitStack() as ctx:
            pb = lambda name, banks=1: ctx.enter_context(nc.psum_tensor(f"{kind}_{name}", [P, banks * SEQ], F32))
            sb = lambda name, s, dt=F32: ctx.enter_context(nc.sbuf_tensor(f"{kind}_{name}", s, dt))
            n.buffers(ctx, nc, run)
            a_bank = [pb("a0"), pb("a1")]
            b_bank = [pb("b0", 2), pb("b1", 2)]
            o_bank = pb("o")
            m_bank = pb("m")
            m16 = m_bank[:, :].bitcast(BF16)
            xs = sb("xs", [P, 2, NB, DIM])
            hT = sb("hTs", [P, SEQ])
            full = sb("full", [P, 2, SEQ])
            t1 = sb("t1", [P, SEQ])
            t2 = sb("t2", [P, SEQ])
            rest = sb("rest", [P, SEQ])
            parts = sb("parts", [P, 2, SPLIT, SEQ], BF16)
            rep = {x: sb(x + "_rows", [ROWS + 1, 2, HEADS, SEQ], BF16) for x in "qk"}
            vs = sb("vs", [P, 2, NB, HEADS, PANE])
            tops = sb("tops", [P, 2, NB, HEADS])
            toprest = sb("toprest", [P, NB, 4])
            topp = sb("topp", [P, NB, SPLIT, 4], BF16)
            mT = sb("mT", [SPLIT * 4, SEQ], BF16)
            pT = sb("pT", [P, 2, 4, 2, SEQ] if not causal else [P, 2, 4, 2, SEQ])
            oT = sb("oT", [P, GROUPS, SEQ])
            den = sb("den", [P, 2, 3, HEADS])
            on = sb("on", [P, NB, HEADS, HD])
            onT = sb("onT", [P, SEQ])
            total = sb("total", [P, NB, DIM])
            if causal:
                floor = sb("floor", [P, 4, SEQ])
                away = sb("away", [P, NB, HEADS])
                vsum = sb("vsum", [P, NB, HEADS, HD])
                ot = sb("ot", [P, 2, 2, HEADS, HD])
                ones_rows = sb("ones_rows", [ROWS + 1, P], BF16)
                diag = sb("diag", [P, 2, P], BF16)
            block = ctx.enter_context(nc.Block())

            def width(kb):
                return P * kb if causal else 0

            def a_unit(s, i):
                a = 2 * s + i + 2 * ATOPS
                return a >= GROUPS * ATOPS, a % (GROUPS * ATOPS)

            HEAD = dict(norm=0, transpose=4, q=5, k=6, v=7) if causal else dict(norm=0, transpose=2, q=3, qs=4, k=5, ks=6, v=7)
            TOP = (2, 3, 4) if causal else (0, 1, 2)

            @block.sync
            def _(sp):
                for s in (self.spread_q, self.spread_k, self.m_spread):
                    sp.sem_inc(s.sem, s.credit())
                sp.wait_ge(self.setup, 1)

                def spread(g, par):
                    for x, (name, signal) in enumerate((("q", self.spread_q), ("k", self.spread_k))):
                        sp.wait_ge(self.part.sem, self.part.at(g, 3 * x + 3))
                        for i in range(SPLIT):
                            for j in range(SPLIT):
                                r = (SPLIT * i + j) * HD
                                sp.dma_start(rep[name][r:r + HD, par, :, :],
                                                              parts[:, x, (i, j)[x], :]).then_inc(signal.sem, 16)

                def spread_top(g, par, gr):
                    sp.wait_ge(self.mT_ready.sem, self.mT_ready.at(g, gr + 1))
                    sp.dma_start(rep["q"][PAIR_ROWS:ROWS, par, 4 * gr:4 * gr + 4, :], mT[:, :]).then_inc(self.m_spread.sem, 16)

                def head(g, par):
                    spread(g, par)
                    spread_top(g, par, 0)
                    spread_top(g, par, 1)

                def body(g, par, more):
                    if more:
                        spread(g + 1, 1 - par)
                    spread_top(g, par, 2)
                    spread_top(g, par, 3)
                    if more:
                        spread_top(g + 1, 1 - par, 0)
                        spread_top(g + 1, 1 - par, 1)

                pipeline(sp, first, head, body)

            @block.gpsimd
            def _(pl):
                for s in (n.rstd_ready, self.rest):
                    pl.sem_inc(s.sem, s.credit())
                pl.memset(rep["k"][64:ROWS + 1, :, :, :], 1.0).then_inc(self.setup, 1)
                pl.wait_ge(self.setup, 1)
                pl.memset(rep["q"][64:ROWS + 1, :, :, :], 0.0).then_inc(self.setup, 1)
                pl.wait_ge(self.setup, 2)
                pl.memset(vs[:, :, :, :, :], 0.0).then_inc(self.setup, 1)
                pl.wait_ge(self.setup, 3)
                pl.memset(vs[:, :, :, :, HD:HD + 1], 1.0).then_inc(self.setup, 1)

                def head(g, par):
                    n.pool(pl, g, W["minus_half"])
                    for x in range(2):
                        for i in range(2):
                            pl.wait_ge(self.part.sem, self.part.at(g, 3 * x + i + 1))
                            src = full[:, x, :] if i == 0 else rest[:, :]
                            pl.tensor_tensor(rest[:, :], src, parts[:, x, i, :], ALU.subtract)\
                                .then_inc(self.rest.sem, 1)

                def body(g, par, more):
                    if more:
                        head(g + 1, 1 - par)

                pipeline(pl, first, head, body)

            @block.vector
            def _(v):
                for s in (*n.of_vector, self.xs_ready, self.turn, self.top, self.top_step, self.clipped,
                          self.out_step, self.on_ready, self.vsum_step, self.biased, self.moved):
                    v.sem_inc(s.sem, s.credit())
                if not causal:
                    v.sem_inc(self.qk_ready.sem, self.qk_ready.credit())
                if causal:
                    v.tensor_copy(ones_rows[0:ROWS, :], W["ones_rows"]).then_inc(self.tables_made, 1)
                    v.tensor_copy(diag[:, :, :], W["diag"]).then_inc(self.tables_made, 1)

                def tokens(g, par):
                    v.wait_ge(self.moved.sem, self.moved.at(g, -1))
                    v.tensor_scalar(xs[:, par, :, :], slot(X, g, first), 1.0, None, ALU.mult)\
                        .then_inc(self.xs_ready.sem, 1)
                    v.wait_ge(self.xs_ready.sem, self.xs_ready.at(g, 1))
                    n.vector(v, g, par, xs[:, par, :, :], lambda: v.wait_ge(self.hT_ps.sem, self.hT_ps.at(g, -1)))

                def turn(g, x, swapped):
                    if not swapped:
                        v.wait_ge(self.made.sem, self.made.at(g, 2 * x + 1))
                        v.wait_ge(self.qk_ready.sem, self.qk_ready.at(g, x))
                        v.tensor_tensor(t1[:, :], m_bank[:, :], W["rope"][:, x, 0, :], ALU.mult)\
                            .then_inc(self.turn.sem, 1)
                    else:
                        v.wait_ge(self.made.sem, self.made.at(g, 2 * x + 2))
                        v.tensor_tensor(t2[:, :], m_bank[:, :], W["rope"][:, x, 1, :], ALU.mult)\
                            .then_inc(self.turn.sem, 1)
                        v.wait_ge(self.turn.sem, self.turn.at(g, 2 * x + 2))
                        v.wait_ge(self.rest.sem, self.rest.at(g, 2 * x + 1 - 4))
                        v.wait_ge(self.part.sem, self.part.at(g, 3 * x + 1 - 6))
                        v.tensor_tensor(full[:, x, :], t1[:, :], t2[:, :], ALU.add).then_inc(self.qk_ready.sem, 1)

                def top(g, par, a):
                    gr, b, j = a // ATOPS, a % ATOPS // 4, a % 4
                    v.wait_ge(self.a_scores.sem, self.a_scores.at(g, a + 1))
                    if a % ATOPS == 0:
                        v.wait_ge(self.top_step.sem, self.top_step.at(g, gr * self.top_step.per // GROUPS - 2 * self.top_step.per))
                    keys = P * (b + 1) if causal else SEQ
                    h = 4 * gr + j
                    v.tensor_reduce(tops[:, par, b, h:h + 1], a_bank[a % 2][:, 0:keys], AX.X, ALU.max,
                                                       negate=True).then_inc(self.top.sem, 1)

                def top_parts(g, par, gr):
                    n0 = gr * (self.top_step.per // GROUPS)
                    v.wait_ge(self.top.sem, self.top.at(g, ATOPS * (gr + 1)))
                    m = tops[:, par, :, 4 * gr:4 * gr + 4]
                    if causal:
                        v.wait_ge(self.away_ready.sem, self.away_ready.at(g, -1))
                        v.tensor_scalar(m, m, -100.0, 100.0, ALU.max, ALU.min).then_inc(self.top_step.sem, 1)
                        n0 += 1
                        v.wait_ge(self.top_step.sem, self.top_step.at(g, n0))
                    v.wait_ge(self.mT_ps.sem, self.mT_ps.at(g, gr))
                    for i in range(SPLIT):
                        src = m if i == 0 else toprest[:, :, :]
                        v.tensor_copy(topp[:, :, i, :], src).then_inc(self.top_step.sem, 1)
                        v.wait_ge(self.top_step.sem, self.top_step.at(g, n0 + 2 * i + 1))
                        if i < SPLIT - 1:
                            v.tensor_tensor(toprest[:, :, :], src, topp[:, :, i, :], ALU.subtract)\
                                .then_inc(self.top_step.sem, 1)
                            v.wait_ge(self.top_step.sem, self.top_step.at(g, n0 + 2 * i + 2))

                def clip(g, s):
                    gr, c, j = s // STEPS, s % STEPS // 4, s % 4
                    v.wait_ge(self.b_scores.sem, self.b_scores.at(g, s + 1))
                    v.wait_ge(self.floor.sem, self.floor.at(g, 4 * gr + j + 1))
                    v.wait_ge(self.pv.sem, self.pv.at(g, 2 * gr + c - 1))
                    for i in range(2):
                        q0 = width(2 * c + i)
                        v.scalar_tensor_tensor(
                            out=pT[:, c, j, i, q0:SEQ], in0=b_bank[s % 2][:, i * SEQ + q0:(i + 1) * SEQ], scalar=0.0,
                            in1=floor[:, j, q0:SEQ], op0=ALU.min, op1=ALU.max).then_inc(self.clipped.sem, 1)

                def v_sums(g):
                    v.wait_ge(self.vsum_ready.sem, self.vsum_ready.at(g, 1))
                    for i, b in enumerate((2, 1, 0)):
                        v.tensor_tensor(vsum[:, b, :, :], vsum[:, b, :, :], vsum[:, b + 1, :, :],
                                                                 ALU.add).then_inc(self.vsum_step.sem, 1)
                        v.wait_ge(self.vsum_step.sem, self.vsum_step.at(g, i + 1))

                def output(g, par, b):
                    o3 = a_bank[b % 2][:, :].rearrange("p (h c) -> p h c", c=PANE)
                    o, sums = o3[:, :, 0:HD], o3[:, :, HD]
                    bc = lambda t: t.unsqueeze(2).broadcast_to([P, HEADS, HD])
                    n0 = b * (8 if causal else 1)
                    d = lambda i: den[:, b % 2, i, :]
                    v.wait_ge(self.o_ps.sem, self.o_ps.at(g, b + 1))
                    v.wait_ge(self.onT_ps.sem, self.onT_ps.at(g, 0))
                    v.wait_ge(self.on_ready.sem, self.on_ready.at(g, b - 1))
                    if not causal:
                        v.reciprocal(d(0), sums).then_inc(self.out_step.sem, 1)
                        v.wait_ge(self.out_step.sem, self.out_step.at(g, n0 + 1))
                        v.tensor_tensor(on[:, b, :, :], o, bc(d(0)), ALU.mult).then_inc(self.on_ready.sem, 1)
                        return
                    v.scalar_tensor_tensor(out=d(0), in0=away[:, b, :], scalar=float(SEQ - P * (b + 1)), in1=sums,
                                           op0=ALU.mult, op1=ALU.add).then_inc(self.out_step.sem, 1)
                    v.wait_ge(self.out_step.sem, self.out_step.at(g, n0 + 1))
                    v.tensor_scalar(d(1), d(0), 1e-6, 1e-8, ALU.add, ALU.mult).then_inc(self.out_step.sem, 1)
                    v.wait_ge(self.out_step.sem, self.out_step.at(g, n0 + 2))
                    v.scalar_tensor_tensor(out=d(2), in0=d(1), scalar=float(SEQ), in1=d(0), op0=ALU.mult,
                                           op1=ALU.add).then_inc(self.out_step.sem, 1)
                    v.wait_ge(self.out_step.sem, self.out_step.at(g, n0 + 3))
                    v.reciprocal(d(2), d(2)).then_inc(self.out_step.sem, 1)
                    u, w = ot[:, b % 2, 0, :, :], ot[:, b % 2, 1, :, :]
                    v.tensor_tensor(u, vsum[:, 0, :, :], bc(d(1)), ALU.mult).then_inc(self.out_step.sem, 1)
                    v.wait_ge(self.out_step.sem, self.out_step.at(g, n0 + 5))
                    if b < NB - 1:
                        v.tensor_tensor(w, vsum[:, b + 1, :, :], bc(away[:, b, :]), ALU.mult)\
                            .then_inc(self.out_step.sem, 1)
                        v.wait_ge(self.out_step.sem, self.out_step.at(g, n0 + 6))
                        v.tensor_tensor(u, u, w, ALU.add).then_inc(self.out_step.sem, 1)
                        v.wait_ge(self.out_step.sem, self.out_step.at(g, n0 + 7))
                        n0 += 2
                    v.tensor_tensor(w, o, u, ALU.add).then_inc(self.out_step.sem, 1)
                    v.wait_ge(self.out_step.sem, self.out_step.at(g, n0 + 6))
                    v.tensor_tensor(on[:, b, :, :], w, bc(d(2)), ALU.mult).then_inc(self.on_ready.sem, 1)

                def result(g, par):
                    v.wait_ge(self.proj.sem, self.proj.at(g, 1))
                    out3 = m_bank[:, :].rearrange("p (b d) -> p b d", b=NB)
                    v.wait_ge(self.moved.sem, self.moved.at(g, 0))
                    if causal:
                        v.tensor_tensor(slot(X, g, first), out3, xs[:, par, :, :], ALU.add)\
                            .then_inc(self.moved.sem, 1)
                    else:
                        v.tensor_tensor(
                            total[:, :, :], out3, W["b_proj"].unsqueeze(1).broadcast_to([P, NB, DIM]), ALU.add)\
                                .then_inc(self.biased.sem, 1)
                        v.wait_ge(self.biased.sem, self.biased.at(g, 1))
                        v.tensor_tensor(slot(X, g, first), total[:, :, :], xs[:, par, :, :], ALU.add)\
                            .then_inc(self.moved.sem, 1)

                def head_step(g, par, name):
                    if name == "norm":
                        tokens(g, par)
                    if not causal and name in ("q", "qs", "k", "ks"):
                        turn(g, int(name[0] == "k"), name[-1] == "s")

                def head(g, par):
                    for name in HEAD:
                        head_step(g, par, name)
                    for gr in range(2):
                        for a in range(ATOPS * gr, ATOPS * (gr + 1)):
                            top(g, par, a)
                        top_parts(g, par, gr)

                def body(g, par, more):
                    for s in range(SLOTS):
                        gr, u = s // STEPS, s % STEPS
                        if u == TOP[0] and gr >= 1:
                            later, which = gr + 1 >= GROUPS, (gr + 1) % GROUPS
                            if not later:
                                top_parts(g, par, which)
                            elif more:
                                top_parts(g + 1, 1 - par, which)
                        if causal:
                            clip(g, s)
                        for i in range(2):
                            later, a = a_unit(s, i)
                            if not later:
                                top(g, par, a)
                            elif more:
                                top(g + 1, 1 - par, a)
                        if more:
                            for name, at in HEAD.items():
                                if at == s:
                                    head_step(g + 1, 1 - par, name)
                    if more:
                        top_parts(g + 1, 1 - par, 1)
                    if causal:
                        v_sums(g)
                        v.wait_ge(self.away_ready.sem, self.away_ready.at(g, 1))
                    for b in range(NB):
                        output(g, par, b)
                    result(g, par)

                pipeline(v, first, head, body)

            @block.scalar
            def _(act):
                for s in (self.hT_ready, self.v_ready, self.part, self.mT_ready, self.floor, self.probs, self.oT_ready,
                          self.vsum_ready, self.away_ready, self.onT_ready):
                    act.sem_inc(s.sem, s.credit())
                if causal:
                    act.sem_inc(self.qk_ready.sem, self.qk_ready.credit())
                act.wait_ge(self.setup, 4)
                copy = lambda o, i: act.activation(o, i, ACT.Copy)

                def split(g, x):
                    act.wait_ge(self.qk_ready.sem, self.qk_ready.at(g, x + 1))
                    for i in range(SPLIT):
                        act.wait_ge((self.spread_q, self.spread_k)[x].sem, (self.spread_q, self.spread_k)[x].at(g, 0))
                        if i:
                            act.wait_ge(self.rest.sem, self.rest.at(g, 2 * x + i))
                        copy(parts[:, x, i, :], full[:, x, :] if i == 0 else rest[:, :]).then_inc(self.part.sem, 1)

                def head_step(g, par, name):
                    if name == "transpose":
                        act.wait_ge(self.hT_ps.sem, self.hT_ps.at(g, 1))
                        act.wait_ge(self.made.sem, self.made.at(g, 0))
                        copy(hT[:, :], m_bank[:, :]).then_inc(self.hT_ready.sem, 1)
                    elif name in ("q", "k") and causal:
                        x = int(name == "k")
                        act.wait_ge(self.made.sem, self.made.at(g, x + 1))
                        act.wait_ge(self.rest.sem, self.rest.at(g, 2 * x + 1 - 4))
                        act.activation(full[:, x, :], m_bank[:, :], ACT.Copy,
                                                               scale=1.0 if x else float(HD) ** -0.5)\
                                                                   .then_inc(self.qk_ready.sem, 1)
                        act.wait_ge(self.qk_ready.sem, self.qk_ready.at(g, x + 1))
                        split(g, x)
                    elif name in ("qs", "ks") and not causal:
                        split(g, int(name == "ks"))
                    elif name == "v":
                        act.wait_ge(self.made.sem, self.made.at(g, self.made.per))
                        act.wait_ge(self.pv.sem, self.pv.at(g, -2 * GROUPS))
                        if causal:
                            act.wait_ge(self.vsum_ps.sem, self.vsum_ps.at(g, -1))
                        copy(vs[:, par, :, :, 0:HD],
                                                    m_bank[:, :].rearrange("p (b h d) -> p b h d", b=NB, d=HD))\
                                                        .then_inc(self.v_ready.sem, 1)

                def take_mT(g, gr):
                    act.wait_ge(self.mT_ps.sem, self.mT_ps.at(g, gr + 1))
                    act.wait_ge(self.m_spread.sem, self.m_spread.at(g, gr))
                    copy(mT[:, :], m16[0:SPLIT * 4, 0:SEQ]).then_inc(self.mT_ready.sem, 1)

                def take_floor(g, h):
                    act.wait_ge(self.floor_ps.sem, self.floor_ps.at(g, h + 1))
                    act.wait_ge(self.clipped.sem, self.clipped.at(g, 2 * STEPS * (h // 4)))
                    act.activation(floor[:, h % 4, :], m_bank[:, :], ACT.Identity,
                                                        bias=W["minus_100"]).then_inc(self.floor.sem, 1)

                def exp(g, s):
                    gr, c, j = s // STEPS, s % STEPS // 4, s % 4
                    if causal:
                        act.wait_ge(self.clipped.sem, self.clipped.at(g, 2 * s + 2))
                        for i in range(2):
                            q0 = width(2 * c + i)
                            p_ = pT[:, c, j, i, q0:SEQ]
                            ins = act.activation(p_, p_, ACT.Exp)
                        ins.then_inc(self.probs.sem, 1)
                    else:
                        act.wait_ge(self.b_scores.sem, self.b_scores.at(g, s + 1))
                        act.wait_ge(self.pv.sem, self.pv.at(g, 2 * gr + c - 1))
                        act.activation(pT[:, c, j, :, :].rearrange("p a b -> p (a b)"),
                                                            b_bank[s % 2][:, :], ACT.Exp).then_inc(self.probs.sem, 1)

                def take_o(g, gr):
                    act.wait_ge(self.pv.sem, self.pv.at(g, 2 * gr + 2))
                    act.wait_ge(self.o_ps.sem, self.o_ps.at(g, 0))
                    copy(oT[:, gr, :], o_bank[:, :]).then_inc(self.oT_ready.sem, 1)

                def head(g, par):
                    for name in HEAD:
                        head_step(g, par, name)
                    for gr in range(2):
                        take_mT(g, gr)
                    if causal:
                        take_floor(g, 0)

                def body(g, par, more):
                    for s in range(SLOTS + 2):
                        gr, u = s // STEPS, s % STEPS
                        if s < SLOTS:
                            if causal and s > 0 and u < 4:
                                take_floor(g, 4 * gr + u)
                            exp(g, s)
                            if more:
                                for name, at in HEAD.items():
                                    if at == s:
                                        head_step(g + 1, 1 - par, name)
                            if u == TOP[2] and gr >= 1:
                                later, which = gr + 1 >= GROUPS, (gr + 1) % GROUPS
                                if not later:
                                    take_mT(g, which)
                                elif more:
                                    take_mT(g + 1, which)
                        if s >= STEPS + 1 and (s - STEPS - 1) % STEPS == 0:
                            take_o(g, (s - STEPS - 1) // STEPS)
                    if more:
                        take_mT(g + 1, 1)
                    if causal:
                        act.wait_ge(self.vsum_ps.sem, self.vsum_ps.at(g, 1))
                        act.wait_ge(self.on_ready.sem, self.on_ready.at(g, 0))
                        copy(vsum[:, :, :, :],
                                                       m_bank[:, :].rearrange("p (b h d) -> p b h d", b=NB, d=HD))\
                                                           .then_inc(self.vsum_ready.sem, 1)
                        act.wait_ge(self.top_step.sem, self.top_step.at(g, self.top_step.per))
                        act.activation(away[:, :, :], tops[:, par, :, :], ACT.Exp,
                                                                 bias=W["minus_100"]).then_inc(self.away_ready.sem, 1)
                    act.wait_ge(self.onT_ps.sem, self.onT_ps.at(g, 1))
                    act.wait_ge(self.proj.sem, self.proj.at(g, 0))
                    copy(onT[:, :], m_bank[:, :]).then_inc(self.onT_ready.sem, 1)
                    if causal and more:
                        take_floor(g + 1, 0)

                pipeline(act, first, head, body)

            @block.tensor
            def _(pe):
                for s in (self.hT_ps, self.made, self.a_scores, self.mT_ps, self.floor_ps, self.b_scores, self.pv,
                          self.o_ps, self.vsum_ps, self.onT_ps, self.proj):
                    pe.sem_inc(s.sem, s.credit())
                pe.wait_ge(self.setup, 4)
                if causal:
                    pe.wait_ge(self.tables_made, 2)


                def head_step(g, par, name):
                    mul = lambda o, l, r: pe.matmul(o, l, r, start=True, stop=True)
                    col = lambda i: slice(i * P, (i + 1) * P)
                    if name == "transpose":
                        for b in range(NB):
                            pe.wait_ge(n.out_ready.sem, n.out_ready.at(g, b + 1))
                            ins = pe.transpose(m_bank[:, col(b)], n.out[:, par, b, :], W["ident"])
                        ins.then_inc(self.hT_ps.sem, 1)
                    elif name in ("q", "k", "qs", "ks"):
                        x = int(name[0] == "k")
                        if causal:
                            if len(name) == 2:
                                return
                            if x:
                                pe.wait_ge(self.qk_ready.sem, self.qk_ready.at(g, 1))
                            i = x
                        else:
                            if name != "q":
                                pe.wait_ge(self.turn.sem, self.turn.at(g, 2 * x + len(name) - 1))
                            i = x + (2 if len(name) == 2 else 0)
                        pe.wait_ge(self.hT_ready.sem, self.hT_ready.at(g, 1))
                        mul(m_bank[:, :], wq[:, col(i)], hT[:, :]).then_inc(self.made.sem, 1)
                    elif name == "v":
                        if causal:
                            pe.wait_ge(self.qk_ready.sem, self.qk_ready.at(g, 2))
                        else:
                            pe.wait_ge(self.turn.sem, self.turn.at(g, 4))
                        i = 2 if causal else 4
                        for b in range(NB):
                            ins = mul(m_bank[:, col(b)], hT[:, col(b)], wq[:, col(i)])
                        ins.then_inc(self.made.sem, 1)

                def a_scores(g, par, a):
                    gr, b, j = a // ATOPS, a % ATOPS // 4, a % 4
                    h = 4 * gr + j
                    if a == 0:
                        pe.wait_ge(self.spread_q.sem, self.spread_q.at(g, 9))
                        pe.wait_ge(self.spread_k.sem, self.spread_k.at(g, 9))
                    bank = a_bank[a % 2]
                    pe.wait_ge(self.top.sem, self.top.at(g, a - 1))
                    if a in (2 * ATOPS, 2 * ATOPS + 1):
                        pe.wait_ge(self.on_ready.sem, self.on_ready.at(g, a - 2 * ATOPS - 1))
                    keys = P * (b + 1) if causal else SEQ
                    ins = pe.matmul(bank[:, 0:keys], rep["q"][0:PAIR_ROWS, par, h, b * P:(b + 1) * P],
                                    rep["k"][0:PAIR_ROWS, par, h, 0:keys], start=True, stop=not causal)
                    if causal:
                        ins = pe.matmul(bank[:, keys - P:keys], W["ident16"], diag[:, 0, :], start=False, stop=True)
                    ins.then_inc(self.a_scores.sem, 1)

                def transpose_tops(g, gr):
                    pe.wait_ge(self.top_step.sem, self.top_step.at(g, (gr + 1) * self.top_step.per // GROUPS))
                    for b in range(NB):
                        ins = pe.transpose(m16[0:SPLIT * 4, b * P:(b + 1) * P],
                                           topp[:, b, :, :].rearrange("p i j -> p (i j)"), W["ident16"])
                    ins.then_inc(self.mT_ps.sem, 1)

                def floors(g, par, h):
                    if h % 4:
                        pe.wait_ge(self.floor.sem, self.floor.at(g, h))
                    pe.wait_ge(self.m_spread.sem, self.m_spread.at(g, h // 4 + 1))
                    pe.matmul(m_bank[:, :], ones_rows[0:ROWS, :], rep["q"][0:ROWS, par, h, :],
                                                      start=True, stop=True).then_inc(self.floor_ps.sem, 1)

                def b_scores(g, par, s):
                    gr, c, j = s // STEPS, s % STEPS // 4, s % 4
                    h = 4 * gr + j
                    pe.wait_ge(self.m_spread.sem, self.m_spread.at(g, gr + 1))
                    if causal:
                        pe.wait_ge(self.clipped.sem, self.clipped.at(g, 2 * (s - 1)))
                    else:
                        pe.wait_ge(self.probs.sem, self.probs.at(g, s - 1))
                    for i in range(2):
                        kb = 2 * c + i
                        q0 = width(kb)
                        o = b_bank[s % 2][:, i * SEQ + q0:(i + 1) * SEQ]
                        ins = pe.matmul(o, rep["k"][0:ROWS, par, h, kb * P:(kb + 1) * P],
                                        rep["q"][0:ROWS, par, h, q0:SEQ], start=True, stop=not causal)
                        if causal:
                            ins = pe.matmul(o[:, 0:P], W["ident16"], diag[:, 1, :], start=False, stop=True)
                    ins.then_inc(self.b_scores.sem, 1)

                def times_v(g, par, e):
                    gr, c = e // 2, e % 2
                    pe.wait_ge(self.probs.sem, self.probs.at(g, 4 * e + 4))
                    if e == 0:
                        pe.wait_ge(self.v_ready.sem, self.v_ready.at(g, 1))
                    if c == 0:
                        pe.wait_ge(self.oT_ready.sem, self.oT_ready.at(g, gr))
                    for i in range(2):
                        kb = 2 * c + i
                        q0 = width(kb)
                        for j in range(4):
                            ins = pe.matmul(o_bank[PANE * j:PANE * (j + 1), q0:SEQ], vs[:, par, kb, 4 * gr + j, :],
                                            pT[:, c, j, i, q0:SEQ], start=(kb == 0), stop=(kb == NB - 1))
                    ins.then_inc(self.pv.sem, 1)

                def tail(g, par, more):
                    last = (g + 1, 2) if more else (g, GROUPS)
                    pe.wait_ge(self.mT_ready.sem, self.mT_ready.at(*last))
                    if causal:
                        pe.wait_ge(self.floor.sem, self.floor.at(g, HEADS))
                        for b in range(NB):
                            ins = pe.matmul(m_bank[:, b * P:(b + 1) * P], W["ones"],
                                            vs[:, par, b, :, 0:HD], start=True, stop=True)
                        ins.then_inc(self.vsum_ps.sem, 1)
                    pe.wait_ge(self.oT_ready.sem, self.oT_ready.at(g, GROUPS))
                    for b in range(NB):
                        if b < 2:
                            pe.wait_ge(self.top.sem, self.top.at(g + 1, (2 * ATOPS if more else 0) - 1 + b))
                        else:
                            pe.wait_ge(self.on_ready.sem, self.on_ready.at(g, b - 1))
                        for gr in range(GROUPS):
                            ins = pe.transpose(a_bank[b % 2][:, gr * P:(gr + 1) * P], oT[:, gr, b * P:(b + 1) * P],
                                               W["ident"])
                        ins.then_inc(self.o_ps.sem, 1)
                    if causal:
                        pe.wait_ge(self.vsum_ready.sem, self.vsum_ready.at(g, 1))
                    for b in range(NB):
                        pe.wait_ge(self.on_ready.sem, self.on_ready.at(g, b + 1))
                        ins = pe.transpose(m_bank[:, b * P:(b + 1) * P], on[:, b, :, :].rearrange("p h d -> p (h d)"),
                                           W["ident"])
                    ins.then_inc(self.onT_ps.sem, 1)
                    pe.wait_ge(self.onT_ready.sem, self.onT_ready.at(g, 1))
                    for b in range(NB):
                        ins = pe.matmul(m_bank[:, b * P:(b + 1) * P], onT[:, b * P:(b + 1) * P], wproj,
                                        start=True, stop=True)
                    ins.then_inc(self.proj.sem, 1)
                    if causal and more:
                        pe.wait_ge(self.moved.sem, self.moved.at(g, 1))
                        floors(g + 1, 1 - par, 0)

                def head(g, par):
                    for name in HEAD:
                        head_step(g, par, name)
                    for gr in range(2):
                        for a in range(ATOPS * gr, ATOPS * (gr + 1)):
                            a_scores(g, par, a)
                        if gr == 0:
                            pe.wait_ge(self.v_ready.sem, self.v_ready.at(g, 1))
                        else:
                            pe.wait_ge(self.mT_ready.sem, self.mT_ready.at(g, 1))
                        transpose_tops(g, gr)
                    if causal:
                        pe.wait_ge(self.mT_ready.sem, self.mT_ready.at(g, 2))
                        floors(g, par, 0)

                def body(g, par, more):
                    for s in range(SLOTS + 2):
                        gr, u = s // STEPS, s % STEPS
                        if s < SLOTS:
                            if causal and 0 < s and u < 4:
                                if s == STEPS and more:
                                    pe.wait_ge(self.v_ready.sem, self.v_ready.at(g + 1, 1))
                                elif u == 0:
                                    pe.wait_ge(self.mT_ready.sem, self.mT_ready.at(g, gr + 1))
                                floors(g, par, 4 * gr + u)
                            b_scores(g, par, s)
                            for i in range(2):
                                later, a = a_unit(s, i)
                                if not later:
                                    a_scores(g, par, a)
                                elif more:
                                    a_scores(g + 1, 1 - par, a)
                            if more:
                                for name, at in HEAD.items():
                                    if at == s:
                                        if name == "transpose" and causal:
                                            pe.wait_ge(self.floor.sem, self.floor.at(g, 4))
                                        elif name == "transpose":
                                            pe.wait_ge(self.moved.sem, self.moved.at(g, 0))
                                            pe.wait_ge(self.mT_ready.sem, self.mT_ready.at(g, 2))
                                        head_step(g + 1, 1 - par, name)
                            if u == TOP[1] and gr >= 1:
                                if causal:
                                    pe.wait_ge(self.floor.sem, self.floor.at(g, 4 * gr + 4))
                                elif gr > 1:
                                    pe.wait_ge(self.mT_ready.sem, self.mT_ready.at(g, gr + 1))
                                elif more:
                                    pe.wait_ge(self.v_ready.sem, self.v_ready.at(g + 1, 1))
                                else:
                                    pe.wait_ge(self.moved.sem, self.moved.at(g, 0))
                                later, which = gr + 1 >= GROUPS, (gr + 1) % GROUPS
                                if not later:
                                    transpose_tops(g, which)
                                elif more:
                                    transpose_tops(g + 1, which)
                        if s >= 5 and (s - 5) % 4 == 0:
                            times_v(g, par, (s - 5) // 4)
                    if more:
                        pe.wait_ge(self.mT_ready.sem, self.mT_ready.at(g + 1, 1))
                        transpose_tops(g + 1, 1)
                    tail(g, par, more)

                pipeline(pe, first, head, body)


MOE_ARRAYS = {"lower": [P, NB * EXPERTS, EXPERTS], "wg": [P, EXPERTS], "wup": [P, MOE_UP_COLS],
              "wdm": [P, 1 + EXPERTS, DIM], "wdt": [P, MOE_PASSES, DIM]}
CAUSAL_ARRAYS = {"causal_wqkv": [P, 3 * P], "causal_wproj": [P, DIM], "diag": [P, 2, P], "ones": [P, P],
                 "ones_rows": [ROWS, P], "minus_100": [P, 1]}
ROTARY_ARRAYS = {"rotary_wqkv": [P, 5 * P], "rotary_wproj": [P, DIM], "b_proj": [P, DIM], "rope": [P, 2, 2, SEQ]}
LOCAL_ARRAYS = {"wqkv": [P, DEPTH, 3 * INNER], "wo": [P, DEPTH, PAIRS, DIM], "qk_scale": [P, DEPTH, 2, LD],
                "qk_scale_swapped": [P, DEPTH, 2, LD], "turn_cos": [P, NB, 2, LD], "turn_sin": [P, NB, 2, LD],
                "band": [P, 2, 2 * BAND], "w1": [P, DEPTH, 2 * HID], "w2": [P, DEPTH, 3, DIM], "b1": [P, DEPTH, 6],
                "b2": [P, DEPTH, DIM], "ln_g": [P, DEPTH], "ln_b": [P, DEPTH]}
STAGES = ["moe", "causal", "moe", "local", "rotary", "local"]


class Loader:

    def __init__(self, ctx, nc, ins):
        self.nc, self.ins, self.count = nc, ins, 0
        self.sem = ctx.enter_context(nc.semaphore("loaded"))

    def load(self, ctx, name, arrays, sp):
        W = {}
        for n, s in arrays.items():
            W[n] = ctx.enter_context(self.nc.sbuf_tensor(f"{name}_{n}", s, F32))[tuple(slice(None) for _ in s)]
            sp.dma_start(W[n], self.ins[n]).then_inc(self.sem, 16)
            self.count += 16
        return W


def program(nc, ins, out, stages):
    with ExitStack() as ctx:
        sb = lambda n, s, dt=F32: ctx.enter_context(nc.sbuf_tensor(n, s, dt))
        X = sb("X", [P, NSEQ * NB, DIM])
        common = {"ident16": sb("ident16", [P, P], BF16)[:, :]}
        loader = Loader(ctx, nc, ins)
        stored = ctx.enter_context(nc.semaphore("stored"))
        made = ctx.enter_context(nc.semaphore("made"))
        with nc.Block() as block:
            @block.sync
            def _(sp):
                common.update(loader.load(ctx, "common", {"ident": [P, P], "minus_half": [P, 64]}, sp))
                x = ins["x"].rearrange("(n p) d -> p n d", p=P)
                for s in range(0, NSEQ, 4):
                    sp.dma_start(X[:, s * NB:(s + 4) * NB, :], x[:, s * NB:(s + 4) * NB, :]).then_inc(loader.sem, 16)
                    loader.count += 16
                sp.wait_ge(loader.sem, loader.count)
        with nc.Block() as block:
            @block.vector
            def _(v):
                v.tensor_copy(common["ident16"], common["ident"]).then_inc(made, 1)
                v.wait_ge(made, 1)
        kinds = {"moe": Moe(ctx, nc), "ffn": Geglu(ctx, nc), "attention": LocalAttention(ctx, nc)}
        arrays = {"moe": MOE_ARRAYS, "causal": CAUSAL_ARRAYS, "rotary": ROTARY_ARRAYS, "local": LOCAL_ARRAYS}
        runs = {}
        for number, kind in enumerate(stages):
            with ExitStack() as own:
                W = dict(common)
                with nc.Block() as block:
                    @block.sync
                    def _(sp):
                        W.update(loader.load(own, f"stage{number}", arrays[kind.split("_")[0]], sp))
                        sp.wait_ge(loader.sem, loader.count)
                run = runs.setdefault(kind.split("_")[0], 0)
                runs[kind.split("_")[0]] += 1
                if kind in ("causal", "rotary"):
                    GlobalAttention(own, nc, kind).emit(nc, 0, X, W)
                elif kind == "moe":
                    kinds["moe"].emit(nc, run, X, W)
                else:
                    local_tables(nc, own, W, made, 1 + run * (1 + 2 * DEPTH), number)
                    if kind == "local_attention":
                        kinds["attention"].emit(nc, 0, X, X, W, 1)
                    elif kind == "local_ffn":
                        kinds["ffn"].emit(nc, 0, X, X, W, 1, False)
                    else:
                        Y = own.enter_context(nc.sbuf_tensor(f"stage{number}_Y", [P, NSEQ * NB, DIM], F32))
                        for layer in range(DEPTH):
                            kinds["attention"].emit(nc, DEPTH * run + layer, X, Y, W, layer)
                            kinds["ffn"].emit(nc, DEPTH * run + layer, X, Y, W, layer, layer == DEPTH - 1)
        with nc.Block() as block:
            @block.sync
            def _(sp):
                y = out.rearrange("(n p) d -> p n d", p=P)
                for s in range(0, NSEQ, 4):
                    sp.dma_start(y[:, s * NB:(s + 4) * NB, :], X[:, s * NB:(s + 4) * NB, :]).then_inc(stored, 16)
                sp.wait_ge(stored, 16 * (NSEQ // 4))


def local_tables(nc, ctx, W, made, count, number):
    sb = lambda n, s, dt=F32: ctx.enter_context(nc.sbuf_tensor(f"stage{number}_{n}", s, dt))
    band16 = sb("band16", [P, 2, 2 * BAND], BF16)
    turn = {n: sb(n + "_scaled", [P, DEPTH, NB, 2, LD]) for n in ("turn_cos", "turn_sin")}
    with nc.Block() as block:
        @block.vector
        def _(v):
            v.tensor_copy(band16[:, :, :], W["band"]).then_inc(made, 1)
            for name, scale in (("turn_cos", "qk_scale"), ("turn_sin", "qk_scale_swapped")):
                for l in range(DEPTH):
                    v.tensor_tensor(turn[name][:, l, :, :, :], W[name],
                                    W[scale][:, l, :, :].unsqueeze(1).broadcast_to([P, NB, 2, LD]), ALU.mult)\
                        .then_inc(made, 1)
            v.wait_ge(made, count + 1 + 2 * DEPTH)
    W["band"] = band16[:, :, :]
    for name, t in turn.items():
        W[name] = t[:, :, :, :, :]


def constants():
    e = np.arange(EXPERTS)
    lower = (e[None, :] < e[:, None]).astype(np.float32)
    half = np.arange(0, LD, 2, dtype=np.float32)
    pos = np.arange(SEQ, dtype=np.float32)
    freqs = pos[:, None] * (1.0 / 10000.0 ** (half / LD)).astype(np.float32)[None, :]
    power = (pos - SEQ // 2) / float(WINDOW // 2)
    scale = ((half + 0.4 * LD) / (1.4 * LD))[None, :] ** power[:, None]
    two = lambda t: np.concatenate([t, t], 1)
    cos, scale = two(np.cos(freqs)), two(scale)
    sin = np.concatenate([-np.sin(freqs), np.sin(freqs)], 1)
    blocks = lambda q, k: np.ascontiguousarray(
        np.stack([8.0 * q, k], 1).reshape(NB, P, 2, LD).transpose(1, 0, 2, 3), dtype=np.float32)
    lag = np.arange(P)[:, None] + WINDOW - np.arange(BAND)[None, :]
    seen = (lag >= 0) & (lag <= WINDOW)
    band = np.stack([np.where(seen & (np.arange(BAND) >= WINDOW), 0, -1e30), np.where(seen, 0, -1e30)], 1)
    theta = (1.0 / 10000.0 ** (np.arange(0, HD, 2, dtype=np.float32) / HD) * 3.0).astype(np.float32)
    ang = pos[:, None] * theta[None, :]
    by_d = lambda t: np.repeat(t.T, HEADS, 0)
    rc = by_d(np.repeat(np.cos(ang), 2, 1))
    rs = by_d(np.stack([-np.sin(ang), np.sin(ang)], 2).reshape(SEQ, HD))
    f = np.float32(HD ** -0.5)
    later = np.where(np.arange(P)[None, :] > np.arange(P)[:, None], -1e30, 0)
    ones_rows = np.zeros((ROWS, P), np.float32)
    ones_rows[PAIR_ROWS:] = 1
    return {
        "rope": np.ascontiguousarray(np.stack([np.stack([rc * f, rs * f], 1), np.stack([rc, rs], 1)], 1), np.float32),
        "diag": np.ascontiguousarray(np.stack([later, later.T], 1), np.float32),
        "ones": np.ones((P, P), np.float32),
        "ones_rows": ones_rows,
        "minus_100": np.full((P, 1), -100.0, np.float32),
        "turn_cos": blocks(cos * scale, cos / scale),
        "turn_sin": blocks(sin * scale, sin / scale),
        "band": np.ascontiguousarray(np.concatenate([band, band], 2), dtype=np.float32),
        "ident": np.eye(P, dtype=np.float32),
        "lower": np.ascontiguousarray(np.broadcast_to(np.tile(lower, (NB, 1)), (P, NB * EXPERTS, EXPERTS))),
        "minus_half": np.full((P, 64), -0.5, np.float32),
    }


def layouts(a):
    up = np.concatenate([np.asarray(a["L0_ffn_w_up"]),
                         np.concatenate([a["L0_ffn_sg_gate"], a["L0_ffn_sg_up"]], 0)[None]], 0)
    down = np.concatenate([np.asarray(a["L0_ffn_w_down"]), np.asarray(a["L0_ffn_sg_down"])[None]], 0)
    S = EXPERTS
    rows = [up[S, 0:P], up[S, HALF:HALF + P], up[S, P:HALF], up[S, HALF + P:]]
    for p in range(EXPERTS // 2):
        for e in (2 * p, 2 * p + 1):
            rows += [up[e, 0:P], up[e, HALF:HALF + P]]
        rows += [up[e, o + P:o + HALF] for o in (0, HALF) for e in (2 * p, 2 * p + 1)]
    order = [S, *range(EXPERTS)]
    tail = np.zeros((MOE_PASSES, P, DIM), np.float32)
    tail[0, 0:TAIL] = down[S, :, P:].T
    for p in range(EXPERTS // 2):
        tail[1 + p] = np.concatenate([down[2 * p, :, P:].T, down[2 * p + 1, :, P:].T], 0)
    c = np.ascontiguousarray
    f32 = lambda n: np.asarray(a["L1_ffn_" + n])

    def blocks(rows):
        out = np.zeros((P, DEPTH, 3, rows.shape[-1]), np.float32)
        for j, (r, m) in enumerate(HID_BLOCKS):
            out[0:m, :, j] = rows[:, r:r + m].transpose(1, 0, 2)
        return out

    def global_qkv(w, swapped):
        q, k = (w[:, i * DIM:(i + 1) * DIM].reshape(DIM, HEADS, HD).transpose(0, 2, 1) for i in range(2))
        pairs = [x.reshape(DIM, HD // 2, 2, HEADS)[:, :, ::-1] for x in (q, k)] if swapped else []
        return c(np.concatenate([x.reshape(DIM, DIM) for x in (q, k, *pairs)] + [w[:, 2 * DIM:]], 1))

    scales = np.stack([f32("q_scale"), f32("k_scale")], 1)
    b1 = f32("b1")[:, :, None]
    spread = lambda t: c(np.broadcast_to(t, (P, *t.shape)))
    return {
        "causal_wqkv": global_qkv(np.asarray(a["L0_attn_w_qkv"]).T, False),
        "causal_wproj": c(np.asarray(a["L0_attn_w_proj"]).T),
        "rotary_wqkv": global_qkv(np.asarray(a["L1_attn_w_qkv"]), True),
        "rotary_wproj": c(np.asarray(a["L1_attn_w_proj"])),
        "b_proj": spread(np.asarray(a["L1_attn_b_proj"])),
        "wqkv": c(f32("wqkv").transpose(1, 0, 2)),
        "wo": c(f32("wo").reshape(DEPTH, PAIRS, P, DIM).transpose(2, 0, 1, 3)),
        "qk_scale": spread(scales),
        "qk_scale_swapped": spread(np.concatenate([scales[..., LD // 2:], scales[..., :LD // 2]], -1)),
        "w1": c(f32("w1").transpose(1, 0, 2)),
        "w2": blocks(f32("w2")),
        "b1": c(np.concatenate([blocks(b1[:, :HID]), blocks(b1[:, HID:])], 2)[..., 0]),
        "b2": spread(f32("b2")),
        "ln_g": c(f32("ln_g").T),
        "ln_b": c(f32("ln_b").T),
        "x": c(np.asarray(a["L0_attn_x"]).reshape(NSEQ * SEQ, DIM)),
        "wg": c(np.asarray(a["L0_ffn_gate_w"]).T),
        "wup": c(np.concatenate(rows, 0).T),
        "wdm": c(down[order, :, 0:P].transpose(2, 0, 1)),
        "wdt": c(tail.transpose(1, 0, 2)),
    }


def kernel(**inputs):
    import concourse.bacc as bacc
    from concourse.bass_utils import run_bass_kernel_spmd

    nc = bacc.Bacc("TRN2", target_bir_lowering=False, num_devices=1)
    arrays = {**layouts(inputs), **constants()}
    ins = {n: nc.dram_tensor(n + "_in", a.shape, mybir.dt.from_np(a.dtype), kind="ExternalInput").ap()
           for n, a in arrays.items()}
    out = nc.dram_tensor("out", (NSEQ * SEQ, DIM), F32, kind="ExternalOutput").ap()
    program(nc, ins, out, STAGES)
    r = run_bass_kernel_spmd(nc, [{n + "_in": a for n, a in arrays.items()}], core_ids=[0])
    return r.results[0]["out"].reshape(NSEQ, SEQ, DIM)
```

```python
from contextlib import ExitStack

import numpy as np

import concourse.bass as bass
from concourse import mybir

F32 = mybir.dt.float32
BF16 = mybir.dt.bfloat16
ALU = mybir.AluOpType
ACT = mybir.ActivationFunctionType
AX = mybir.AxisListType

P = 128
NSEQ, SEQ, DIM = 16, 512, 128
NB = SEQ // P
EXPERTS, HALF = 8, 192
TAIL = HALF - P
HEADS, HD = 16, 8
LH, LD = 8, 64
INNER = LH * LD
WINDOW = 64
HID = 341
DEPTH = 2
LN_EPS = 1e-5


class Signal:

    def __init__(self, ctx, nc, name, per, unit=1):
        self.sem = ctx.enter_context(nc.semaphore(name))
        self.per, self.unit = per, unit

    def at(self, g, n):
        return g * (self.per * self.unit) + n * self.unit

    def credit(self):
        return 2 * self.per * self.unit


class Norm:

    behind = 0

    def __init__(self, ctx, nc, name):
        sig = lambda n, per: Signal(ctx, nc, f"{name}_{n}", per)
        self.name = name
        self.stats_ready = sig("stats_ready", NB)
        self.moment = sig("moment", 6)
        self.veps_ready = sig("veps_ready", 1)
        self.rstd_ready = sig("rstd_ready", 1)
        self.out_ready = sig("out_ready", NB)
        self.of_vector = [self.stats_ready, self.moment, self.veps_ready, self.out_ready]

    def buffers(self, ctx, nc, stage):
        sb = lambda n, s: ctx.enter_context(nc.sbuf_tensor(f"{self.name}{stage}_{n}", s, F32))
        self.stats = sb("stats", [P, NB, 6])
        self.mean = sb("mean", [P, NB])
        self.diff = sb("diff", [P, NB])
        self.veps = sb("veps", [P, NB])
        self.rstd = sb("rstd", [P, NB])
        self.out = sb("out", [P, 2, NB, DIM])

    def vector(self, v, g, par, src, out_free):
        self.vector_stats(v, g, src)
        self.vector_apply(v, g, par, src, out_free)

    def vector_stats(self, v, g, src):
        g = g - self.behind
        for b in range(NB):
            v.bn_stats(self.stats[:, b, :], src[:, b, :]).then_inc(self.stats_ready.sem, 1)
        me, mo = self.stats[:, :, 1], self.stats[:, :, 4]
        v.wait_ge(self.stats_ready.sem, self.stats_ready.at(g, NB))
        v.wait_ge(self.rstd_ready.sem, self.rstd_ready.at(g, 0))
        v.wait_ge(self.moment.sem, self.moment.at(g, 0))
        v.tensor_tensor(self.veps[:, :], self.stats[:, :, 2], self.stats[:, :, 5], ALU.add)\
            .then_inc(self.moment.sem, 1)
        v.tensor_tensor(self.diff[:, :], me, mo, ALU.subtract).then_inc(self.moment.sem, 1)
        v.tensor_tensor(self.mean[:, :], me, mo, ALU.add).then_inc(self.moment.sem, 1)
        v.wait_ge(self.moment.sem, self.moment.at(g, 1))
        v.tensor_scalar(self.veps[:, :], self.veps[:, :], 1.0 / DIM, LN_EPS, ALU.mult, ALU.add)\
            .then_inc(self.moment.sem, 1)
        v.wait_ge(self.moment.sem, self.moment.at(g, 2))
        v.scalar_tensor_tensor(out=self.diff[:, :], in0=self.diff[:, :], scalar=0.25, in1=self.diff[:, :],
                                    op0=ALU.mult, op1=ALU.mult).then_inc(self.moment.sem, 1)
        v.wait_ge(self.moment.sem, self.moment.at(g, 3))
        v.tensor_scalar(self.mean[:, :], self.mean[:, :], 0.5, None, ALU.mult).then_inc(self.moment.sem, 1)
        v.wait_ge(self.moment.sem, self.moment.at(g, 5))
        v.tensor_tensor(self.veps[:, :], self.veps[:, :], self.diff[:, :], ALU.add).then_inc(self.veps_ready.sem, 1)

    def vector_apply(self, v, g, par, src, out_free):
        out_free()
        g = g - self.behind
        v.wait_ge(self.moment.sem, self.moment.at(g, 6))
        v.wait_ge(self.rstd_ready.sem, self.rstd_ready.at(g, 1))
        for b in range(NB):
            v.tensor_scalar(self.out[:, par, b, :], src[:, b, :], self.mean[:, b:b + 1],
                                                     self.rstd[:, b:b + 1], ALU.subtract, ALU.mult)\
                                                         .then_inc(self.out_ready.sem, 1)

    def pool(self, pl, g, minus_half):
        pl.wait_ge(self.out_ready.sem, self.out_ready.at(g, 0))
        g = g - self.behind
        pl.wait_ge(self.veps_ready.sem, self.veps_ready.at(g, 1))
        pl.tensor_tensor(self.rstd[:, :], self.veps[:, :], minus_half[:, 0:NB], ALU.pow)\
            .then_inc(self.rstd_ready.sem, 1)


def pipeline(eng, first, head, body):
    head(first + 2, 0)
    with eng.Fori(first + 2, first + NSEQ, 2) as g:
        body(g, 0, True)
        body(g + 1, 1, True)
    body(first + NSEQ, 0, True)
    body(first + NSEQ + 1, 1, False)


def due(s, slots, offset, count, every=1):
    return [(d, j) for d in (-1, 0, 1) for j in range(count) if every * j + offset == s - slots * d]


def modulo_pipeline(eng, first, body):
    body(first + 1, 1, (1,))
    body(first + 2, 0, (0, 1))
    with eng.Fori(first + 3, first + NSEQ, 2) as g:
        body(g, 1, (-1, 0, 1))
        body(g + 1, 0, (-1, 0, 1))
    body(first + NSEQ + 1, 1, (-1, 0))
    body(first + NSEQ + 2, 0, (-1,))


def slot(T, g, first, b=0, n=NB):
    return T[:, bass.ds((g - (first + 2)) * NB + b, n), :]


MOE_UNITS = [(0, P), (0, TAIL)] + [(1 + p, P) for p in range(EXPERTS // 2) for _ in range(3)]
MOE_PASSES = 1 + EXPERTS // 2
MOE_PASS_UNITS = [[u for u, (q, _) in enumerate(MOE_UNITS) if q == p] for p in range(MOE_PASSES)]
MOE_UP_COLS = sum(2 * m for _, m in MOE_UNITS)


class Moe:

    def __init__(self, ctx, nc):
        sig = lambda n, per: Signal(ctx, nc, f"moe_{n}", per)
        self.norm = Norm(ctx, nc, "moe_norm")
        self.xs_ready = sig("xs_ready", 1)
        self.hT_ps = sig("hT_in_psum", 1)
        self.hT_ready = sig("hT_ready", 1)
        self.logits = sig("logits", 1)
        self.gate_step = sig("gate_step", 13)
        self.ex_ready = sig("ex_ready", 1)
        self.up = sig("up_ready", len(MOE_UNITS))
        self.silu = sig("silu_ready", len(MOE_UNITS))
        self.hid = sig("hidden_ready", len(MOE_UNITS))
        self.down = sig("down_ready", 1 + EXPERTS)
        self.accd = sig("accumulated", NB * (1 + EXPERTS))

    def emit(self, nc, run, X, W):
        n, first = self.norm, run * NSEQ
        with ExitStack() as ctx:
            pb = lambda name: ctx.enter_context(nc.psum_tensor(f"moe{run}_{name}", [P, SEQ], F32))
            sb = lambda name, s, dt=F32: ctx.enter_context(nc.sbuf_tensor(f"moe{run}_{name}", s, dt))
            n.buffers(ctx, nc, run)
            gate_bank, up_bank = [pb("g0"), pb("g1")], [pb("u0"), pb("u1")]
            down_bank = [pb("d0"), pb("d1")]
            hT_bank, lg_bank = pb("hT"), pb("lg")
            xs = sb("xs", [P, 2, NB, DIM])
            hT = sb("hTs", [P, 2, SEQ])
            self.lg = sb("lgs", [P, NB, EXPERTS])
            self.gt = sb("gt", [P, NB * EXPERTS, EXPERTS])
            self.ge = sb("ge", [P, NB * EXPERTS, EXPERTS])
            self.rank = sb("rank", [P, NB, EXPERTS])
            self.top = sb("top", [P, NB])
            self.ex = sb("ex", [P, NB, EXPERTS])
            self.den = sb("den", [P, NB])
            self.comb = sb("comb", [P, 2, NB, EXPERTS])
            sg = sb("sg", [P, 2, SEQ])
            h = sb("h", [P, 2, 3, SEQ])
            acc = sb("acc", [P, NB, DIM])
            block = ctx.enter_context(nc.Block())

            @block.gpsimd
            def _(pl):
                if run == 0:
                    pl.sem_inc(n.rstd_ready.sem, n.rstd_ready.credit())

                def head(g, par):
                    n.pool(pl, g, W["minus_half"])

                def body(g, par, more):
                    if more:
                        head(g + 1, 1 - par)

                pipeline(pl, first, head, body)

            @block.vector
            def _(v):
                if run == 0:
                    for s in (*n.of_vector, self.xs_ready, self.gate_step, self.hid, self.accd):
                        v.sem_inc(s.sem, s.credit())

                def normed(g, par):
                    v.wait_ge(self.accd.sem, self.accd.at(g, -self.accd.per))
                    v.tensor_scalar(xs[:, par, :, :], slot(X, g, first), 1.0, None, ALU.mult)\
                        .then_inc(self.xs_ready.sem, 1)
                    v.wait_ge(self.xs_ready.sem, self.xs_ready.at(g, 1))
                    n.vector(v, g, par, xs[:, par, :, :], lambda: v.wait_ge(self.hT_ps.sem, self.hT_ps.at(g, -1)))

                def head(g, par):
                    normed(g, par)
                    self.gate(v, g, par, lg_bank, W)

                def body(g, par, more):
                    def hidden(q):
                        v.wait_ge(self.down.sem, self.down.at(g, 1 + 2 * (q - 2) if q >= 2 else (0, -2)[q]))
                        for u in MOE_PASS_UNITS[q]:
                            m, part = MOE_UNITS[u][1], u - MOE_PASS_UNITS[q][0]
                            v.wait_ge(self.silu.sem, self.silu.at(g, u + 1))
                            v.tensor_tensor(h[0:m, q % 2, part, :], sg[0:m, u % 2, :],
                                                               up_bank[u % 2][0:m, :], ALU.mult)\
                                                                   .then_inc(self.hid.sem, 1)

                    def add(e):
                        v.wait_ge(self.down.sem, self.down.at(g, e + 1))
                        for b in range(NB):
                            v.wait_ge(self.accd.sem, self.accd.at(g, NB * (e - 1) + b + 1 if e else 0))
                            scalar, other = (self.comb[:, par, b, e - 1:e], acc[:, b, :]) if e else (0.5, xs[:, par, b, :])
                            o = acc[:, b, :] if e < EXPERTS else slot(X, g, first, b, 1)
                            v.scalar_tensor_tensor(
                                out=o, in0=down_bank[e % 2][:, b * DIM:(b + 1) * DIM], scalar=scalar, in1=other,
                                op0=ALU.mult, op1=ALU.add).then_inc(self.accd.sem, 1)

                    hidden(0)
                    hidden(1)
                    add(0)
                    hidden(2)
                    add(1)
                    add(2)
                    if more:
                        normed(g + 1, 1 - par)
                    hidden(3)
                    add(3)
                    add(4)
                    hidden(4)
                    add(5)
                    add(6)
                    if more:
                        self.gate(v, g + 1, 1 - par, lg_bank, W)
                    add(7)
                    add(8)

                pipeline(v, first, head, body)

            @block.scalar
            def _(act):
                if run == 0:
                    for s in (self.hT_ready, self.ex_ready, self.silu):
                        act.sem_inc(s.sem, s.credit())

                def move_hT(g, par):
                    act.wait_ge(self.hT_ps.sem, self.hT_ps.at(g, 1))
                    act.wait_ge(self.up.sem, self.up.at(g, -self.up.per))
                    act.activation(hT[:, par, :], hT_bank[:, :], ACT.Copy).then_inc(self.hT_ready.sem, 1)

                def exp_logits(g):
                    act.wait_ge(self.gate_step.sem, self.gate_step.at(g, 8))
                    act.activation(self.ex[:, :, :], self.ex[:, :, :], ACT.Exp).then_inc(self.ex_ready.sem, 1)

                def silus(g, units):
                    for u in units:
                        m = MOE_UNITS[u][1]
                        act.wait_ge(self.up.sem, self.up.at(g, u + 1))
                        act.wait_ge(self.hid.sem, self.hid.at(g, u - 1))
                        act.activation(sg[0:m, u % 2, :], gate_bank[u % 2][0:m, :], ACT.Silu)\
                            .then_inc(self.silu.sem, 1)

                def head(g, par):
                    move_hT(g, par)
                    exp_logits(g)

                def body(g, par, more):
                    last = MOE_PASS_UNITS[MOE_PASSES - 1]
                    silus(g, range(last[0]))
                    if more:
                        move_hT(g + 1, 1 - par)
                    silus(g, last)
                    if more:
                        exp_logits(g + 1)

                pipeline(act, first, head, body)

            @block.tensor
            def _(pe):
                if run == 0:
                    for s in (self.hT_ps, self.logits, self.up, self.down):
                        pe.sem_inc(s.sem, s.credit())

                def head(g, par):
                    pe.wait_ge(self.hT_ready.sem, self.hT_ready.at(g, 0))
                    for b in range(NB):
                        pe.wait_ge(n.out_ready.sem, n.out_ready.at(g, b + 1))
                        ins = pe.transpose(hT_bank[:, b * P:(b + 1) * P], n.out[:, par, b, :], W["ident"])
                    ins.then_inc(self.hT_ps.sem, 1)
                    pe.wait_ge(self.hT_ready.sem, self.hT_ready.at(g, 1))
                    pe.wait_ge(self.gate_step.sem, self.gate_step.at(g, 1 - self.gate_step.per))
                    for b in range(NB):
                        ins = pe.matmul(lg_bank[:, b * EXPERTS:(b + 1) * EXPERTS], hT[:, par, b * P:(b + 1) * P],
                                        W["wg"], start=True, stop=True)
                    ins.then_inc(self.logits.sem, 1)

                def body(g, par, more):
                    def up(q):
                        for u in MOE_PASS_UNITS[q]:
                            m, col = MOE_UNITS[u][1], 2 * sum(m for _, m in MOE_UNITS[:u])
                            pe.wait_ge(self.hid.sem, self.hid.at(g, u - 1))
                            pe.matmul(gate_bank[u % 2][0:m, :], W["wup"][:, col:col + m], hT[:, par, :],
                                      start=True, stop=True)
                            pe.matmul(up_bank[u % 2][0:m, :], W["wup"][:, col + m:col + 2 * m],
                                                        hT[:, par, :], start=True, stop=True).then_inc(self.up.sem, 1)

                    def down(q):
                        pe.wait_ge(self.hid.sem, self.hid.at(g, MOE_PASS_UNITS[q][-1] + 1))
                        tail = len(MOE_PASS_UNITS[q]) - 1
                        for j in range(tail):
                            e = 2 * q - 1 + j if q else 0
                            pe.wait_ge(self.accd.sem, self.accd.at(g, NB * (e - 1) if e >= 2 else (0, -NB)[e]))
                            r = TAIL * j
                            for b in range(NB):
                                o = down_bank[e % 2][:, b * DIM:(b + 1) * DIM]
                                pe.matmul(o, h[:, q % 2, j, b * P:(b + 1) * P], W["wdm"][:, e, :],
                                          start=True, stop=False)
                                ins = pe.matmul(o, h[r:r + TAIL, q % 2, tail, b * P:(b + 1) * P],
                                                W["wdt"][r:r + TAIL, q, :], start=False, stop=True)
                            ins.then_inc(self.down.sem, 1)

                    up(0)
                    for q in range(MOE_PASSES):
                        if q == 3 and more:
                            head(g + 1, 1 - par)
                        if q + 1 < MOE_PASSES:
                            up(q + 1)
                        down(q)

                pipeline(pe, first, head, body)

    def gate(self, v, g, par, lg_bank, W):
        v.wait_ge(self.accd.sem, self.accd.at(g, -self.accd.per))
        v.wait_ge(self.logits.sem, self.logits.at(g, 1))
        lg, gt, ge, ex = self.lg, self.gt, self.ge, self.ex
        v.tensor_scalar(lg[:, :, :], lg_bank[:, 0:NB * EXPERTS].rearrange("p (b e) -> p b e", b=NB), 1.0,
                             None, ALU.mult).then_inc(self.gate_step.sem, 1)
        v.wait_ge(self.gate_step.sem, self.gate_step.at(g, 1))
        shape = [P, NB, EXPERTS, EXPERTS]
        other = lg[:, :, :].unsqueeze(2).broadcast_to(shape)
        own = lg[:, :, :].unsqueeze(3).broadcast_to(shape)
        v4 = lambda t: t[:, :, :].rearrange("p (b e) j -> p b e j", b=NB)
        v.tensor_tensor(v4(gt), other, own, ALU.is_gt).then_inc(self.gate_step.sem, 1)
        v.wait_ge(self.gate_step.sem, self.gate_step.at(g, 2))
        v.tensor_tensor(v4(ge), other, own, ALU.is_ge).then_inc(self.gate_step.sem, 1)
        v.wait_ge(self.gate_step.sem, self.gate_step.at(g, 3))
        v.tensor_tensor(ge[:, :, :], ge[:, :, :], W["lower"], ALU.mult).then_inc(self.gate_step.sem, 1)
        v.wait_ge(self.gate_step.sem, self.gate_step.at(g, 4))
        v.tensor_tensor(gt[:, :, :], gt[:, :, :], ge[:, :, :], ALU.max).then_inc(self.gate_step.sem, 1)
        v.wait_ge(self.gate_step.sem, self.gate_step.at(g, 5))
        v.tensor_reduce(self.rank[:, :, :].rearrange("p b e -> p (b e)"), gt[:, :, :], AX.X, ALU.add)\
            .then_inc(self.gate_step.sem, 1)
        v.wait_ge(self.gate_step.sem, self.gate_step.at(g, 6))
        v.tensor_reduce(self.top[:, :], lg[:, :, :], AX.X, ALU.max).then_inc(self.gate_step.sem, 1)
        v.wait_ge(self.gate_step.sem, self.gate_step.at(g, 7))
        bc = lambda t: t[:, :].unsqueeze(2).broadcast_to([P, NB, EXPERTS])
        v.tensor_tensor(ex[:, :, :], lg[:, :, :], bc(self.top), ALU.subtract).then_inc(self.gate_step.sem, 1)
        v.wait_ge(self.gate_step.sem, self.gate_step.at(g, 8))
        v.wait_ge(self.ex_ready.sem, self.ex_ready.at(g, 1))
        v.scalar_tensor_tensor(out=ex[:, :, :], in0=self.rank[:, :, :], scalar=1.5, in1=ex[:, :, :],
                                    op0=ALU.is_lt, op1=ALU.mult).then_inc(self.gate_step.sem, 1)
        v.wait_ge(self.gate_step.sem, self.gate_step.at(g, 9))
        v.tensor_reduce(self.den[:, :], ex[:, :, :], AX.X, ALU.add).then_inc(self.gate_step.sem, 1)
        v.wait_ge(self.gate_step.sem, self.gate_step.at(g, 10))
        v.reciprocal(self.den[:, :], self.den[:, :]).then_inc(self.gate_step.sem, 1)
        v.wait_ge(self.gate_step.sem, self.gate_step.at(g, 11))
        v.tensor_scalar(self.den[:, :], self.den[:, :], 0.5, None, ALU.mult).then_inc(self.gate_step.sem, 1)
        v.wait_ge(self.gate_step.sem, self.gate_step.at(g, 12))
        v.tensor_tensor(self.comb[:, par, :, :], ex[:, :, :], bc(self.den), ALU.mult).then_inc(self.gate_step.sem, 1)
        v.wait_ge(self.gate_step.sem, self.gate_step.at(g, 13))


HID_BLOCKS = [(0, P), (P, P), (2 * P, HID - 2 * P)]


class Geglu:

    def __init__(self, ctx, nc):
        sig = lambda n, per, unit=1: Signal(ctx, nc, f"ffn_{n}", per, unit)
        self.norm = Norm(ctx, nc, "ffn_norm")
        self.shifted = sig("shifted", 3, 16)
        self.hT_ps = sig("hT_in_psum", 1)
        self.hT_ready = sig("hT_ready", 1)
        self.up = sig("up_ready", 3)
        self.gelu = sig("gelu_ready", 3)
        self.hid = sig("hidden_ready", 3)
        self.down = sig("down_ready", 1)
        self.sum = sig("sum_ready", 1)
        self.summed = sig("summed", 1)
        self.moved = sig("result_stored", 1)
        self.first_token = ctx.enter_context(nc.semaphore("ffn_first_token"))

    def emit(self, nc, run, X, Y, W, layer, last):
        n, first = self.norm, run * NSEQ
        others = (run - run // DEPTH) * NSEQ
        w1, w2 = W["w1"][:, layer, :], W["w2"][:, layer, :, :]
        b1, b2, lg, lb = W["b1"][:, layer, :], W["b2"][:, layer, :], W["ln_g"], W["ln_b"]
        with ExitStack() as ctx:
            pb = lambda name: ctx.enter_context(nc.psum_tensor(f"ffn{run}_{name}", [P, SEQ], F32))
            sb = lambda name, s, dt=F32: ctx.enter_context(nc.sbuf_tensor(f"ffn{run}_{name}", s, dt))
            n.buffers(ctx, nc, run)
            a_bank, g_bank = [pb(f"a{j}") for j in range(3)], [pb(f"g{j}") for j in range(3)]
            hT_bank, out_bank = pb("hT"), pb("out")
            hs = sb("shifted", [P, 2, NB, DIM])
            hT = sb("hTs", [P, 2, SEQ])
            gl = sb("gelu", [P, 3, SEQ])
            hid = sb("hidden", [P, 2, 3, SEQ])
            total = sb("total", [P, NB, DIM])
            H = DIM // 2
            block = ctx.enter_context(nc.Block())

            @block.sync
            def _(sp):
                if run == 0:
                    sp.sem_inc(self.shifted.sem, self.shifted.credit())
                sp.wait_ge(self.first_token, run + 1)

                def head(g, par):
                    sp.wait_ge(self.shifted.sem, self.shifted.at(g, 0))
                    sp.wait_ge(n.out_ready.sem, n.out_ready.at(g, -NB))
                    y = lambda b, c: slot(Y, g, first, b, c)
                    sp.dma_start(hs[:, par, :, 0:H], y(0, NB)[:, :, 0:H]).then_inc(self.shifted.sem, 16)
                    sp.dma_start(hs[1:P, par, :, H:DIM], y(0, NB)[0:P - 1, :, H:DIM]).then_inc(self.shifted.sem, 16)
                    sp.dma_start(hs[0:1, par, 1:NB, H:DIM], y(0, NB - 1)[P - 1:P, :, H:DIM]).then_inc(self.shifted.sem, 16)

                def body(g, par, more):
                    if more:
                        head(g + 1, 1 - par)

                pipeline(sp, first, head, body)

            @block.gpsimd
            def _(pl):
                if run == 0:
                    pl.sem_inc(n.rstd_ready.sem, n.rstd_ready.credit())

                def head(g, par):
                    n.pool(pl, g, W["minus_half"])

                def body(g, par, more):
                    if more:
                        head(g + 1, 1 - par)

                pipeline(pl, first, head, body)

            @block.vector
            def _(v):
                if run == 0:
                    for s in (*n.of_vector, self.hid, self.sum, self.summed, self.moved):
                        v.sem_inc(s.sem, s.credit())
                v.memset(hs[0:1, :, 0:1, H:DIM], 0.0).then_inc(self.first_token, 1)

                def head(g, par):
                    v.wait_ge(self.shifted.sem, self.shifted.at(g, 3))
                    n.vector(v, g, par, hs[:, par, :, :], lambda: v.wait_ge(self.hT_ps.sem, self.hT_ps.at(g, -1)))

                def body(g, par, more):
                    for j, (_, m) in enumerate(HID_BLOCKS):
                        v.wait_ge(self.gelu.sem, self.gelu.at(g, j + 1))
                        v.wait_ge(self.down.sem, self.down.at(g, -1))
                        v.scalar_tensor_tensor(
                            out=hid[0:m, par, j, :], in0=a_bank[j][0:m, :], scalar=b1[0:m, j:j + 1],
                            in1=gl[0:m, j, :], op0=ALU.add, op1=ALU.mult).then_inc(self.hid.sem, 1)
                    if more:
                        head(g + 1, 1 - par)
                    v.wait_ge(self.down.sem, self.down.at(g, 1))
                    v.wait_ge(self.moved.sem, self.moved.at(g, 0))
                    out3 = out_bank[:, :].rearrange("p (b d) -> p b d", b=NB)
                    v.tensor_tensor(total[:, :, :], out3,
                                                       b2.unsqueeze(1).broadcast_to([P, NB, DIM]), ALU.add)\
                                                           .then_inc(self.sum.sem, 1)
                    v.wait_ge(self.sum.sem, self.sum.at(g, 1))
                    y = slot(Y, g, first)
                    if last:
                        v.tensor_tensor(total[:, :, :], total[:, :, :], y, ALU.add).then_inc(self.summed.sem, 1)
                        v.wait_ge(self.summed.sem, self.summed.at(g - others, 1))
                        x = slot(X, g, first)
                        v.scalar_tensor_tensor(out=x, in0=total[:, :, :], scalar=0.5, in1=x,
                                                                    op0=ALU.mult, op1=ALU.add)\
                                                                        .then_inc(self.moved.sem, 1)
                    else:
                        v.tensor_tensor(y, total[:, :, :], y, ALU.add).then_inc(self.moved.sem, 1)

                pipeline(v, first, head, body)

            @block.scalar
            def _(act):
                if run == 0:
                    for s in (self.hT_ready, self.gelu):
                        act.sem_inc(s.sem, s.credit())

                def head(g, par):
                    act.wait_ge(self.hT_ps.sem, self.hT_ps.at(g, 1))
                    act.wait_ge(self.up.sem, self.up.at(g, -3))
                    act.activation(hT[:, par, :], hT_bank[:, :], ACT.Identity,
                                                           bias=lb[:, layer:layer + 1], scale=lg[:, layer:layer + 1])\
                                                               .then_inc(self.hT_ready.sem, 1)

                def body(g, par, more):
                    for j, (_, m) in enumerate(HID_BLOCKS):
                        act.wait_ge(self.up.sem, self.up.at(g, j + 1))
                        act.wait_ge(self.hid.sem, self.hid.at(g, j - 2))
                        act.activation(gl[0:m, j, :], g_bank[j][0:m, :], ACT.Gelu,
                                                           bias=b1[0:m, 3 + j:4 + j]).then_inc(self.gelu.sem, 1)
                    if more:
                        head(g + 1, 1 - par)

                pipeline(act, first, head, body)

            @block.tensor
            def _(pe):
                if run == 0:
                    for s in (self.hT_ps, self.up, self.down):
                        pe.sem_inc(s.sem, s.credit())

                def head(g, par):
                    pe.wait_ge(self.hT_ready.sem, self.hT_ready.at(g, 0))
                    for b in range(NB):
                        pe.wait_ge(n.out_ready.sem, n.out_ready.at(g, b + 1))
                        ins = pe.transpose(hT_bank[:, b * P:(b + 1) * P], n.out[:, par, b, :], W["ident"])
                    ins.then_inc(self.hT_ps.sem, 1)

                def body(g, par, more):
                    pe.wait_ge(self.hT_ready.sem, self.hT_ready.at(g, 1))
                    for j, (r, m) in enumerate(HID_BLOCKS):
                        pe.wait_ge(self.hid.sem, self.hid.at(g, j - 2))
                        pe.matmul(g_bank[j][0:m, :], w1[:, HID + r:HID + r + m], hT[:, par, :], start=True, stop=True)
                        pe.matmul(a_bank[j][0:m, :], w1[:, r:r + m], hT[:, par, :],
                                                    start=True, stop=True).then_inc(self.up.sem, 1)
                    if more:
                        head(g + 1, 1 - par)
                    pe.wait_ge(self.hid.sem, self.hid.at(g, 3))
                    pe.wait_ge(self.sum.sem, self.sum.at(g, 0))
                    for b in range(NB):
                        for j, (_, m) in enumerate(HID_BLOCKS):
                            ins = pe.matmul(out_bank[:, b * DIM:(b + 1) * DIM], hid[0:m, par, j, b * P:(b + 1) * P],
                                            w2[0:m, j, :], start=(j == 0), stop=(j == 2))
                    ins.then_inc(self.down.sem, 1)

                pipeline(pe, first, head, body)


PAIRS = LH // 2
UNITS = NB * PAIRS
BAND = P + WINDOW


def unit_heads(k):
    a = k % PAIRS
    return [4 * (a // 2) + a % 2 + 2 * j for j in range(2)]


class LocalAttention:

    def __init__(self, ctx, nc):
        sig = lambda n, per, unit=1: Signal(ctx, nc, f"loc_{n}", per, unit)
        self.norm = Norm(ctx, nc, "loc_norm")
        self.xs_ready = sig("xs_ready", 1)
        self.y_made = sig("y_made", 1)
        self.q_turned = sig("q_turned", NB)
        self.k_turned = sig("k_turned", NB)
        self.v_ps = sig("v_in_psum", NB)
        self.yT_ps = sig("yT_in_psum", 1)
        self.hT_ready = sig("hT_ready", 2)
        self.qkv = sig("qkv_ready", NB)
        self.squares = sig("squares", NB)
        self.v_ready = sig("v_ready", NB)
        self.ss_ready = sig("ss_ready", 2 * NB)
        self.terms = sig("turn_terms", 3 * NB)
        self.rn_ready = sig("rn_ready", NB)
        self.k_normed = sig("k_normed", NB)
        self.qT_ps = sig("qT_in_psum", NB)
        self.kT_ps = sig("kT_in_psum", NB)
        self.qT_ready = sig("qT_ready", NB)
        self.kT_ready = sig("kT_ready", NB)
        self.scores = sig("scores", UNITS)
        self.top = sig("top", UNITS)
        self.bias = sig("bias", UNITS)
        self.probs = sig("probs", 2 * UNITS)
        self.rsum = sig("rsum", UNITS)
        self.divided = sig("divided", UNITS)
        self.pT_ps = sig("pT_in_psum", UNITS)
        self.pT_ready = [sig(f"pT_ready{j}", UNITS // 2) for j in range(2)]
        self.pv = sig("pv", UNITS // 2)
        self.oT_ready = sig("oT_ready", NB)
        self.wo = sig("wo_ready", NB)
        self.moved = sig("result_stored", NB)
        self.cleared = ctx.enter_context(nc.semaphore("loc_cleared"))

    def emit(self, nc, run, X, Y, W, layer):
        n, first = self.norm, run * NSEQ
        n.behind = (run - run // DEPTH) * NSEQ
        wqkv, wo = W["wqkv"][:, layer, :], W["wo"][:, layer, :, :]
        turn_cos, turn_sin = W["turn_cos"][:, layer, :, :, :], W["turn_sin"][:, layer, :, :, :]
        H = DIM // 2
        with ExitStack() as ctx:
            pb = lambda name, banks=1: ctx.enter_context(nc.psum_tensor(f"loc{run}_{name}", [P, banks * SEQ], F32))
            sb = lambda name, s, dt=F32: ctx.enter_context(nc.sbuf_tensor(f"loc{run}_{name}", s, dt))
            n.buffers(ctx, nc, run)
            qk_bank = pb("qk", 2)
            v_bank = pb("v")
            t_bank = pb("t")
            s_bank = [pb("s0"), pb("s1")]
            p_bank = pb("p")
            o_bank = pb("o")
            xs = sb("xs", [P, NB, DIM])
            hT = sb("hTs", [P, 2, SEQ])
            sq = sb("sq", [P, 2 * INNER])
            ss = sb("ss", [P, 2 * LH])
            rn = sb("rn", [P, NB, 2 * LH])
            t1 = sb("t1", [P, 2 * INNER])
            t2 = sb("t2", [P, 2 * INNER])
            qk = sb("qk_turned", [P, 2 * INNER])
            vs = sb("vs", [P, 2, NB, INNER])
            qT = sb("qT", [P, 2, PAIRS, P])
            kT = sb("kT", [P, PAIRS, SEQ])
            top = sb("tops", [P, UNITS, 2])
            bias = sb("biases", [P, UNITS, 2])
            sums = sb("sums", [P, UNITS, 2])
            rs = sb("rs", [P, UNITS, 2])
            probs = sb("probs_s", [P, 8, 2, 2 * P])
            pT = sb("pT", [P, 4, 2, BAND])
            oT = sb("oT", [P, PAIRS, P])
            block = ctx.enter_context(nc.Block())
            by_head = lambda t: t.rearrange("p (h d) -> p h d", d=LD)

            STATS, APPLY, Y_T = -15, -14, -13
            QK, V, SQUARE, MOVE_V, COS, SIN, SQUARES, RN = -10, -9, -9, -8, -8, -7, -6, -5
            TURN_Q, TURN_K, NORM_K, Q_T, K_T = -6, -5, -4, -4, -3
            O_T, PROJECT, ADD = 9, 10, 11
            SCORE, INVERSE, P_T, TIMES_V = -1, 1, 4, 6
            in_slot = lambda s, offset, count=1, every=PAIRS: due(s, UNITS, offset, count, every)

            @block.gpsimd
            def _(pl):
                if run == 0:
                    for s in (n.rstd_ready, self.rn_ready, self.q_turned, self.k_normed, self.divided):
                        pl.sem_inc(s.sem, s.credit())

                def norms(g, t):
                    pl.wait_ge(self.ss_ready.sem, self.ss_ready.at(g, 2 * t + 2))
                    pl.wait_ge(self.probs.sem, self.probs.at(g, 2 * PAIRS * (t + 1) - 2 * UNITS))
                    pl.wait_ge(self.k_normed.sem, self.k_normed.at(g, t + 1 - NB))
                    pl.tensor_tensor(rn[:, t, :], ss[:, :], W["minus_half"][:, 0:2 * LH], ALU.pow)\
                        .then_inc(self.rn_ready.sem, 1)

                def turn_q(g, t):
                    pl.wait_ge(self.terms.sem, self.terms.at(g, 3 * t + 3))
                    pl.wait_ge(self.qT_ps.sem, self.qT_ps.at(g, t))
                    q = slice(0, INNER)
                    pl.tensor_tensor(qk[:, q], t1[:, q], t2[:, q], ALU.add).then_inc(self.q_turned.sem, 1)

                def norm_k(g, t):
                    pl.wait_ge(self.rn_ready.sem, self.rn_ready.at(g, t + 1))
                    pl.wait_ge(self.k_turned.sem, self.k_turned.at(g, t + 1))
                    k3 = by_head(qk[:, INNER:2 * INNER])
                    pl.tensor_tensor(k3, k3, rn[:, t, LH:2 * LH].unsqueeze(2).broadcast_to([P, LH, LD]), ALU.mult)\
                        .then_inc(self.k_normed.sem, 1)

                def divide(g, k):
                    pl.wait_ge(self.rsum.sem, self.rsum.at(g, k + 1))
                    p_ = probs[:, k % 8, :, H:2 * P]
                    pl.tensor_tensor(p_, p_, rs[:, k, :].unsqueeze(2).broadcast_to([P, 2, BAND]), ALU.mult)\
                        .then_inc(self.divided.sem, 1)

                def body(g, par, there):
                    for s in range(UNITS):
                        for d, k in in_slot(s, INVERSE, UNITS, 1):
                            if d in there:
                                divide(g + d, k)
                        for d, _ in in_slot(s, STATS):
                            if d in there and layer == 0:
                                n.pool(pl, g + d, W["minus_half"])
                        for d, t in in_slot(s, NORM_K, NB):
                            if d in there:
                                norm_k(g + d, t)
                        for d, t in in_slot(s, TURN_Q, NB):
                            if d in there:
                                turn_q(g + d, t)
                        for d, t in in_slot(s, RN, NB):
                            if d in there:
                                norms(g + d, t)

                modulo_pipeline(pl, first, body)

            @block.vector
            def _(v):
                if run == 0:
                    for s in (*n.of_vector, self.xs_ready, self.y_made, self.ss_ready, self.terms, self.k_turned, self.top, self.bias,
                              self.rsum, self.pT_ready[0], self.moved):
                        v.sem_inc(s.sem, s.credit())
                v.memset(hT[H:P, :, 0:1], 0.0).then_inc(self.cleared, 1)
                v.memset(probs[:, :, :, 0:H], 0.0).then_inc(self.cleared, 1)

                def stats(g):
                    v.wait_ge(n.out_ready.sem, n.out_ready.at(g, 0))
                    v.tensor_scalar(xs[:, :, :], slot(X, g, first), 1.0, None, ALU.mult)\
                        .then_inc(self.xs_ready.sem, 1)
                    v.wait_ge(self.xs_ready.sem, self.xs_ready.at(g - n.behind, 1))
                    n.vector_stats(v, g, xs)

                def tokens(g, par):
                    if layer == 0:
                        n.vector_apply(v, g, par, xs, lambda: v.wait_ge(self.yT_ps.sem, self.yT_ps.at(g, -1)))
                        v.wait_ge(n.out_ready.sem, n.out_ready.at(g, NB))
                        v.tensor_scalar(slot(Y, g, first), n.out[:, par, :, :], 1.0, None, ALU.mult)\
                            .then_inc(self.y_made.sem, 1)
                    else:
                        v.wait_ge(self.yT_ps.sem, self.yT_ps.at(g, -1))
                        for b in range(NB):
                            v.tensor_scalar(n.out[:, par, b:b + 1, :], slot(Y, g, first, b, 1), 1.0, None, ALU.mult)\
                                .then_inc(n.out_ready.sem, 1)

                def squares(g, t):
                    v.wait_ge(self.squares.sem, self.squares.at(g, t + 1))
                    v.wait_ge(self.rn_ready.sem, self.rn_ready.at(g, t))
                    v.tensor_reduce(ss[:, :], by_head(sq[:, :]), AX.X, ALU.add).then_inc(self.ss_ready.sem, 1)
                    v.wait_ge(self.ss_ready.sem, self.ss_ready.at(g, 2 * t + 1))
                    v.tensor_scalar(ss[:, :], ss[:, :], 1e-24, None, ALU.max).then_inc(self.ss_ready.sem, 1)

                q4 = qk_bank[:, :].rearrange("p (j h d) -> p j h d", j=2, d=LD)

                def cos_terms(g, t):
                    v.wait_ge(self.squares.sem, self.squares.at(g, t + 1))
                    v.wait_ge(self.q_turned.sem, self.q_turned.at(g, t))
                    v.wait_ge(self.k_turned.sem, self.k_turned.at(g, t))
                    cos = turn_cos[:, t, :, :].unsqueeze(2).broadcast_to([P, 2, LH, LD])
                    v.tensor_tensor(t1[:, :].rearrange("p (j h d) -> p j h d", j=2, d=LD), q4, cos, ALU.mult)\
                        .then_inc(self.terms.sem, 1)

                def sin_terms(g, t):
                    for j in range(2):
                        halves = lambda ap: ap.rearrange("p h (s d) -> p h s d", s=2)
                        sin = turn_sin[:, t, j, :].unsqueeze(1).broadcast_to([P, LH, LD])
                        v.tensor_tensor(halves(by_head(t2[:, j * INNER:(j + 1) * INNER])),
                                        halves(q4[:, j, :, :])[:, :, ::-1, :], halves(sin), ALU.mult)\
                            .then_inc(self.terms.sem, 1)

                def turn_k(g, t):
                    v.wait_ge(self.terms.sem, self.terms.at(g, 3 * t + 3))
                    v.wait_ge(self.kT_ps.sem, self.kT_ps.at(g, t))
                    k_ = slice(INNER, 2 * INNER)
                    v.tensor_tensor(qk[:, k_], t1[:, k_], t2[:, k_], ALU.add).then_inc(self.k_turned.sem, 1)

                def top_of(g, k):
                    v.wait_ge(self.scores.sem, self.scores.at(g, k + 1))
                    s3 = s_bank[k % 2][:, 0:2 * BAND].rearrange("p (j c) -> p j c", j=2)
                    v.tensor_reduce(top[:, k, :], s3, AX.X, ALU.max, negate=True).then_inc(self.top.sem, 1)

                def bias_of(g, k):
                    v.wait_ge(self.top.sem, self.top.at(g, k + 1))
                    v.wait_ge(self.rn_ready.sem, self.rn_ready.at(g, k // PAIRS + 1))
                    h = unit_heads(k)
                    v.tensor_tensor(bias[:, k, :], top[:, k, :], rn[:, k // PAIRS, h[0]:h[1] + 1:2], ALU.mult)\
                        .then_inc(self.bias.sem, 1)

                def inverse(g, k):
                    v.wait_ge(self.probs.sem, self.probs.at(g, 2 * k + 2))
                    v.reciprocal(rs[:, k, :], sums[:, k, :]).then_inc(self.rsum.sem, 1)

                def move_pT(g, k):
                    v.wait_ge(self.pT_ps.sem, self.pT_ps.at(g, k + 1))
                    v.wait_ge(self.pv.sem, self.pv.at(g, k // 2 - 1))
                    c = BAND if k >= PAIRS else P
                    src = p_bank[:, 0:2 * BAND].rearrange("p (j c) -> p j c", j=2)[:, :, 0:c]
                    v.tensor_copy(pT[:, k % 4, :, 0:c], src).then_inc(self.pT_ready[0].sem, 1)

                def add(g, t):
                    v.wait_ge(self.wo.sem, self.wo.at(g, t + 1))
                    if layer == 0:
                        v.wait_ge(self.y_made.sem, self.y_made.at(g - n.behind, 1))
                    y = slot(Y, g, first, t, 1)
                    v.tensor_tensor(y, t_bank[:, 0:DIM].unsqueeze(1), y, ALU.add).then_inc(self.moved.sem, 1)

                def body(g, par, there):
                    for s in range(UNITS):
                        if 0 in there:
                            top_of(g, s)
                        for d, k in in_slot(s, INVERSE, UNITS, 1):
                            if d in there:
                                inverse(g + d, k)
                        if 0 in there:
                            bias_of(g, s)
                        for d, k in in_slot(s, P_T, UNITS, 1):
                            if d in there and k % 2 == 0:
                                move_pT(g + d, k)
                        for d, t in in_slot(s, ADD, NB):
                            if d in there:
                                add(g + d, t)
                        for d, t in in_slot(s, SQUARES, NB):
                            if d in there:
                                squares(g + d, t)
                        for d, t in in_slot(s, COS, NB):
                            if d in there:
                                cos_terms(g + d, t)
                        for d, t in in_slot(s, SIN, NB):
                            if d in there:
                                sin_terms(g + d, t)
                        for d, t in in_slot(s, TURN_K, NB):
                            if d in there:
                                turn_k(g + d, t)
                        for d, _ in in_slot(s, STATS):
                            if d in there and layer == 0:
                                stats(g + d)
                        for d, _ in in_slot(s, APPLY):
                            if d in there:
                                tokens(g + d, par if d == 0 else 1 - par)

                modulo_pipeline(v, first, body)

            @block.scalar
            def _(act):
                if run == 0:
                    for s in (self.hT_ready, self.squares, self.v_ready, self.qT_ready, self.kT_ready, self.probs,
                              self.pT_ready[1], self.oT_ready):
                        act.sem_inc(s.sem, s.credit())
                act.wait_ge(self.cleared, 2 * run + 2)
                copy = lambda o, i: act.activation(o, i, ACT.Copy)

                def move_hT(g, par):
                    act.wait_ge(self.yT_ps.sem, self.yT_ps.at(g, 1))
                    act.wait_ge(self.v_ps.sem, self.v_ps.at(g, -NB))
                    copy(hT[0:H, par, :], t_bank[0:H, :]).then_inc(self.hT_ready.sem, 1)
                    copy(hT[H:P, par, 1:SEQ], t_bank[H:P, 0:SEQ - 1]).then_inc(self.hT_ready.sem, 1)

                def square_qk(g, t):
                    act.wait_ge(self.qkv.sem, self.qkv.at(g, t + 1))
                    act.wait_ge(self.ss_ready.sem, self.ss_ready.at(g, 2 * t))
                    act.activation(sq[:, :], qk_bank[:, :], ACT.Square).then_inc(self.squares.sem, 1)

                def take_v(g, par, t):
                    act.wait_ge(self.v_ps.sem, self.v_ps.at(g, t + 1))
                    act.wait_ge(self.pv.sem, self.pv.at(g, PAIRS * min(t + 2, NB) // 2 - UNITS))
                    copy(vs[:, par, t, :], v_bank[:, :]).then_inc(self.v_ready.sem, 1)

                def take_qT(g, t):
                    act.wait_ge(self.qT_ps.sem, self.qT_ps.at(g, t + 1))
                    act.wait_ge(self.scores.sem, self.scores.at(g, PAIRS * (t - 1)))
                    copy(qT[:, t % 2, :, :], t_bank[:, :].rearrange("p (a c) -> p a c", c=P))\
                        .then_inc(self.qT_ready.sem, 1)

                def take_kT(g, t):
                    act.wait_ge(self.kT_ps.sem, self.kT_ps.at(g, t + 1))
                    act.wait_ge(self.scores.sem, self.scores.at(g, PAIRS * min(t + 2, NB) - UNITS))
                    copy(kT[:, :, t * P:(t + 1) * P], t_bank[:, :].rearrange("p (a c) -> p a c", c=P))\
                        .then_inc(self.kT_ready.sem, 1)

                def exp(g, k):
                    act.wait_ge(self.bias.sem, self.bias.at(g, k + 1))
                    act.wait_ge(self.pT_ps.sem, self.pT_ps.at(g, k - 7))
                    act.wait_ge(self.rsum.sem, self.rsum.at(g, k + 1 - UNITS))
                    for j, h in enumerate(unit_heads(k)):
                        act.activation(
                            probs[:, k % 8, j, H:2 * P], s_bank[k % 2][:, j * BAND:(j + 1) * BAND], ACT.Exp,
                            bias=bias[:, k, j:j + 1], scale=rn[:, k // PAIRS, h:h + 1],
                            accum_out=sums[:, k, j:j + 1]).then_inc(self.probs.sem, 1)

                def move_pT(g, k):
                    act.wait_ge(self.pT_ps.sem, self.pT_ps.at(g, k + 1))
                    act.wait_ge(self.pv.sem, self.pv.at(g, k // 2 - 1))
                    c = BAND if k >= PAIRS else P
                    src = p_bank[:, 0:2 * BAND].rearrange("p (j c) -> p j c", j=2)[:, :, 0:c]
                    copy(pT[:, k % 4, :, 0:c], src).then_inc(self.pT_ready[1].sem, 1)

                def move_oT(g, t):
                    act.wait_ge(self.pv.sem, self.pv.at(g, PAIRS // 2 * (t + 1)))
                    act.wait_ge(self.wo.sem, self.wo.at(g, t))
                    copy(oT[:, :, :], o_bank[:, :].rearrange("p (a c) -> p a c", c=P)).then_inc(self.oT_ready.sem, 1)

                def body(g, par, there):
                    for s in range(UNITS):
                        if 0 in there:
                            exp(g, s)
                        for d, t in in_slot(s, O_T, NB):
                            if d in there:
                                move_oT(g + d, t)
                        for d, k in in_slot(s, P_T, UNITS, 1):
                            if d in there and k % 2 == 1:
                                move_pT(g + d, k)
                        for d, t in in_slot(s, Q_T, NB):
                            if d in there:
                                take_qT(g + d, t)
                        for d, t in in_slot(s, K_T, NB):
                            if d in there:
                                take_kT(g + d, t)
                        for d, _ in in_slot(s, Y_T):
                            if d in there:
                                move_hT(g + d, par if d == 0 else 1 - par)
                        for d, t in in_slot(s, MOVE_V, NB):
                            if d in there:
                                take_v(g + d, par if d == 0 else 1 - par, t)
                        for d, t in in_slot(s, SQUARE, NB):
                            if d in there:
                                square_qk(g + d, t)

                modulo_pipeline(act, first, body)

            @block.tensor
            def _(pe):
                if run == 0:
                    for s in (self.yT_ps, self.qkv, self.v_ps, self.qT_ps, self.kT_ps, self.scores, self.pT_ps, self.pv, self.wo):
                        pe.sem_inc(s.sem, s.credit())
                pe.wait_ge(self.cleared, 2 * run + 2)


                def transpose_y(g, par):
                    pe.wait_ge(self.kT_ready.sem, self.kT_ready.at(g, 2 - NB))
                    pe.wait_ge(self.moved.sem, self.moved.at(g, 3 - 2 * NB))
                    for b in range(NB):
                        pe.wait_ge(n.out_ready.sem, n.out_ready.at(g, b + 1))
                        ins = pe.transpose(t_bank[:, b * P:(b + 1) * P], n.out[:, par, b, :], W["ident"])
                    ins.then_inc(self.yT_ps.sem, 1)

                def make_qk(g, par, t):
                    pe.wait_ge(self.hT_ready.sem, self.hT_ready.at(g, 2))
                    pe.wait_ge(self.squares.sem, self.squares.at(g, t))
                    pe.wait_ge(self.terms.sem, self.terms.at(g, 3 * t))
                    for j in range(2):
                        part = slice(j * INNER, (j + 1) * INNER)
                        ins = pe.matmul(qk_bank[:, part], hT[:, par, t * P:(t + 1) * P], wqkv[:, part],
                                        start=True, stop=True)
                    ins.then_inc(self.qkv.sem, 1)

                def make_v(g, par, t):
                    pe.wait_ge(self.v_ready.sem, self.v_ready.at(g, t))
                    pe.matmul(v_bank[:, :], hT[:, par, t * P:(t + 1) * P], wqkv[:, 2 * INNER:3 * INNER],
                              start=True, stop=True).then_inc(self.v_ps.sem, 1)

                def transpose_q(g, t, more):
                    pe.wait_ge(self.q_turned.sem, self.q_turned.at(g, t + 1))
                    pe.wait_ge(self.kT_ready.sem, self.kT_ready.at(g, t))
                    if t == NB - 2 and more:
                        pe.wait_ge(self.hT_ready.sem, self.hT_ready.at(g + 1, 2))
                    else:
                        pe.wait_ge(self.moved.sem, self.moved.at(g, t + 1 - NB))
                    for a in range(PAIRS):
                        ins = pe.transpose(t_bank[:, a * P:(a + 1) * P], qk[:, a * P:(a + 1) * P], W["ident"])
                    ins.then_inc(self.qT_ps.sem, 1)

                def transpose_k(g, t):
                    pe.wait_ge(self.k_normed.sem, self.k_normed.at(g, t + 1))
                    pe.wait_ge(self.qT_ready.sem, self.qT_ready.at(g, t + 1))
                    for a in range(PAIRS):
                        ins = pe.transpose(t_bank[:, a * P:(a + 1) * P], qk[:, INNER + a * P:INNER + (a + 1) * P],
                                           W["ident"])
                    ins.then_inc(self.kT_ps.sem, 1)

                def score(g, k):
                    t = k // PAIRS
                    pe.wait_ge(self.qT_ready.sem, self.qT_ready.at(g, t + 1))
                    pe.wait_ge(self.kT_ready.sem, self.kT_ready.at(g, t + 1))
                    pe.wait_ge(self.probs.sem, self.probs.at(g, 2 * (k - 1)))
                    skip = WINDOW if t == 0 else 0
                    bank = s_bank[k % 2]
                    pe.matmul(bank[:, 0:2 * BAND], W["ident16"], W["band"][:, min(t, 1), :], start=True, stop=False)
                    for j, h in enumerate(unit_heads(k)):
                        rows = slice(LD * (h % 2), LD * (h % 2) + LD)
                        ins = pe.matmul(bank[:, j * BAND + skip:(j + 1) * BAND], qT[rows, t % 2, h // 2, :],
                                        kT[rows, h // 2, t * P - WINDOW + skip:(t + 1) * P], start=False, stop=(j == 1))
                    ins.then_inc(self.scores.sem, 1)

                def transpose_p(g, k):
                    pe.wait_ge(self.divided.sem, self.divided.at(g, k + 1))
                    copied = self.pT_ready[(k - 1) % 2]
                    pe.wait_ge(copied.sem, copied.at(g, (k + 1) // 2 if k % 2 else k // 2))
                    for j in range(2):
                        o = p_bank[:, j * BAND:(j + 1) * BAND]
                        ins = pe.transpose(o[:, 0:P], probs[:, k % 8, j, P:2 * P], W["ident"])
                        if k >= PAIRS:
                            ins = pe.transpose(o[:, P:BAND], probs[0:WINDOW, k % 8, j, 0:P],
                                               W["ident"][0:WINDOW, 0:WINDOW])
                    ins.then_inc(self.pT_ps.sem, 1)

                def times_v(g, par, k):
                    t = k // PAIRS
                    pe.wait_ge(self.pT_ready[0].sem, self.pT_ready[0].at(g, k // 2 + 1))
                    pe.wait_ge(self.pT_ready[1].sem, self.pT_ready[1].at(g, k // 2 + 1))
                    if k % PAIRS == 0:
                        pe.wait_ge(self.oT_ready.sem, self.oT_ready.at(g, t))
                    for j in range(2):
                        for own in (True, False)[0:2 if t else 1]:
                            for u in (k, k + 1):
                                h = unit_heads(u)[j]
                                o = o_bank[LD * (h % 2):LD * (h % 2) + LD, h // 2 * P:(h // 2 + 1) * P]
                                v_ = vs[:, par, t if own else t - 1, h * LD:(h + 1) * LD]
                                if own:
                                    ins = pe.matmul(o, v_, pT[:, u % 4, j, 0:P], start=True, stop=(t == 0))
                                else:
                                    ins = pe.matmul(o[:, 0:WINDOW], v_, pT[:, u % 4, j, P:BAND],
                                                    start=False, stop=True)
                    ins.then_inc(self.pv.sem, 1)

                def project(g, t, more):
                    pe.wait_ge(self.oT_ready.sem, self.oT_ready.at(g, t + 1))
                    pe.wait_ge(self.kT_ready.sem, self.kT_ready.at(g, t + 4 if more else NB))
                    pe.wait_ge(self.moved.sem, self.moved.at(g, t))
                    for a in range(PAIRS):
                        ins = pe.matmul(t_bank[:, 0:DIM], oT[:, a, :], wo[:, a, :], start=(a == 0),
                                        stop=(a == PAIRS - 1))
                    ins.then_inc(self.wo.sem, 1)

                def body(g, par, there):
                    for s in range(UNITS):
                        for d, k in in_slot(s, SCORE, UNITS, 1):
                            if d in there:
                                score(g + d, k)
                        for d, k in in_slot(s, P_T, UNITS, 1):
                            if d in there:
                                transpose_p(g + d, k)
                        for d, t in in_slot(s, PROJECT, NB):
                            if d in there:
                                project(g + d, t, d + 1 in there)
                        for d, t in in_slot(s, Q_T, NB):
                            if d in there:
                                transpose_q(g + d, t, d + 1 in there)
                        for d, t in in_slot(s, K_T, NB):
                            if d in there:
                                transpose_k(g + d, t)
                        for d, _ in in_slot(s, Y_T):
                            if d in there:
                                transpose_y(g + d, par if d == 0 else 1 - par)
                        for d, k in in_slot(s, TIMES_V, UNITS, 1):
                            if d in there and k % 2 == 0:
                                times_v(g + d, par if d == 0 else 1 - par, k)
                        for d, t in in_slot(s, QK, NB):
                            if d in there:
                                make_qk(g + d, par if d == 0 else 1 - par, t)
                        for d, t in in_slot(s, V, NB):
                            if d in there:
                                make_v(g + d, par if d == 0 else 1 - par, t)

                modulo_pipeline(pe, first, body)


SPLIT = 3
PAIR_ROWS = SPLIT * SPLIT * HD
ROWS = PAIR_ROWS + SPLIT
GROUPS = HEADS // 4
PANE = 32
STEPS = 8
SLOTS = GROUPS * STEPS
ATOPS = NB * 4


class GlobalAttention:

    def __init__(self, ctx, nc, kind):
        sig = lambda n, per, unit=1: Signal(ctx, nc, f"{kind}_{n}", per, unit)
        self.kind, self.causal = kind, kind == "causal"
        self.norm = Norm(ctx, nc, kind + "_norm")
        self.xs_ready = sig("xs_ready", 1)
        self.hT_ps = sig("hT_in_psum", 1)
        self.hT_ready = sig("hT_ready", 1)
        self.made = sig("qkv_in_psum", 3 if self.causal else 5)
        self.turn = sig("turn_step", 4)
        self.qk_ready = sig("qk_ready", 2)
        self.v_ready = sig("v_ready", 1)
        self.part = sig("part_ready", 6)
        self.rest = sig("rest_ready", 4)
        self.spread_q = sig("spread_q", 9, 16)
        self.spread_k = sig("spread_k", 9, 16)
        self.a_scores = sig("a_scores", GROUPS * ATOPS)
        self.top = sig("top", GROUPS * ATOPS)
        self.top_step = sig("top_step", GROUPS * (6 if self.causal else 5))
        self.mT_ps = sig("mT_in_psum", GROUPS)
        self.mT_ready = sig("mT_ready", GROUPS)
        self.m_spread = sig("m_spread", GROUPS, 16)
        self.floor_ps = sig("floor_in_psum", HEADS)
        self.floor = sig("floor_ready", HEADS)
        self.b_scores = sig("b_scores", SLOTS)
        self.clipped = sig("clipped", 2 * SLOTS)
        self.probs = sig("probs", SLOTS)
        self.pv = sig("pv", 2 * GROUPS)
        self.oT_ready = sig("oT_ready", GROUPS)
        self.o_ps = sig("o_in_psum", NB)
        self.out_step = sig("out_step", NB * 8 - 2 if self.causal else NB)
        self.on_ready = sig("on_ready", NB)
        self.vsum_ps = sig("vsum_in_psum", 1)
        self.vsum_ready = sig("vsum_ready", 1)
        self.vsum_step = sig("vsum_step", 3)
        self.away_ready = sig("away_ready", 1)
        self.onT_ps = sig("onT_in_psum", 1)
        self.onT_ready = sig("onT_ready", 1)
        self.proj = sig("proj_ready", 1)
        self.biased = sig("biased", 1)
        self.moved = sig("result_stored", 1)
        self.setup = ctx.enter_context(nc.semaphore(kind + "_setup"))
        self.tables_made = ctx.enter_context(nc.semaphore(kind + "_tables_made"))

    def emit(self, nc, run, X, W):
        assert run == 0
        n, first, causal, kind = self.norm, 0, self.causal, self.kind
        wq, wproj = W[kind + "_wqkv"], W[kind + "_wproj"]
        with ExitStack() as ctx:
            pb = lambda name, banks=1: ctx.enter_context(nc.psum_tensor(f"{kind}_{name}", [P, banks * SEQ], F32))
            sb = lambda name, s, dt=F32: ctx.enter_context(nc.sbuf_tensor(f"{kind}_{name}", s, dt))
            n.buffers(ctx, nc, run)
            a_bank = [pb("a0"), pb("a1")]
            b_bank = [pb("b0", 2), pb("b1", 2)]
            o_bank = pb("o")
            m_bank = pb("m")
            m16 = m_bank[:, :].bitcast(BF16)
            xs = sb("xs", [P, 2, NB, DIM])
            hT = sb("hTs", [P, SEQ])
            full = sb("full", [P, 2, SEQ])
            t1 = sb("t1", [P, SEQ])
            t2 = sb("t2", [P, SEQ])
            rest = sb("rest", [P, SEQ])
            parts = sb("parts", [P, 2, SPLIT, SEQ], BF16)
            rep = {x: sb(x + "_rows", [ROWS + 1, 2, HEADS, SEQ], BF16) for x in "qk"}
            vs = sb("vs", [P, 2, NB, HEADS, PANE])
            tops = sb("tops", [P, 2, NB, HEADS])
            toprest = sb("toprest", [P, NB, 4])
            topp = sb("topp", [P, NB, SPLIT, 4], BF16)
            mT = sb("mT", [SPLIT * 4, SEQ], BF16)
            pT = sb("pT", [P, 2, 4, 2, SEQ] if not causal else [P, 2, 4, 2, SEQ])
            oT = sb("oT", [P, GROUPS, SEQ])
            den = sb("den", [P, 2, 3, HEADS])
            on = sb("on", [P, NB, HEADS, HD])
            onT = sb("onT", [P, SEQ])
            total = sb("total", [P, NB, DIM])
            if causal:
                floor = sb("floor", [P, 4, SEQ])
                away = sb("away", [P, NB, HEADS])
                vsum = sb("vsum", [P, NB, HEADS, HD])
                ot = sb("ot", [P, 2, 2, HEADS, HD])
                ones_rows = sb("ones_rows", [ROWS + 1, P], BF16)
                diag = sb("diag", [P, 2, P], BF16)
            block = ctx.enter_context(nc.Block())

            def width(kb):
                return P * kb if causal else 0

            def a_unit(s, i):
                a = 2 * s + i + 2 * ATOPS
                return a >= GROUPS * ATOPS, a % (GROUPS * ATOPS)

            HEAD = dict(norm=0, transpose=4, q=5, k=6, v=7) if causal else dict(norm=0, transpose=2, q=3, qs=4, k=5, ks=6, v=7)
            TOP = (2, 3, 4) if causal else (0, 1, 2)

            @block.sync
            def _(sp):
                for s in (self.spread_q, self.spread_k, self.m_spread):
                    sp.sem_inc(s.sem, s.credit())
                sp.wait_ge(self.setup, 1)

                def spread(g, par):
                    for x, (name, signal) in enumerate((("q", self.spread_q), ("k", self.spread_k))):
                        sp.wait_ge(self.part.sem, self.part.at(g, 3 * x + 3))
                        for i in range(SPLIT):
                            for j in range(SPLIT):
                                r = (SPLIT * i + j) * HD
                                sp.dma_start(rep[name][r:r + HD, par, :, :],
                                                              parts[:, x, (i, j)[x], :]).then_inc(signal.sem, 16)

                def spread_top(g, par, gr):
                    sp.wait_ge(self.mT_ready.sem, self.mT_ready.at(g, gr + 1))
                    sp.dma_start(rep["q"][PAIR_ROWS:ROWS, par, 4 * gr:4 * gr + 4, :], mT[:, :]).then_inc(self.m_spread.sem, 16)

                def head(g, par):
                    spread(g, par)
                    spread_top(g, par, 0)
                    spread_top(g, par, 1)

                def body(g, par, more):
                    if more:
                        spread(g + 1, 1 - par)
                    spread_top(g, par, 2)
                    spread_top(g, par, 3)
                    if more:
                        spread_top(g + 1, 1 - par, 0)
                        spread_top(g + 1, 1 - par, 1)

                pipeline(sp, first, head, body)

            @block.gpsimd
            def _(pl):
                for s in (n.rstd_ready, self.rest):
                    pl.sem_inc(s.sem, s.credit())
                pl.memset(rep["k"][64:ROWS + 1, :, :, :], 1.0).then_inc(self.setup, 1)
                pl.wait_ge(self.setup, 1)
                pl.memset(rep["q"][64:ROWS + 1, :, :, :], 0.0).then_inc(self.setup, 1)
                pl.wait_ge(self.setup, 2)
                pl.memset(vs[:, :, :, :, :], 0.0).then_inc(self.setup, 1)
                pl.wait_ge(self.setup, 3)
                pl.memset(vs[:, :, :, :, HD:HD + 1], 1.0).then_inc(self.setup, 1)

                def head(g, par):
                    n.pool(pl, g, W["minus_half"])
                    for x in range(2):
                        for i in range(2):
                            pl.wait_ge(self.part.sem, self.part.at(g, 3 * x + i + 1))
                            src = full[:, x, :] if i == 0 else rest[:, :]
                            pl.tensor_tensor(rest[:, :], src, parts[:, x, i, :], ALU.subtract)\
                                .then_inc(self.rest.sem, 1)

                def body(g, par, more):
                    if more:
                        head(g + 1, 1 - par)

                pipeline(pl, first, head, body)

            @block.vector
            def _(v):
                for s in (*n.of_vector, self.xs_ready, self.turn, self.top, self.top_step, self.clipped,
                          self.out_step, self.on_ready, self.vsum_step, self.biased, self.moved):
                    v.sem_inc(s.sem, s.credit())
                if not causal:
                    v.sem_inc(self.qk_ready.sem, self.qk_ready.credit())
                if causal:
                    v.tensor_copy(ones_rows[0:ROWS, :], W["ones_rows"]).then_inc(self.tables_made, 1)
                    v.tensor_copy(diag[:, :, :], W["diag"]).then_inc(self.tables_made, 1)

                def tokens(g, par):
                    v.wait_ge(self.moved.sem, self.moved.at(g, -1))
                    v.tensor_scalar(xs[:, par, :, :], slot(X, g, first), 1.0, None, ALU.mult)\
                        .then_inc(self.xs_ready.sem, 1)
                    v.wait_ge(self.xs_ready.sem, self.xs_ready.at(g, 1))
                    n.vector(v, g, par, xs[:, par, :, :], lambda: v.wait_ge(self.hT_ps.sem, self.hT_ps.at(g, -1)))

                def turn(g, x, swapped):
                    if not swapped:
                        v.wait_ge(self.made.sem, self.made.at(g, 2 * x + 1))
                        v.wait_ge(self.qk_ready.sem, self.qk_ready.at(g, x))
                        v.tensor_tensor(t1[:, :], m_bank[:, :], W["rope"][:, x, 0, :], ALU.mult)\
                            .then_inc(self.turn.sem, 1)
                    else:
                        v.wait_ge(self.made.sem, self.made.at(g, 2 * x + 2))
                        v.tensor_tensor(t2[:, :], m_bank[:, :], W["rope"][:, x, 1, :], ALU.mult)\
                            .then_inc(self.turn.sem, 1)
                        v.wait_ge(self.turn.sem, self.turn.at(g, 2 * x + 2))
                        v.wait_ge(self.rest.sem, self.rest.at(g, 2 * x + 1 - 4))
                        v.wait_ge(self.part.sem, self.part.at(g, 3 * x + 1 - 6))
                        v.tensor_tensor(full[:, x, :], t1[:, :], t2[:, :], ALU.add).then_inc(self.qk_ready.sem, 1)

                def top(g, par, a):
                    gr, b, j = a // ATOPS, a % ATOPS // 4, a % 4
                    v.wait_ge(self.a_scores.sem, self.a_scores.at(g, a + 1))
                    if a % ATOPS == 0:
                        v.wait_ge(self.top_step.sem, self.top_step.at(g, gr * self.top_step.per // GROUPS - 2 * self.top_step.per))
                    keys = P * (b + 1) if causal else SEQ
                    h = 4 * gr + j
                    v.tensor_reduce(tops[:, par, b, h:h + 1], a_bank[a % 2][:, 0:keys], AX.X, ALU.max,
                                                       negate=True).then_inc(self.top.sem, 1)

                def top_parts(g, par, gr):
                    n0 = gr * (self.top_step.per // GROUPS)
                    v.wait_ge(self.top.sem, self.top.at(g, ATOPS * (gr + 1)))
                    m = tops[:, par, :, 4 * gr:4 * gr + 4]
                    if causal:
                        v.wait_ge(self.away_ready.sem, self.away_ready.at(g, -1))
                        v.tensor_scalar(m, m, -100.0, 100.0, ALU.max, ALU.min).then_inc(self.top_step.sem, 1)
                        n0 += 1
                        v.wait_ge(self.top_step.sem, self.top_step.at(g, n0))
                    v.wait_ge(self.mT_ps.sem, self.mT_ps.at(g, gr))
                    for i in range(SPLIT):
                        src = m if i == 0 else toprest[:, :, :]
                        v.tensor_copy(topp[:, :, i, :], src).then_inc(self.top_step.sem, 1)
                        v.wait_ge(self.top_step.sem, self.top_step.at(g, n0 + 2 * i + 1))
                        if i < SPLIT - 1:
                            v.tensor_tensor(toprest[:, :, :], src, topp[:, :, i, :], ALU.subtract)\
                                .then_inc(self.top_step.sem, 1)
                            v.wait_ge(self.top_step.sem, self.top_step.at(g, n0 + 2 * i + 2))

                def clip(g, s):
                    gr, c, j = s // STEPS, s % STEPS // 4, s % 4
                    v.wait_ge(self.b_scores.sem, self.b_scores.at(g, s + 1))
                    v.wait_ge(self.floor.sem, self.floor.at(g, 4 * gr + j + 1))
                    v.wait_ge(self.pv.sem, self.pv.at(g, 2 * gr + c - 1))
                    for i in range(2):
                        q0 = width(2 * c + i)
                        v.scalar_tensor_tensor(
                            out=pT[:, c, j, i, q0:SEQ], in0=b_bank[s % 2][:, i * SEQ + q0:(i + 1) * SEQ], scalar=0.0,
                            in1=floor[:, j, q0:SEQ], op0=ALU.min, op1=ALU.max).then_inc(self.clipped.sem, 1)

                def v_sums(g):
                    v.wait_ge(self.vsum_ready.sem, self.vsum_ready.at(g, 1))
                    for i, b in enumerate((2, 1, 0)):
                        v.tensor_tensor(vsum[:, b, :, :], vsum[:, b, :, :], vsum[:, b + 1, :, :],
                                                                 ALU.add).then_inc(self.vsum_step.sem, 1)
                        v.wait_ge(self.vsum_step.sem, self.vsum_step.at(g, i + 1))

                def output(g, par, b):
                    o3 = a_bank[b % 2][:, :].rearrange("p (h c) -> p h c", c=PANE)
                    o, sums = o3[:, :, 0:HD], o3[:, :, HD]
                    bc = lambda t: t.unsqueeze(2).broadcast_to([P, HEADS, HD])
                    n0 = b * (8 if causal else 1)
                    d = lambda i: den[:, b % 2, i, :]
                    v.wait_ge(self.o_ps.sem, self.o_ps.at(g, b + 1))
                    v.wait_ge(self.onT_ps.sem, self.onT_ps.at(g, 0))
                    v.wait_ge(self.on_ready.sem, self.on_ready.at(g, b - 1))
                    if not causal:
                        v.reciprocal(d(0), sums).then_inc(self.out_step.sem, 1)
                        v.wait_ge(self.out_step.sem, self.out_step.at(g, n0 + 1))
                        v.tensor_tensor(on[:, b, :, :], o, bc(d(0)), ALU.mult).then_inc(self.on_ready.sem, 1)
                        return
                    v.scalar_tensor_tensor(out=d(0), in0=away[:, b, :], scalar=float(SEQ - P * (b + 1)), in1=sums,
                                           op0=ALU.mult, op1=ALU.add).then_inc(self.out_step.sem, 1)
                    v.wait_ge(self.out_step.sem, self.out_step.at(g, n0 + 1))
                    v.tensor_scalar(d(1), d(0), 1e-6, 1e-8, ALU.add, ALU.mult).then_inc(self.out_step.sem, 1)
                    v.wait_ge(self.out_step.sem, self.out_step.at(g, n0 + 2))
                    v.scalar_tensor_tensor(out=d(2), in0=d(1), scalar=float(SEQ), in1=d(0), op0=ALU.mult,
                                           op1=ALU.add).then_inc(self.out_step.sem, 1)
                    v.wait_ge(self.out_step.sem, self.out_step.at(g, n0 + 3))
                    v.reciprocal(d(2), d(2)).then_inc(self.out_step.sem, 1)
                    u, w = ot[:, b % 2, 0, :, :], ot[:, b % 2, 1, :, :]
                    v.tensor_tensor(u, vsum[:, 0, :, :], bc(d(1)), ALU.mult).then_inc(self.out_step.sem, 1)
                    v.wait_ge(self.out_step.sem, self.out_step.at(g, n0 + 5))
                    if b < NB - 1:
                        v.tensor_tensor(w, vsum[:, b + 1, :, :], bc(away[:, b, :]), ALU.mult)\
                            .then_inc(self.out_step.sem, 1)
                        v.wait_ge(self.out_step.sem, self.out_step.at(g, n0 + 6))
                        v.tensor_tensor(u, u, w, ALU.add).then_inc(self.out_step.sem, 1)
                        v.wait_ge(self.out_step.sem, self.out_step.at(g, n0 + 7))
                        n0 += 2
                    v.tensor_tensor(w, o, u, ALU.add).then_inc(self.out_step.sem, 1)
                    v.wait_ge(self.out_step.sem, self.out_step.at(g, n0 + 6))
                    v.tensor_tensor(on[:, b, :, :], w, bc(d(2)), ALU.mult).then_inc(self.on_ready.sem, 1)

                def result(g, par):
                    v.wait_ge(self.proj.sem, self.proj.at(g, 1))
                    out3 = m_bank[:, :].rearrange("p (b d) -> p b d", b=NB)
                    v.wait_ge(self.moved.sem, self.moved.at(g, 0))
                    if causal:
                        v.tensor_tensor(slot(X, g, first), out3, xs[:, par, :, :], ALU.add)\
                            .then_inc(self.moved.sem, 1)
                    else:
                        v.tensor_tensor(
                            total[:, :, :], out3, W["b_proj"].unsqueeze(1).broadcast_to([P, NB, DIM]), ALU.add)\
                                .then_inc(self.biased.sem, 1)
                        v.wait_ge(self.biased.sem, self.biased.at(g, 1))
                        v.tensor_tensor(slot(X, g, first), total[:, :, :], xs[:, par, :, :], ALU.add)\
                            .then_inc(self.moved.sem, 1)

                def head_step(g, par, name):
                    if name == "norm":
                        tokens(g, par)
                    if not causal and name in ("q", "qs", "k", "ks"):
                        turn(g, int(name[0] == "k"), name[-1] == "s")

                def head(g, par):
                    for name in HEAD:
                        head_step(g, par, name)
                    for gr in range(2):
                        for a in range(ATOPS * gr, ATOPS * (gr + 1)):
                            top(g, par, a)
                        top_parts(g, par, gr)

                def body(g, par, more):
                    for s in range(SLOTS):
                        gr, u = s // STEPS, s % STEPS
                        if u == TOP[0] and gr >= 1:
                            later, which = gr + 1 >= GROUPS, (gr + 1) % GROUPS
                            if not later:
                                top_parts(g, par, which)
                            elif more:
                                top_parts(g + 1, 1 - par, which)
                        if causal:
                            clip(g, s)
                        for i in range(2):
                            later, a = a_unit(s, i)
                            if not later:
                                top(g, par, a)
                            elif more:
                                top(g + 1, 1 - par, a)
                        if more:
                            for name, at in HEAD.items():
                                if at == s:
                                    head_step(g + 1, 1 - par, name)
                    if more:
                        top_parts(g + 1, 1 - par, 1)
                    if causal:
                        v_sums(g)
                        v.wait_ge(self.away_ready.sem, self.away_ready.at(g, 1))
                    for b in range(NB):
                        output(g, par, b)
                    result(g, par)

                pipeline(v, first, head, body)

            @block.scalar
            def _(act):
                for s in (self.hT_ready, self.v_ready, self.part, self.mT_ready, self.floor, self.probs, self.oT_ready,
                          self.vsum_ready, self.away_ready, self.onT_ready):
                    act.sem_inc(s.sem, s.credit())
                if causal:
                    act.sem_inc(self.qk_ready.sem, self.qk_ready.credit())
                act.wait_ge(self.setup, 4)
                copy = lambda o, i: act.activation(o, i, ACT.Copy)

                def split(g, x):
                    act.wait_ge(self.qk_ready.sem, self.qk_ready.at(g, x + 1))
                    for i in range(SPLIT):
                        act.wait_ge((self.spread_q, self.spread_k)[x].sem, (self.spread_q, self.spread_k)[x].at(g, 0))
                        if i:
                            act.wait_ge(self.rest.sem, self.rest.at(g, 2 * x + i))
                        copy(parts[:, x, i, :], full[:, x, :] if i == 0 else rest[:, :]).then_inc(self.part.sem, 1)

                def head_step(g, par, name):
                    if name == "transpose":
                        act.wait_ge(self.hT_ps.sem, self.hT_ps.at(g, 1))
                        act.wait_ge(self.made.sem, self.made.at(g, 0))
                        copy(hT[:, :], m_bank[:, :]).then_inc(self.hT_ready.sem, 1)
                    elif name in ("q", "k") and causal:
                        x = int(name == "k")
                        act.wait_ge(self.made.sem, self.made.at(g, x + 1))
                        act.wait_ge(self.rest.sem, self.rest.at(g, 2 * x + 1 - 4))
                        act.activation(full[:, x, :], m_bank[:, :], ACT.Copy,
                                                               scale=1.0 if x else float(HD) ** -0.5)\
                                                                   .then_inc(self.qk_ready.sem, 1)
                        act.wait_ge(self.qk_ready.sem, self.qk_ready.at(g, x + 1))
                        split(g, x)
                    elif name in ("qs", "ks") and not causal:
                        split(g, int(name == "ks"))
                    elif name == "v":
                        act.wait_ge(self.made.sem, self.made.at(g, self.made.per))
                        act.wait_ge(self.pv.sem, self.pv.at(g, -2 * GROUPS))
                        if causal:
                            act.wait_ge(self.vsum_ps.sem, self.vsum_ps.at(g, -1))
                        copy(vs[:, par, :, :, 0:HD],
                                                    m_bank[:, :].rearrange("p (b h d) -> p b h d", b=NB, d=HD))\
                                                        .then_inc(self.v_ready.sem, 1)

                def take_mT(g, gr):
                    act.wait_ge(self.mT_ps.sem, self.mT_ps.at(g, gr + 1))
                    act.wait_ge(self.m_spread.sem, self.m_spread.at(g, gr))
                    copy(mT[:, :], m16[0:SPLIT * 4, 0:SEQ]).then_inc(self.mT_ready.sem, 1)

                def take_floor(g, h):
                    act.wait_ge(self.floor_ps.sem, self.floor_ps.at(g, h + 1))
                    act.wait_ge(self.clipped.sem, self.clipped.at(g, 2 * STEPS * (h // 4)))
                    act.activation(floor[:, h % 4, :], m_bank[:, :], ACT.Identity,
                                                        bias=W["minus_100"]).then_inc(self.floor.sem, 1)

                def exp(g, s):
                    gr, c, j = s // STEPS, s % STEPS // 4, s % 4
                    if causal:
                        act.wait_ge(self.clipped.sem, self.clipped.at(g, 2 * s + 2))
                        for i in range(2):
                            q0 = width(2 * c + i)
                            p_ = pT[:, c, j, i, q0:SEQ]
                            ins = act.activation(p_, p_, ACT.Exp)
                        ins.then_inc(self.probs.sem, 1)
                    else:
                        act.wait_ge(self.b_scores.sem, self.b_scores.at(g, s + 1))
                        act.wait_ge(self.pv.sem, self.pv.at(g, 2 * gr + c - 1))
                        act.activation(pT[:, c, j, :, :].rearrange("p a b -> p (a b)"),
                                                            b_bank[s % 2][:, :], ACT.Exp).then_inc(self.probs.sem, 1)

                def take_o(g, gr):
                    act.wait_ge(self.pv.sem, self.pv.at(g, 2 * gr + 2))
                    act.wait_ge(self.o_ps.sem, self.o_ps.at(g, 0))
                    copy(oT[:, gr, :], o_bank[:, :]).then_inc(self.oT_ready.sem, 1)

                def head(g, par):
                    for name in HEAD:
                        head_step(g, par, name)
                    for gr in range(2):
                        take_mT(g, gr)
                    if causal:
                        take_floor(g, 0)

                def body(g, par, more):
                    for s in range(SLOTS + 2):
                        gr, u = s // STEPS, s % STEPS
                        if s < SLOTS:
                            if causal and s > 0 and u < 4:
                                take_floor(g, 4 * gr + u)
                            exp(g, s)
                            if more:
                                for name, at in HEAD.items():
                                    if at == s:
                                        head_step(g + 1, 1 - par, name)
                            if u == TOP[2] and gr >= 1:
                                later, which = gr + 1 >= GROUPS, (gr + 1) % GROUPS
                                if not later:
                                    take_mT(g, which)
                                elif more:
                                    take_mT(g + 1, which)
                        if s >= STEPS + 1 and (s - STEPS - 1) % STEPS == 0:
                            take_o(g, (s - STEPS - 1) // STEPS)
                    if more:
                        take_mT(g + 1, 1)
                    if causal:
                        act.wait_ge(self.vsum_ps.sem, self.vsum_ps.at(g, 1))
                        act.wait_ge(self.on_ready.sem, self.on_ready.at(g, 0))
                        copy(vsum[:, :, :, :],
                                                       m_bank[:, :].rearrange("p (b h d) -> p b h d", b=NB, d=HD))\
                                                           .then_inc(self.vsum_ready.sem, 1)
                        act.wait_ge(self.top_step.sem, self.top_step.at(g, self.top_step.per))
                        act.activation(away[:, :, :], tops[:, par, :, :], ACT.Exp,
                                                                 bias=W["minus_100"]).then_inc(self.away_ready.sem, 1)
                    act.wait_ge(self.onT_ps.sem, self.onT_ps.at(g, 1))
                    act.wait_ge(self.proj.sem, self.proj.at(g, 0))
                    copy(onT[:, :], m_bank[:, :]).then_inc(self.onT_ready.sem, 1)
                    if causal and more:
                        take_floor(g + 1, 0)

                pipeline(act, first, head, body)

            @block.tensor
            def _(pe):
                for s in (self.hT_ps, self.made, self.a_scores, self.mT_ps, self.floor_ps, self.b_scores, self.pv,
                          self.o_ps, self.vsum_ps, self.onT_ps, self.proj):
                    pe.sem_inc(s.sem, s.credit())
                pe.wait_ge(self.setup, 4)
                if causal:
                    pe.wait_ge(self.tables_made, 2)


                def head_step(g, par, name):
                    mul = lambda o, l, r: pe.matmul(o, l, r, start=True, stop=True)
                    col = lambda i: slice(i * P, (i + 1) * P)
                    if name == "transpose":
                        for b in range(NB):
                            pe.wait_ge(n.out_ready.sem, n.out_ready.at(g, b + 1))
                            ins = pe.transpose(m_bank[:, col(b)], n.out[:, par, b, :], W["ident"])
                        ins.then_inc(self.hT_ps.sem, 1)
                    elif name in ("q", "k", "qs", "ks"):
                        x = int(name[0] == "k")
                        if causal:
                            if len(name) == 2:
                                return
                            if x:
                                pe.wait_ge(self.qk_ready.sem, self.qk_ready.at(g, 1))
                            i = x
                        else:
                            if name != "q":
                                pe.wait_ge(self.turn.sem, self.turn.at(g, 2 * x + len(name) - 1))
                            i = x + (2 if len(name) == 2 else 0)
                        pe.wait_ge(self.hT_ready.sem, self.hT_ready.at(g, 1))
                        mul(m_bank[:, :], wq[:, col(i)], hT[:, :]).then_inc(self.made.sem, 1)
                    elif name == "v":
                        if causal:
                            pe.wait_ge(self.qk_ready.sem, self.qk_ready.at(g, 2))
                        else:
                            pe.wait_ge(self.turn.sem, self.turn.at(g, 4))
                        i = 2 if causal else 4
                        for b in range(NB):
                            ins = mul(m_bank[:, col(b)], hT[:, col(b)], wq[:, col(i)])
                        ins.then_inc(self.made.sem, 1)

                def a_scores(g, par, a):
                    gr, b, j = a // ATOPS, a % ATOPS // 4, a % 4
                    h = 4 * gr + j
                    if a == 0:
                        pe.wait_ge(self.spread_q.sem, self.spread_q.at(g, 9))
                        pe.wait_ge(self.spread_k.sem, self.spread_k.at(g, 9))
                    bank = a_bank[a % 2]
                    pe.wait_ge(self.top.sem, self.top.at(g, a - 1))
                    if a in (2 * ATOPS, 2 * ATOPS + 1):
                        pe.wait_ge(self.on_ready.sem, self.on_ready.at(g, a - 2 * ATOPS - 1))
                    keys = P * (b + 1) if causal else SEQ
                    ins = pe.matmul(bank[:, 0:keys], rep["q"][0:PAIR_ROWS, par, h, b * P:(b + 1) * P],
                                    rep["k"][0:PAIR_ROWS, par, h, 0:keys], start=True, stop=not causal)
                    if causal:
                        ins = pe.matmul(bank[:, keys - P:keys], W["ident16"], diag[:, 0, :], start=False, stop=True)
                    ins.then_inc(self.a_scores.sem, 1)

                def transpose_tops(g, gr):
                    pe.wait_ge(self.top_step.sem, self.top_step.at(g, (gr + 1) * self.top_step.per // GROUPS))
                    for b in range(NB):
                        ins = pe.transpose(m16[0:SPLIT * 4, b * P:(b + 1) * P],
                                           topp[:, b, :, :].rearrange("p i j -> p (i j)"), W["ident16"])
                    ins.then_inc(self.mT_ps.sem, 1)

                def floors(g, par, h):
                    if h % 4:
                        pe.wait_ge(self.floor.sem, self.floor.at(g, h))
                    pe.wait_ge(self.m_spread.sem, self.m_spread.at(g, h // 4 + 1))
                    pe.matmul(m_bank[:, :], ones_rows[0:ROWS, :], rep["q"][0:ROWS, par, h, :],
                                                      start=True, stop=True).then_inc(self.floor_ps.sem, 1)

                def b_scores(g, par, s):
                    gr, c, j = s // STEPS, s % STEPS // 4, s % 4
                    h = 4 * gr + j
                    pe.wait_ge(self.m_spread.sem, self.m_spread.at(g, gr + 1))
                    if causal:
                        pe.wait_ge(self.clipped.sem, self.clipped.at(g, 2 * (s - 1)))
                    else:
                        pe.wait_ge(self.probs.sem, self.probs.at(g, s - 1))
                    for i in range(2):
                        kb = 2 * c + i
                        q0 = width(kb)
                        o = b_bank[s % 2][:, i * SEQ + q0:(i + 1) * SEQ]
                        ins = pe.matmul(o, rep["k"][0:ROWS, par, h, kb * P:(kb + 1) * P],
                                        rep["q"][0:ROWS, par, h, q0:SEQ], start=True, stop=not causal)
                        if causal:
                            ins = pe.matmul(o[:, 0:P], W["ident16"], diag[:, 1, :], start=False, stop=True)
                    ins.then_inc(self.b_scores.sem, 1)

                def times_v(g, par, e):
                    gr, c = e // 2, e % 2
                    pe.wait_ge(self.probs.sem, self.probs.at(g, 4 * e + 4))
                    if e == 0:
                        pe.wait_ge(self.v_ready.sem, self.v_ready.at(g, 1))
                    if c == 0:
                        pe.wait_ge(self.oT_ready.sem, self.oT_ready.at(g, gr))
                    for i in range(2):
                        kb = 2 * c + i
                        q0 = width(kb)
                        for j in range(4):
                            ins = pe.matmul(o_bank[PANE * j:PANE * (j + 1), q0:SEQ], vs[:, par, kb, 4 * gr + j, :],
                                            pT[:, c, j, i, q0:SEQ], start=(kb == 0), stop=(kb == NB - 1))
                    ins.then_inc(self.pv.sem, 1)

                def tail(g, par, more):
                    last = (g + 1, 2) if more else (g, GROUPS)
                    pe.wait_ge(self.mT_ready.sem, self.mT_ready.at(*last))
                    if causal:
                        pe.wait_ge(self.floor.sem, self.floor.at(g, HEADS))
                        for b in range(NB):
                            ins = pe.matmul(m_bank[:, b * P:(b + 1) * P], W["ones"],
                                            vs[:, par, b, :, 0:HD], start=True, stop=True)
                        ins.then_inc(self.vsum_ps.sem, 1)
                    pe.wait_ge(self.oT_ready.sem, self.oT_ready.at(g, GROUPS))
                    for b in range(NB):
                        if b < 2:
                            pe.wait_ge(self.top.sem, self.top.at(g + 1, (2 * ATOPS if more else 0) - 1 + b))
                        else:
                            pe.wait_ge(self.on_ready.sem, self.on_ready.at(g, b - 1))
                        for gr in range(GROUPS):
                            ins = pe.transpose(a_bank[b % 2][:, gr * P:(gr + 1) * P], oT[:, gr, b * P:(b + 1) * P],
                                               W["ident"])
                        ins.then_inc(self.o_ps.sem, 1)
                    if causal:
                        pe.wait_ge(self.vsum_ready.sem, self.vsum_ready.at(g, 1))
                    for b in range(NB):
                        pe.wait_ge(self.on_ready.sem, self.on_ready.at(g, b + 1))
                        ins = pe.transpose(m_bank[:, b * P:(b + 1) * P], on[:, b, :, :].rearrange("p h d -> p (h d)"),
                                           W["ident"])
                    ins.then_inc(self.onT_ps.sem, 1)
                    pe.wait_ge(self.onT_ready.sem, self.onT_ready.at(g, 1))
                    for b in range(NB):
                        ins = pe.matmul(m_bank[:, b * P:(b + 1) * P], onT[:, b * P:(b + 1) * P], wproj,
                                        start=True, stop=True)
                    ins.then_inc(self.proj.sem, 1)
                    if causal and more:
                        pe.wait_ge(self.moved.sem, self.moved.at(g, 1))
                        floors(g + 1, 1 - par, 0)

                def head(g, par):
                    for name in HEAD:
                        head_step(g, par, name)
                    for gr in range(2):
                        for a in range(ATOPS * gr, ATOPS * (gr + 1)):
                            a_scores(g, par, a)
                        if gr == 0:
                            pe.wait_ge(self.v_ready.sem, self.v_ready.at(g, 1))
                        else:
                            pe.wait_ge(self.mT_ready.sem, self.mT_ready.at(g, 1))
                        transpose_tops(g, gr)
                    if causal:
                        pe.wait_ge(self.mT_ready.sem, self.mT_ready.at(g, 2))
                        floors(g, par, 0)

                def body(g, par, more):
                    for s in range(SLOTS + 2):
                        gr, u = s // STEPS, s % STEPS
                        if s < SLOTS:
                            if causal and 0 < s and u < 4:
                                if s == STEPS and more:
                                    pe.wait_ge(self.v_ready.sem, self.v_ready.at(g + 1, 1))
                                elif u == 0:
                                    pe.wait_ge(self.mT_ready.sem, self.mT_ready.at(g, gr + 1))
                                floors(g, par, 4 * gr + u)
                            b_scores(g, par, s)
                            for i in range(2):
                                later, a = a_unit(s, i)
                                if not later:
                                    a_scores(g, par, a)
                                elif more:
                                    a_scores(g + 1, 1 - par, a)
                            if more:
                                for name, at in HEAD.items():
                                    if at == s:
                                        if name == "transpose" and causal:
                                            pe.wait_ge(self.floor.sem, self.floor.at(g, 4))
                                        elif name == "transpose":
                                            pe.wait_ge(self.moved.sem, self.moved.at(g, 0))
                                            pe.wait_ge(self.mT_ready.sem, self.mT_ready.at(g, 2))
                                        head_step(g + 1, 1 - par, name)
                            if u == TOP[1] and gr >= 1:
                                if causal:
                                    pe.wait_ge(self.floor.sem, self.floor.at(g, 4 * gr + 4))
                                elif gr > 1:
                                    pe.wait_ge(self.mT_ready.sem, self.mT_ready.at(g, gr + 1))
                                elif more:
                                    pe.wait_ge(self.v_ready.sem, self.v_ready.at(g + 1, 1))
                                else:
                                    pe.wait_ge(self.moved.sem, self.moved.at(g, 0))
                                later, which = gr + 1 >= GROUPS, (gr + 1) % GROUPS
                                if not later:
                                    transpose_tops(g, which)
                                elif more:
                                    transpose_tops(g + 1, which)
                        if s >= 5 and (s - 5) % 4 == 0:
                            times_v(g, par, (s - 5) // 4)
                    if more:
                        pe.wait_ge(self.mT_ready.sem, self.mT_ready.at(g + 1, 1))
                        transpose_tops(g + 1, 1)
                    tail(g, par, more)

                pipeline(pe, first, head, body)


MOE_ARRAYS = {"lower": [P, NB * EXPERTS, EXPERTS], "wg": [P, EXPERTS], "wup": [P, MOE_UP_COLS],
              "wdm": [P, 1 + EXPERTS, DIM], "wdt": [P, MOE_PASSES, DIM]}
CAUSAL_ARRAYS = {"causal_wqkv": [P, 3 * P], "causal_wproj": [P, DIM], "diag": [P, 2, P], "ones": [P, P],
                 "ones_rows": [ROWS, P], "minus_100": [P, 1]}
ROTARY_ARRAYS = {"rotary_wqkv": [P, 5 * P], "rotary_wproj": [P, DIM], "b_proj": [P, DIM], "rope": [P, 2, 2, SEQ]}
LOCAL_ARRAYS = {"wqkv": [P, DEPTH, 3 * INNER], "wo": [P, DEPTH, PAIRS, DIM], "qk_scale": [P, DEPTH, 2, LD],
                "qk_scale_swapped": [P, DEPTH, 2, LD], "turn_cos": [P, NB, 2, LD], "turn_sin": [P, NB, 2, LD],
                "band": [P, 2, 2 * BAND], "w1": [P, DEPTH, 2 * HID], "w2": [P, DEPTH, 3, DIM], "b1": [P, DEPTH, 6],
                "b2": [P, DEPTH, DIM], "ln_g": [P, DEPTH], "ln_b": [P, DEPTH]}
STAGES = ["moe", "causal", "moe", "local", "rotary", "local"]


class Loader:

    def __init__(self, ctx, nc, ins):
        self.nc, self.ins, self.count = nc, ins, 0
        self.sem = ctx.enter_context(nc.semaphore("loaded"))

    def load(self, ctx, name, arrays, sp):
        W = {}
        for n, s in arrays.items():
            W[n] = ctx.enter_context(self.nc.sbuf_tensor(f"{name}_{n}", s, F32))[tuple(slice(None) for _ in s)]
            sp.dma_start(W[n], self.ins[n]).then_inc(self.sem, 16)
            self.count += 16
        return W


def program(nc, ins, out, stages):
    with ExitStack() as ctx:
        sb = lambda n, s, dt=F32: ctx.enter_context(nc.sbuf_tensor(n, s, dt))
        X = sb("X", [P, NSEQ * NB, DIM])
        common = {"ident16": sb("ident16", [P, P], BF16)[:, :]}
        loader = Loader(ctx, nc, ins)
        stored = ctx.enter_context(nc.semaphore("stored"))
        made = ctx.enter_context(nc.semaphore("made"))
        with nc.Block() as block:
            @block.sync
            def _(sp):
                common.update(loader.load(ctx, "common", {"ident": [P, P], "minus_half": [P, 64]}, sp))
                x = ins["x"].rearrange("(n p) d -> p n d", p=P)
                for s in range(0, NSEQ, 4):
                    sp.dma_start(X[:, s * NB:(s + 4) * NB, :], x[:, s * NB:(s + 4) * NB, :]).then_inc(loader.sem, 16)
                    loader.count += 16
                sp.wait_ge(loader.sem, loader.count)
        with nc.Block() as block:
            @block.vector
            def _(v):
                v.tensor_copy(common["ident16"], common["ident"]).then_inc(made, 1)
                v.wait_ge(made, 1)
        kinds = {"moe": Moe(ctx, nc), "ffn": Geglu(ctx, nc), "attention": LocalAttention(ctx, nc)}
        arrays = {"moe": MOE_ARRAYS, "causal": CAUSAL_ARRAYS, "rotary": ROTARY_ARRAYS, "local": LOCAL_ARRAYS}
        runs = {}
        for number, kind in enumerate(stages):
            with ExitStack() as own:
                W = dict(common)
                with nc.Block() as block:
                    @block.sync
                    def _(sp):
                        W.update(loader.load(own, f"stage{number}", arrays[kind.split("_")[0]], sp))
                        sp.wait_ge(loader.sem, loader.count)
                run = runs.setdefault(kind.split("_")[0], 0)
                runs[kind.split("_")[0]] += 1
                if kind in ("causal", "rotary"):
                    GlobalAttention(own, nc, kind).emit(nc, 0, X, W)
                elif kind == "moe":
                    kinds["moe"].emit(nc, run, X, W)
                else:
                    local_tables(nc, own, W, made, 1 + run * (1 + 2 * DEPTH), number)
                    if kind == "local_attention":
                        kinds["attention"].emit(nc, 0, X, X, W, 1)
                    elif kind == "local_ffn":
                        kinds["ffn"].emit(nc, 0, X, X, W, 1, False)
                    else:
                        Y = own.enter_context(nc.sbuf_tensor(f"stage{number}_Y", [P, NSEQ * NB, DIM], F32))
                        for layer in range(DEPTH):
                            kinds["attention"].emit(nc, DEPTH * run + layer, X, Y, W, layer)
                            kinds["ffn"].emit(nc, DEPTH * run + layer, X, Y, W, layer, layer == DEPTH - 1)
        with nc.Block() as block:
            @block.sync
            def _(sp):
                y = out.rearrange("(n p) d -> p n d", p=P)
                for s in range(0, NSEQ, 4):
                    sp.dma_start(y[:, s * NB:(s + 4) * NB, :], X[:, s * NB:(s + 4) * NB, :]).then_inc(stored, 16)
                sp.wait_ge(stored, 16 * (NSEQ // 4))


def local_tables(nc, ctx, W, made, count, number):
    sb = lambda n, s, dt=F32: ctx.enter_context(nc.sbuf_tensor(f"stage{number}_{n}", s, dt))
    band16 = sb("band16", [P, 2, 2 * BAND], BF16)
    turn = {n: sb(n + "_scaled", [P, DEPTH, NB, 2, LD]) for n in ("turn_cos", "turn_sin")}
    with nc.Block() as block:
        @block.vector
        def _(v):
            v.tensor_copy(band16[:, :, :], W["band"]).then_inc(made, 1)
            for name, scale in (("turn_cos", "qk_scale"), ("turn_sin", "qk_scale_swapped")):
                for l in range(DEPTH):
                    v.tensor_tensor(turn[name][:, l, :, :, :], W[name],
                                    W[scale][:, l, :, :].unsqueeze(1).broadcast_to([P, NB, 2, LD]), ALU.mult)\
                        .then_inc(made, 1)
            v.wait_ge(made, count + 1 + 2 * DEPTH)
    W["band"] = band16[:, :, :]
    for name, t in turn.items():
        W[name] = t[:, :, :, :, :]


def constants():
    e = np.arange(EXPERTS)
    lower = (e[None, :] < e[:, None]).astype(np.float32)
    half = np.arange(0, LD, 2, dtype=np.float32)
    pos = np.arange(SEQ, dtype=np.float32)
    freqs = pos[:, None] * (1.0 / 10000.0 ** (half / LD)).astype(np.float32)[None, :]
    power = (pos - SEQ // 2) / float(WINDOW // 2)
    scale = ((half + 0.4 * LD) / (1.4 * LD))[None, :] ** power[:, None]
    two = lambda t: np.concatenate([t, t], 1)
    cos, scale = two(np.cos(freqs)), two(scale)
    sin = np.concatenate([-np.sin(freqs), np.sin(freqs)], 1)
    blocks = lambda q, k: np.ascontiguousarray(
        np.stack([8.0 * q, k], 1).reshape(NB, P, 2, LD).transpose(1, 0, 2, 3), dtype=np.float32)
    lag = np.arange(P)[:, None] + WINDOW - np.arange(BAND)[None, :]
    seen = (lag >= 0) & (lag <= WINDOW)
    band = np.stack([np.where(seen & (np.arange(BAND) >= WINDOW), 0, -1e30), np.where(seen, 0, -1e30)], 1)
    theta = (1.0 / 10000.0 ** (np.arange(0, HD, 2, dtype=np.float32) / HD) * 3.0).astype(np.float32)
    ang = pos[:, None] * theta[None, :]
    by_d = lambda t: np.repeat(t.T, HEADS, 0)
    rc = by_d(np.repeat(np.cos(ang), 2, 1))
    rs = by_d(np.stack([-np.sin(ang), np.sin(ang)], 2).reshape(SEQ, HD))
    f = np.float32(HD ** -0.5)
    later = np.where(np.arange(P)[None, :] > np.arange(P)[:, None], -1e30, 0)
    ones_rows = np.zeros((ROWS, P), np.float32)
    ones_rows[PAIR_ROWS:] = 1
    return {
        "rope": np.ascontiguousarray(np.stack([np.stack([rc * f, rs * f], 1), np.stack([rc, rs], 1)], 1), np.float32),
        "diag": np.ascontiguousarray(np.stack([later, later.T], 1), np.float32),
        "ones": np.ones((P, P), np.float32),
        "ones_rows": ones_rows,
        "minus_100": np.full((P, 1), -100.0, np.float32),
        "turn_cos": blocks(cos * scale, cos / scale),
        "turn_sin": blocks(sin * scale, sin / scale),
        "band": np.ascontiguousarray(np.concatenate([band, band], 2), dtype=np.float32),
        "ident": np.eye(P, dtype=np.float32),
        "lower": np.ascontiguousarray(np.broadcast_to(np.tile(lower, (NB, 1)), (P, NB * EXPERTS, EXPERTS))),
        "minus_half": np.full((P, 64), -0.5, np.float32),
    }


def layouts(a):
    up = np.concatenate([np.asarray(a["L0_ffn_w_up"]),
                         np.concatenate([a["L0_ffn_sg_gate"], a["L0_ffn_sg_up"]], 0)[None]], 0)
    down = np.concatenate([np.asarray(a["L0_ffn_w_down"]), np.asarray(a["L0_ffn_sg_down"])[None]], 0)
    S = EXPERTS
    rows = [up[S, 0:P], up[S, HALF:HALF + P], up[S, P:HALF], up[S, HALF + P:]]
    for p in range(EXPERTS // 2):
        for e in (2 * p, 2 * p + 1):
            rows += [up[e, 0:P], up[e, HALF:HALF + P]]
        rows += [up[e, o + P:o + HALF] for o in (0, HALF) for e in (2 * p, 2 * p + 1)]
    order = [S, *range(EXPERTS)]
    tail = np.zeros((MOE_PASSES, P, DIM), np.float32)
    tail[0, 0:TAIL] = down[S, :, P:].T
    for p in range(EXPERTS // 2):
        tail[1 + p] = np.concatenate([down[2 * p, :, P:].T, down[2 * p + 1, :, P:].T], 0)
    c = np.ascontiguousarray
    f32 = lambda n: np.asarray(a["L1_ffn_" + n])

    def blocks(rows):
        out = np.zeros((P, DEPTH, 3, rows.shape[-1]), np.float32)
        for j, (r, m) in enumerate(HID_BLOCKS):
            out[0:m, :, j] = rows[:, r:r + m].transpose(1, 0, 2)
        return out

    def global_qkv(w, swapped):
        q, k = (w[:, i * DIM:(i + 1) * DIM].reshape(DIM, HEADS, HD).transpose(0, 2, 1) for i in range(2))
        pairs = [x.reshape(DIM, HD // 2, 2, HEADS)[:, :, ::-1] for x in (q, k)] if swapped else []
        return c(np.concatenate([x.reshape(DIM, DIM) for x in (q, k, *pairs)] + [w[:, 2 * DIM:]], 1))

    scales = np.stack([f32("q_scale"), f32("k_scale")], 1)
    b1 = f32("b1")[:, :, None]
    spread = lambda t: c(np.broadcast_to(t, (P, *t.shape)))
    return {
        "causal_wqkv": global_qkv(np.asarray(a["L0_attn_w_qkv"]).T, False),
        "causal_wproj": c(np.asarray(a["L0_attn_w_proj"]).T),
        "rotary_wqkv": global_qkv(np.asarray(a["L1_attn_w_qkv"]), True),
        "rotary_wproj": c(np.asarray(a["L1_attn_w_proj"])),
        "b_proj": spread(np.asarray(a["L1_attn_b_proj"])),
        "wqkv": c(f32("wqkv").transpose(1, 0, 2)),
        "wo": c(f32("wo").reshape(DEPTH, PAIRS, P, DIM).transpose(2, 0, 1, 3)),
        "qk_scale": spread(scales),
        "qk_scale_swapped": spread(np.concatenate([scales[..., LD // 2:], scales[..., :LD // 2]], -1)),
        "w1": c(f32("w1").transpose(1, 0, 2)),
        "w2": blocks(f32("w2")),
        "b1": c(np.concatenate([blocks(b1[:, :HID]), blocks(b1[:, HID:])], 2)[..., 0]),
        "b2": spread(f32("b2")),
        "ln_g": c(f32("ln_g").T),
        "ln_b": c(f32("ln_b").T),
        "x": c(np.asarray(a["L0_attn_x"]).reshape(NSEQ * SEQ, DIM)),
        "wg": c(np.asarray(a["L0_ffn_gate_w"]).T),
        "wup": c(np.concatenate(rows, 0).T),
        "wdm": c(down[order, :, 0:P].transpose(2, 0, 1)),
        "wdt": c(tail.transpose(1, 0, 2)),
    }


def kernel(**inputs):
    import concourse.bacc as bacc
    from concourse.bass_utils import run_bass_kernel_spmd

    nc = bacc.Bacc("TRN2", target_bir_lowering=False, num_devices=1)
    arrays = {**layouts(inputs), **constants()}
    ins = {n: nc.dram_tensor(n + "_in", a.shape, mybir.dt.from_np(a.dtype), kind="ExternalInput").ap()
           for n, a in arrays.items()}
    out = nc.dram_tensor("out", (NSEQ * SEQ, DIM), F32, kind="ExternalOutput").ap()
    program(nc, ins, out, STAGES)
    r = run_bass_kernel_spmd(nc, [{n + "_in": a for n, a in arrays.items()}], core_ids=[0])
    return r.results[0]["out"].reshape(NSEQ, SEQ, DIM)
```

```python
from contextlib import ExitStack

import numpy as np

import concourse.bass as bass
from concourse import mybir

F32 = mybir.dt.float32
BF16 = mybir.dt.bfloat16
ALU = mybir.AluOpType
ACT = mybir.ActivationFunctionType
AX = mybir.AxisListType

P = 128
NSEQ, SEQ, DIM = 16, 512, 128
NB = SEQ // P
EXPERTS, HALF = 8, 192
TAIL = HALF - P
HEADS, HD = 16, 8
LH, LD = 8, 64
INNER = LH * LD
WINDOW = 64
HID = 341
DEPTH = 2
LN_EPS = 1e-5


class Signal:

    def __init__(self, ctx, nc, name, per, unit=1):
        self.sem = ctx.enter_context(nc.semaphore(name))
        self.per, self.unit = per, unit

    def at(self, g, n):
        return g * (self.per * self.unit) + n * self.unit

    def credit(self):
        return 2 * self.per * self.unit


class Norm:

    behind = 0

    def __init__(self, ctx, nc, name):
        sig = lambda n, per: Signal(ctx, nc, f"{name}_{n}", per)
        self.name = name
        self.stats_ready = sig("stats_ready", NB)
        self.moment = sig("moment", 6)
        self.veps_ready = sig("veps_ready", 1)
        self.rstd_ready = sig("rstd_ready", 1)
        self.out_ready = sig("out_ready", NB)
        self.of_vector = [self.stats_ready, self.moment, self.veps_ready, self.out_ready]

    def buffers(self, ctx, nc, stage):
        sb = lambda n, s: ctx.enter_context(nc.sbuf_tensor(f"{self.name}{stage}_{n}", s, F32))
        self.stats = sb("stats", [P, NB, 6])
        self.mean = sb("mean", [P, NB])
        self.diff = sb("diff", [P, NB])
        self.veps = sb("veps", [P, NB])
        self.rstd = sb("rstd", [P, NB])
        self.out = sb("out", [P, 2, NB, DIM])

    def vector(self, v, g, par, src, out_free):
        self.vector_stats(v, g, src)
        self.vector_apply(v, g, par, src, out_free)

    def vector_stats(self, v, g, src):
        g = g - self.behind
        for b in range(NB):
            v.bn_stats(self.stats[:, b, :], src[:, b, :]).then_inc(self.stats_ready.sem, 1)
        me, mo = self.stats[:, :, 1], self.stats[:, :, 4]
        v.wait_ge(self.stats_ready.sem, self.stats_ready.at(g, NB))
        v.wait_ge(self.rstd_ready.sem, self.rstd_ready.at(g, 0))
        v.wait_ge(self.moment.sem, self.moment.at(g, 0))
        v.tensor_tensor(self.veps[:, :], self.stats[:, :, 2], self.stats[:, :, 5], ALU.add)\
            .then_inc(self.moment.sem, 1)
        v.tensor_tensor(self.diff[:, :], me, mo, ALU.subtract).then_inc(self.moment.sem, 1)
        v.tensor_tensor(self.mean[:, :], me, mo, ALU.add).then_inc(self.moment.sem, 1)
        v.wait_ge(self.moment.sem, self.moment.at(g, 1))
        v.tensor_scalar(self.veps[:, :], self.veps[:, :], 1.0 / DIM, LN_EPS, ALU.mult, ALU.add)\
            .then_inc(self.moment.sem, 1)
        v.wait_ge(self.moment.sem, self.moment.at(g, 2))
        v.scalar_tensor_tensor(out=self.diff[:, :], in0=self.diff[:, :], scalar=0.25, in1=self.diff[:, :],
                                    op0=ALU.mult, op1=ALU.mult).then_inc(self.moment.sem, 1)
        v.wait_ge(self.moment.sem, self.moment.at(g, 3))
        v.tensor_scalar(self.mean[:, :], self.mean[:, :], 0.5, None, ALU.mult).then_inc(self.moment.sem, 1)
        v.wait_ge(self.moment.sem, self.moment.at(g, 5))
        v.tensor_tensor(self.veps[:, :], self.veps[:, :], self.diff[:, :], ALU.add).then_inc(self.veps_ready.sem, 1)

    def vector_apply(self, v, g, par, src, out_free):
        out_free()
        g = g - self.behind
        v.wait_ge(self.moment.sem, self.moment.at(g, 6))
        v.wait_ge(self.rstd_ready.sem, self.rstd_ready.at(g, 1))
        for b in range(NB):
            v.tensor_scalar(self.out[:, par, b, :], src[:, b, :], self.mean[:, b:b + 1],
                                                     self.rstd[:, b:b + 1], ALU.subtract, ALU.mult)\
                                                         .then_inc(self.out_ready.sem, 1)

    def pool(self, pl, g, minus_half):
        pl.wait_ge(self.out_ready.sem, self.out_ready.at(g, 0))
        g = g - self.behind
        pl.wait_ge(self.veps_ready.sem, self.veps_ready.at(g, 1))
        pl.tensor_tensor(self.rstd[:, :], self.veps[:, :], minus_half[:, 0:NB], ALU.pow)\
            .then_inc(self.rstd_ready.sem, 1)


def pipeline(eng, first, head, body):
    head(first + 2, 0)
    with eng.Fori(first + 2, first + NSEQ, 2) as g:
        body(g, 0, True)
        body(g + 1, 1, True)
    body(first + NSEQ, 0, True)
    body(first + NSEQ + 1, 1, False)


def due(s, slots, offset, count, every=1):
    return [(d, j) for d in (-1, 0, 1) for j in range(count) if every * j + offset == s - slots * d]


def modulo_pipeline(eng, first, body):
    body(first + 1, 1, (1,))
    body(first + 2, 0, (0, 1))
    with eng.Fori(first + 3, first + NSEQ, 2) as g:
        body(g, 1, (-1, 0, 1))
        body(g + 1, 0, (-1, 0, 1))
    body(first + NSEQ + 1, 1, (-1, 0))
    body(first + NSEQ + 2, 0, (-1,))


def slot(T, g, first, b=0, n=NB):
    return T[:, bass.ds((g - (first + 2)) * NB + b, n), :]


MOE_UNITS = [(0, P), (0, TAIL)] + [(1 + p, P) for p in range(EXPERTS // 2) for _ in range(3)]
MOE_PASSES = 1 + EXPERTS // 2
MOE_PASS_UNITS = [[u for u, (q, _) in enumerate(MOE_UNITS) if q == p] for p in range(MOE_PASSES)]
MOE_UP_COLS = sum(2 * m for _, m in MOE_UNITS)


class Moe:

    def __init__(self, ctx, nc):
        sig = lambda n, per: Signal(ctx, nc, f"moe_{n}", per)
        self.norm = Norm(ctx, nc, "moe_norm")
        self.xs_ready = sig("xs_ready", 1)
        self.hT_ps = sig("hT_in_psum", 1)
        self.hT_ready = sig("hT_ready", 1)
        self.logits = sig("logits", 1)
        self.gate_step = sig("gate_step", 13)
        self.ex_ready = sig("ex_ready", 1)
        self.up = sig("up_ready", len(MOE_UNITS))
        self.silu = sig("silu_ready", len(MOE_UNITS))
        self.hid = sig("hidden_ready", len(MOE_UNITS))
        self.down = sig("down_ready", 1 + EXPERTS)
        self.accd = sig("accumulated", NB * (1 + EXPERTS))

    def emit(self, nc, run, X, W):
        n, first = self.norm, run * NSEQ
        with ExitStack() as ctx:
            pb = lambda name: ctx.enter_context(nc.psum_tensor(f"moe{run}_{name}", [P, SEQ], F32))
            sb = lambda name, s, dt=F32: ctx.enter_context(nc.sbuf_tensor(f"moe{run}_{name}", s, dt))
            n.buffers(ctx, nc, run)
            gate_bank, up_bank = [pb("g0"), pb("g1")], [pb("u0"), pb("u1")]
            down_bank = [pb("d0"), pb("d1")]
            hT_bank, lg_bank = pb("hT"), pb("lg")
            xs = sb("xs", [P, 2, NB, DIM])
            hT = sb("hTs", [P, 2, SEQ])
            self.lg = sb("lgs", [P, NB, EXPERTS])
            self.gt = sb("gt", [P, NB * EXPERTS, EXPERTS])
            self.ge = sb("ge", [P, NB * EXPERTS, EXPERTS])
            self.rank = sb("rank", [P, NB, EXPERTS])
            self.top = sb("top", [P, NB])
            self.ex = sb("ex", [P, NB, EXPERTS])
            self.den = sb("den", [P, NB])
            self.comb = sb("comb", [P, 2, NB, EXPERTS])
            sg = sb("sg", [P, 2, SEQ])
            h = sb("h", [P, 2, 3, SEQ])
            acc = sb("acc", [P, NB, DIM])
            block = ctx.enter_context(nc.Block())

            @block.gpsimd
            def _(pl):
                if run == 0:
                    pl.sem_inc(n.rstd_ready.sem, n.rstd_ready.credit())

                def head(g, par):
                    n.pool(pl, g, W["minus_half"])

                def body(g, par, more):
                    if more:
                        head(g + 1, 1 - par)

                pipeline(pl, first, head, body)

            @block.vector
            def _(v):
                if run == 0:
                    for s in (*n.of_vector, self.xs_ready, self.gate_step, self.hid, self.accd):
                        v.sem_inc(s.sem, s.credit())

                def stats(g, par):
                    v.wait_ge(self.accd.sem, self.accd.at(g, -self.accd.per))
                    v.tensor_scalar(xs[:, par, :, :], slot(X, g, first), 1.0, None, ALU.mult)\
                        .then_inc(self.xs_ready.sem, 1)
                    v.wait_ge(self.xs_ready.sem, self.xs_ready.at(g, 1))
                    n.vector_stats(v, g, xs[:, par, :, :])

                def apply(g, par):
                    n.vector_apply(v, g, par, xs[:, par, :, :],
                                   lambda: v.wait_ge(self.hT_ps.sem, self.hT_ps.at(g, -1)))

                def head(g, par):
                    stats(g, par)
                    apply(g, par)
                    self.gate(v, g, par, lg_bank, W)

                def body(g, par, more):
                    def hidden(q):
                        v.wait_ge(self.down.sem, self.down.at(g, 1 + 2 * (q - 2) if q >= 2 else (0, -2)[q]))
                        for u in MOE_PASS_UNITS[q]:
                            m, part = MOE_UNITS[u][1], u - MOE_PASS_UNITS[q][0]
                            v.wait_ge(self.silu.sem, self.silu.at(g, u + 1))
                            v.tensor_tensor(h[0:m, q % 2, part, :], sg[0:m, u % 2, :],
                                            up_bank[u % 2][0:m, :], ALU.mult).then_inc(self.hid.sem, 1)

                    def add(e):
                        v.wait_ge(self.down.sem, self.down.at(g, e + 1))
                        for b in range(NB):
                            v.wait_ge(self.accd.sem, self.accd.at(g, NB * (e - 1) + b + 1 if e else 0))
                            scalar = self.comb[:, par, b, e - 1:e] if e else 0.5
                            other = acc[:, b, :] if e else xs[:, par, b, :]
                            o = acc[:, b, :] if e < EXPERTS else slot(X, g, first, b, 1)
                            v.scalar_tensor_tensor(
                                out=o, in0=down_bank[e % 2][:, b * DIM:(b + 1) * DIM], scalar=scalar, in1=other,
                                op0=ALU.mult, op1=ALU.add).then_inc(self.accd.sem, 1)

                    hidden(0)
                    hidden(1)
                    if more:
                        stats(g + 1, 1 - par)
                    add(0)
                    hidden(2)
                    add(1)
                    add(2)
                    if more:
                        apply(g + 1, 1 - par)
                    hidden(3)
                    add(3)
                    add(4)
                    hidden(4)
                    add(5)
                    add(6)
                    if more:
                        self.gate(v, g + 1, 1 - par, lg_bank, W)
                    add(7)
                    add(8)

                pipeline(v, first, head, body)

            @block.scalar
            def _(act):
                if run == 0:
                    for s in (self.hT_ready, self.ex_ready, self.silu):
                        act.sem_inc(s.sem, s.credit())

                def move_hT(g, par):
                    act.wait_ge(self.hT_ps.sem, self.hT_ps.at(g, 1))
                    act.wait_ge(self.up.sem, self.up.at(g, -self.up.per))
                    act.activation(hT[:, par, :], hT_bank[:, :], ACT.Copy).then_inc(self.hT_ready.sem, 1)

                def exp_logits(g):
                    act.wait_ge(self.gate_step.sem, self.gate_step.at(g, 8))
                    act.activation(self.ex[:, :, :], self.ex[:, :, :], ACT.Exp).then_inc(self.ex_ready.sem, 1)

                def silus(g, units):
                    for u in units:
                        m = MOE_UNITS[u][1]
                        act.wait_ge(self.up.sem, self.up.at(g, u + 1))
                        act.wait_ge(self.hid.sem, self.hid.at(g, u - 1))
                        act.activation(sg[0:m, u % 2, :], gate_bank[u % 2][0:m, :], ACT.Silu)\
                            .then_inc(self.silu.sem, 1)

                def head(g, par):
                    move_hT(g, par)
                    exp_logits(g)

                def body(g, par, more):
                    last = MOE_PASS_UNITS[MOE_PASSES - 1]
                    silus(g, range(0, MOE_PASS_UNITS[4][0]))
                    if more:
                        move_hT(g + 1, 1 - par)
                    silus(g, range(MOE_PASS_UNITS[4][0], MOE_PASS_UNITS[4][-1] + 1))
                    if more:
                        exp_logits(g + 1)

                pipeline(act, first, head, body)

            @block.tensor
            def _(pe):
                if run == 0:
                    for s in (self.hT_ps, self.logits, self.up, self.down):
                        pe.sem_inc(s.sem, s.credit())

                def head(g, par):
                    pe.wait_ge(self.hT_ready.sem, self.hT_ready.at(g, 0))
                    for b in range(NB):
                        pe.wait_ge(n.out_ready.sem, n.out_ready.at(g, b + 1))
                        ins = pe.transpose(hT_bank[:, b * P:(b + 1) * P], n.out[:, par, b, :], W["ident"])
                    ins.then_inc(self.hT_ps.sem, 1)
                    pe.wait_ge(self.hT_ready.sem, self.hT_ready.at(g, 1))
                    pe.wait_ge(self.gate_step.sem, self.gate_step.at(g, 1 - self.gate_step.per))
                    for b in range(NB):
                        ins = pe.matmul(lg_bank[:, b * EXPERTS:(b + 1) * EXPERTS], hT[:, par, b * P:(b + 1) * P],
                                        W["wg"], start=True, stop=True)
                    ins.then_inc(self.logits.sem, 1)

                def body(g, par, more):
                    def up(q):
                        for u in MOE_PASS_UNITS[q]:
                            m, col = MOE_UNITS[u][1], 2 * sum(m for _, m in MOE_UNITS[:u])
                            pe.wait_ge(self.hid.sem, self.hid.at(g, u - 1))
                            pe.matmul(gate_bank[u % 2][0:m, :], W["wup"][:, col:col + m], hT[:, par, :],
                                      start=True, stop=True)
                            pe.matmul(up_bank[u % 2][0:m, :], W["wup"][:, col + m:col + 2 * m],
                                      hT[:, par, :], start=True, stop=True).then_inc(self.up.sem, 1)

                    def down(q):
                        pe.wait_ge(self.hid.sem, self.hid.at(g, MOE_PASS_UNITS[q][-1] + 1))
                        tail = len(MOE_PASS_UNITS[q]) - 1
                        for j in range(tail):
                            e = 2 * q - 1 + j if q else 0
                            pe.wait_ge(self.accd.sem, self.accd.at(g, NB * (e - 1) if e >= 2 else (0, -NB)[e]))
                            r = TAIL * j
                            for b in range(NB):
                                o = down_bank[e % 2][:, b * DIM:(b + 1) * DIM]
                                pe.matmul(o, h[:, q % 2, j, b * P:(b + 1) * P], W["wdm"][:, e, :],
                                          start=True, stop=False)
                                ins = pe.matmul(o, h[r:r + TAIL, q % 2, tail, b * P:(b + 1) * P],
                                                W["wdt"][r:r + TAIL, q, :], start=False, stop=True)
                            ins.then_inc(self.down.sem, 1)

                    up(0)
                    for q in range(MOE_PASSES):
                        if q == 3 and more:
                            head(g + 1, 1 - par)
                        if q + 1 < MOE_PASSES:
                            up(q + 1)
                        down(q)

                pipeline(pe, first, head, body)

    def gate(self, v, g, par, lg_bank, W):
        v.wait_ge(self.accd.sem, self.accd.at(g, -self.accd.per))
        v.wait_ge(self.logits.sem, self.logits.at(g, 1))
        lg, gt, ge, ex = self.lg, self.gt, self.ge, self.ex
        v.tensor_scalar(lg[:, :, :], lg_bank[:, 0:NB * EXPERTS].rearrange("p (b e) -> p b e", b=NB), 1.0,
                             None, ALU.mult).then_inc(self.gate_step.sem, 1)
        v.wait_ge(self.gate_step.sem, self.gate_step.at(g, 1))
        shape = [P, NB, EXPERTS, EXPERTS]
        other = lg[:, :, :].unsqueeze(2).broadcast_to(shape)
        own = lg[:, :, :].unsqueeze(3).broadcast_to(shape)
        v4 = lambda t: t[:, :, :].rearrange("p (b e) j -> p b e j", b=NB)
        v.tensor_tensor(v4(gt), other, own, ALU.is_gt).then_inc(self.gate_step.sem, 1)
        v.wait_ge(self.gate_step.sem, self.gate_step.at(g, 2))
        v.tensor_tensor(v4(ge), other, own, ALU.is_ge).then_inc(self.gate_step.sem, 1)
        v.wait_ge(self.gate_step.sem, self.gate_step.at(g, 3))
        v.tensor_tensor(ge[:, :, :], ge[:, :, :], W["lower"], ALU.mult).then_inc(self.gate_step.sem, 1)
        v.wait_ge(self.gate_step.sem, self.gate_step.at(g, 4))
        v.tensor_tensor(gt[:, :, :], gt[:, :, :], ge[:, :, :], ALU.max).then_inc(self.gate_step.sem, 1)
        v.wait_ge(self.gate_step.sem, self.gate_step.at(g, 5))
        v.tensor_reduce(self.rank[:, :, :].rearrange("p b e -> p (b e)"), gt[:, :, :], AX.X, ALU.add)\
            .then_inc(self.gate_step.sem, 1)
        v.wait_ge(self.gate_step.sem, self.gate_step.at(g, 6))
        v.tensor_reduce(self.top[:, :], lg[:, :, :], AX.X, ALU.max).then_inc(self.gate_step.sem, 1)
        v.wait_ge(self.gate_step.sem, self.gate_step.at(g, 7))
        bc = lambda t: t[:, :].unsqueeze(2).broadcast_to([P, NB, EXPERTS])
        v.tensor_tensor(ex[:, :, :], lg[:, :, :], bc(self.top), ALU.subtract).then_inc(self.gate_step.sem, 1)
        v.wait_ge(self.gate_step.sem, self.gate_step.at(g, 8))
        v.wait_ge(self.ex_ready.sem, self.ex_ready.at(g, 1))
        v.scalar_tensor_tensor(out=ex[:, :, :], in0=self.rank[:, :, :], scalar=1.5, in1=ex[:, :, :],
                                    op0=ALU.is_lt, op1=ALU.mult).then_inc(self.gate_step.sem, 1)
        v.wait_ge(self.gate_step.sem, self.gate_step.at(g, 9))
        v.tensor_reduce(self.den[:, :], ex[:, :, :], AX.X, ALU.add).then_inc(self.gate_step.sem, 1)
        v.wait_ge(self.gate_step.sem, self.gate_step.at(g, 10))
        v.reciprocal(self.den[:, :], self.den[:, :]).then_inc(self.gate_step.sem, 1)
        v.wait_ge(self.gate_step.sem, self.gate_step.at(g, 11))
        v.tensor_scalar(self.den[:, :], self.den[:, :], 0.5, None, ALU.mult).then_inc(self.gate_step.sem, 1)
        v.wait_ge(self.gate_step.sem, self.gate_step.at(g, 12))
        v.tensor_tensor(self.comb[:, par, :, :], ex[:, :, :], bc(self.den), ALU.mult).then_inc(self.gate_step.sem, 1)
        v.wait_ge(self.gate_step.sem, self.gate_step.at(g, 13))


HID_BLOCKS = [(0, P), (P, P), (2 * P, HID - 2 * P)]


class Geglu:

    def __init__(self, ctx, nc):
        sig = lambda n, per, unit=1: Signal(ctx, nc, f"ffn_{n}", per, unit)
        self.norm = Norm(ctx, nc, "ffn_norm")
        self.shifted = sig("shifted", 3, 16)
        self.hT_ps = sig("hT_in_psum", 1)
        self.hT_ready = sig("hT_ready", 1)
        self.up = sig("up_ready", 3)
        self.gelu = sig("gelu_ready", 3)
        self.hid = sig("hidden_ready", 3)
        self.down = sig("down_ready", 1)
        self.sum = sig("sum_ready", 1)
        self.summed = sig("summed", 1)
        self.moved = sig("result_stored", 1)
        self.first_token = ctx.enter_context(nc.semaphore("ffn_first_token"))

    def emit(self, nc, run, X, Y, W, layer, last):
        n, first = self.norm, run * NSEQ
        others = (run - run // DEPTH) * NSEQ
        w1, w2 = W["w1"][:, layer, :], W["w2"][:, layer, :, :]
        b1, b2, lg, lb = W["b1"][:, layer, :], W["b2"][:, layer, :], W["ln_g"], W["ln_b"]
        with ExitStack() as ctx:
            pb = lambda name: ctx.enter_context(nc.psum_tensor(f"ffn{run}_{name}", [P, SEQ], F32))
            sb = lambda name, s, dt=F32: ctx.enter_context(nc.sbuf_tensor(f"ffn{run}_{name}", s, dt))
            n.buffers(ctx, nc, run)
            a_bank, g_bank = [pb(f"a{j}") for j in range(3)], [pb(f"g{j}") for j in range(3)]
            hT_bank, out_bank = pb("hT"), pb("out")
            hs = sb("shifted", [P, 2, NB, DIM])
            hT = sb("hTs", [P, 2, SEQ])
            gl = sb("gelu", [P, 3, SEQ])
            hid = sb("hidden", [P, 2, 3, SEQ])
            total = sb("total", [P, NB, DIM])
            H = DIM // 2
            block = ctx.enter_context(nc.Block())

            STATS, APPLY, H_T, DOWN, SUM = -3, -2, -2, 3, 4
            in_slot = lambda s, offset: due(s, 3, offset, 1)
            later = lambda d, par: par if d == 0 else 1 - par

            @block.sync
            def _(sp):
                if run == 0:
                    sp.sem_inc(self.shifted.sem, self.shifted.credit())
                sp.wait_ge(self.first_token, run + 1)

                def load(g, par):
                    sp.wait_ge(self.shifted.sem, self.shifted.at(g, 0))
                    sp.wait_ge(n.out_ready.sem, n.out_ready.at(g, -NB))
                    y = lambda b, c: slot(Y, g, first, b, c)
                    sp.dma_start(hs[:, par, :, 0:H], y(0, NB)[:, :, 0:H]).then_inc(self.shifted.sem, 16)
                    sp.dma_start(hs[1:P, par, :, H:DIM], y(0, NB)[0:P - 1, :, H:DIM]).then_inc(self.shifted.sem, 16)
                    sp.dma_start(hs[0:1, par, 1:NB, H:DIM], y(0, NB - 1)[P - 1:P, :, H:DIM])\
                        .then_inc(self.shifted.sem, 16)

                def body(g, par, there):
                    if 1 in there:
                        load(g + 1, 1 - par)

                modulo_pipeline(sp, first, body)

            @block.gpsimd
            def _(pl):
                if run == 0:
                    pl.sem_inc(n.rstd_ready.sem, n.rstd_ready.credit())

                def body(g, par, there):
                    for s in range(3):
                        for d, _ in in_slot(s, STATS):
                            if d in there:
                                n.pool(pl, g + d, W["minus_half"])

                modulo_pipeline(pl, first, body)

            @block.vector
            def _(v):
                if run == 0:
                    for s in (*n.of_vector, self.hid, self.sum, self.summed, self.moved):
                        v.sem_inc(s.sem, s.credit())
                v.memset(hs[0:1, :, 0:1, H:DIM], 0.0).then_inc(self.first_token, 1)

                def stats(g, par):
                    v.wait_ge(self.shifted.sem, self.shifted.at(g, 3))
                    n.vector_stats(v, g, hs[:, par, :, :])

                def apply(g, par):
                    n.vector_apply(v, g, par, hs[:, par, :, :],
                                   lambda: v.wait_ge(self.hT_ps.sem, self.hT_ps.at(g, -1)))

                def hidden(g, par, j):
                    m = HID_BLOCKS[j][1]
                    v.wait_ge(self.gelu.sem, self.gelu.at(g, j + 1))
                    v.wait_ge(self.down.sem, self.down.at(g, -1))
                    v.scalar_tensor_tensor(
                        out=hid[0:m, par, j, :], in0=a_bank[j][0:m, :], scalar=b1[0:m, j:j + 1],
                        in1=gl[0:m, j, :], op0=ALU.add, op1=ALU.mult).then_inc(self.hid.sem, 1)

                def add_bias(g):
                    v.wait_ge(self.down.sem, self.down.at(g, 1))
                    v.wait_ge(self.moved.sem, self.moved.at(g, 0))
                    out3 = out_bank[:, :].rearrange("p (b d) -> p b d", b=NB)
                    v.tensor_tensor(total[:, :, :], out3, b2.unsqueeze(1).broadcast_to([P, NB, DIM]), ALU.add)\
                        .then_inc(self.sum.sem, 1)

                def add(g):
                    v.wait_ge(self.sum.sem, self.sum.at(g, 1))
                    y = slot(Y, g, first)
                    if last:
                        v.tensor_tensor(total[:, :, :], total[:, :, :], y, ALU.add).then_inc(self.summed.sem, 1)
                        v.wait_ge(self.summed.sem, self.summed.at(g - others, 1))
                        x = slot(X, g, first)
                        v.scalar_tensor_tensor(out=x, in0=total[:, :, :], scalar=0.5, in1=x, op0=ALU.mult,
                                               op1=ALU.add).then_inc(self.moved.sem, 1)
                    else:
                        v.tensor_tensor(y, total[:, :, :], y, ALU.add).then_inc(self.moved.sem, 1)

                def body(g, par, there):
                    for s in range(3):
                        for d, _ in in_slot(s, SUM):
                            if d in there:
                                add_bias(g + d)
                        for d, _ in in_slot(s, APPLY):
                            if d in there:
                                apply(g + d, later(d, par))
                        for d, _ in in_slot(s, STATS):
                            if d in there:
                                stats(g + d, later(d, par))
                        if 0 in there:
                            hidden(g, par, s)
                        for d, _ in in_slot(s, SUM):
                            if d in there:
                                add(g + d)

                modulo_pipeline(v, first, body)

            @block.scalar
            def _(act):
                if run == 0:
                    for s in (self.hT_ready, self.gelu):
                        act.sem_inc(s.sem, s.credit())

                def move_hT(g, par):
                    act.wait_ge(self.hT_ps.sem, self.hT_ps.at(g, 1))
                    act.wait_ge(self.up.sem, self.up.at(g, -3))
                    act.activation(hT[:, par, :], hT_bank[:, :], ACT.Identity, bias=lb[:, layer:layer + 1],
                                   scale=lg[:, layer:layer + 1]).then_inc(self.hT_ready.sem, 1)

                def gelu(g, j):
                    m = HID_BLOCKS[j][1]
                    act.wait_ge(self.up.sem, self.up.at(g, j + 1))
                    act.wait_ge(self.hid.sem, self.hid.at(g, j - 2))
                    act.activation(gl[0:m, j, :], g_bank[j][0:m, :], ACT.Gelu, bias=b1[0:m, 3 + j:4 + j])\
                        .then_inc(self.gelu.sem, 1)

                def body(g, par, there):
                    for s in range(3):
                        if 0 in there:
                            gelu(g, s)
                        for d, _ in in_slot(s, H_T):
                            if d in there:
                                move_hT(g + d, later(d, par))

                modulo_pipeline(act, first, body)

            @block.tensor
            def _(pe):
                if run == 0:
                    for s in (self.hT_ps, self.up, self.down):
                        pe.sem_inc(s.sem, s.credit())

                def transpose_h(g, par):
                    pe.wait_ge(self.hT_ready.sem, self.hT_ready.at(g, 0))
                    for b in range(NB):
                        pe.wait_ge(n.out_ready.sem, n.out_ready.at(g, b + 1))
                        ins = pe.transpose(hT_bank[:, b * P:(b + 1) * P], n.out[:, par, b, :], W["ident"])
                    ins.then_inc(self.hT_ps.sem, 1)

                def up(g, par, j):
                    r, m = HID_BLOCKS[j]
                    pe.wait_ge(self.hT_ready.sem, self.hT_ready.at(g, 1))
                    pe.wait_ge(self.hid.sem, self.hid.at(g, j - 2))
                    pe.matmul(g_bank[j][0:m, :], w1[:, HID + r:HID + r + m], hT[:, par, :], start=True, stop=True)
                    pe.matmul(a_bank[j][0:m, :], w1[:, r:r + m], hT[:, par, :], start=True, stop=True)\
                        .then_inc(self.up.sem, 1)

                def down(g, par):
                    pe.wait_ge(self.hid.sem, self.hid.at(g, 3))
                    pe.wait_ge(self.sum.sem, self.sum.at(g, 0))
                    for b in range(NB):
                        for j, (_, m) in enumerate(HID_BLOCKS):
                            ins = pe.matmul(out_bank[:, b * DIM:(b + 1) * DIM], hid[0:m, par, j, b * P:(b + 1) * P],
                                            w2[0:m, j, :], start=(j == 0), stop=(j == 2))
                    ins.then_inc(self.down.sem, 1)

                def body(g, par, there):
                    for s in range(3):
                        if 0 in there:
                            up(g, par, s)
                        for d, _ in in_slot(s, H_T):
                            if d in there:
                                transpose_h(g + d, later(d, par))
                        for d, _ in in_slot(s, DOWN):
                            if d in there:
                                down(g + d, later(d, par))

                modulo_pipeline(pe, first, body)


PAIRS = LH // 2
UNITS = NB * PAIRS
BAND = P + WINDOW


def unit_heads(k):
    a = k % PAIRS
    return [4 * (a // 2) + a % 2 + 2 * j for j in range(2)]


class LocalAttention:

    def __init__(self, ctx, nc):
        sig = lambda n, per, unit=1: Signal(ctx, nc, f"loc_{n}", per, unit)
        self.norm = Norm(ctx, nc, "loc_norm")
        self.xs_ready = sig("xs_ready", 1)
        self.y_made = sig("y_made", 1)
        self.q_turned = sig("q_turned", NB)
        self.k_turned = sig("k_turned", NB)
        self.v_ps = sig("v_in_psum", NB)
        self.yT_ps = sig("yT_in_psum", 1)
        self.hT_ready = sig("hT_ready", 2)
        self.qkv = sig("qkv_ready", NB)
        self.squares = sig("squares", NB)
        self.v_ready = sig("v_ready", NB)
        self.ss_ready = sig("ss_ready", 2 * NB)
        self.terms = sig("turn_terms", 3 * NB)
        self.rn_ready = sig("rn_ready", NB)
        self.k_normed = sig("k_normed", NB)
        self.qT_ps = sig("qT_in_psum", NB)
        self.kT_ps = sig("kT_in_psum", NB)
        self.qT_ready = sig("qT_ready", NB)
        self.kT_ready = sig("kT_ready", NB)
        self.scores = sig("scores", UNITS)
        self.top = sig("top", UNITS)
        self.bias = sig("bias", UNITS)
        self.probs = sig("probs", 2 * UNITS)
        self.rsum = sig("rsum", UNITS)
        self.divided = sig("divided", UNITS)
        self.pT_ps = sig("pT_in_psum", UNITS)
        self.pT_ready = [sig(f"pT_ready{j}", UNITS // 2) for j in range(2)]
        self.pv = sig("pv", UNITS // 2)
        self.oT_ready = sig("oT_ready", NB)
        self.wo = sig("wo_ready", NB)
        self.moved = sig("result_stored", NB)
        self.cleared = ctx.enter_context(nc.semaphore("loc_cleared"))

    def emit(self, nc, run, X, Y, W, layer):
        n, first = self.norm, run * NSEQ
        n.behind = (run - run // DEPTH) * NSEQ
        wqkv, wo = W["wqkv"][:, layer, :], W["wo"][:, layer, :, :]
        turn_cos, turn_sin = W["turn_cos"][:, layer, :, :, :], W["turn_sin"][:, layer, :, :, :]
        H = DIM // 2
        with ExitStack() as ctx:
            pb = lambda name, banks=1: ctx.enter_context(nc.psum_tensor(f"loc{run}_{name}", [P, banks * SEQ], F32))
            sb = lambda name, s, dt=F32: ctx.enter_context(nc.sbuf_tensor(f"loc{run}_{name}", s, dt))
            n.buffers(ctx, nc, run)
            qk_bank = pb("qk", 2)
            v_bank = pb("v")
            t_bank = pb("t")
            s_bank = [pb("s0"), pb("s1")]
            p_bank = pb("p")
            o_bank = pb("o")
            xs = sb("xs", [P, NB, DIM])
            hT = sb("hTs", [P, 2, SEQ])
            sq = sb("sq", [P, 2 * INNER])
            ss = sb("ss", [P, 2 * LH])
            rn = sb("rn", [P, NB, 2 * LH])
            t1 = sb("t1", [P, 2 * INNER])
            t2 = sb("t2", [P, 2 * INNER])
            qk = sb("qk_turned", [P, 2 * INNER])
            vs = sb("vs", [P, 2, NB, INNER])
            qT = sb("qT", [P, 2, PAIRS, P])
            kT = sb("kT", [P, PAIRS, SEQ])
            top = sb("tops", [P, UNITS, 2])
            bias = sb("biases", [P, UNITS, 2])
            sums = sb("sums", [P, UNITS, 2])
            rs = sb("rs", [P, UNITS, 2])
            probs = sb("probs_s", [P, 8, 2, 2 * P])
            pT = sb("pT", [P, 4, 2, BAND])
            oT = sb("oT", [P, PAIRS, P])
            block = ctx.enter_context(nc.Block())
            by_head = lambda t: t.rearrange("p (h d) -> p h d", d=LD)

            STATS, APPLY, Y_T = -15, -14, -13
            QK, V, SQUARE, MOVE_V, COS, SIN, SQUARES, RN = -10, -9, -10, -8, -8, -7, -6, -5
            TURN_Q, TURN_K, NORM_K, Q_T, K_T = -6, -5, -4, -4, -3
            O_T, PROJECT, ADD = 9, 10, 11
            SCORE, INVERSE, P_T, TIMES_V = -1, 1, 4, 6
            in_slot = lambda s, offset, count=1, every=PAIRS: due(s, UNITS, offset, count, every)

            @block.gpsimd
            def _(pl):
                if run == 0:
                    for s in (n.rstd_ready, self.rn_ready, self.q_turned, self.k_normed, self.divided):
                        pl.sem_inc(s.sem, s.credit())

                def norms(g, t):
                    pl.wait_ge(self.ss_ready.sem, self.ss_ready.at(g, 2 * t + 2))
                    pl.wait_ge(self.probs.sem, self.probs.at(g, 2 * PAIRS * (t + 1) - 2 * UNITS))
                    pl.wait_ge(self.k_normed.sem, self.k_normed.at(g, t + 1 - NB))
                    pl.tensor_tensor(rn[:, t, :], ss[:, :], W["minus_half"][:, 0:2 * LH], ALU.pow)\
                        .then_inc(self.rn_ready.sem, 1)

                def turn_q(g, t):
                    pl.wait_ge(self.terms.sem, self.terms.at(g, 3 * t + 3))
                    pl.wait_ge(self.qT_ps.sem, self.qT_ps.at(g, t))
                    q = slice(0, INNER)
                    pl.tensor_tensor(qk[:, q], t1[:, q], t2[:, q], ALU.add).then_inc(self.q_turned.sem, 1)

                def norm_k(g, t):
                    pl.wait_ge(self.rn_ready.sem, self.rn_ready.at(g, t + 1))
                    pl.wait_ge(self.k_turned.sem, self.k_turned.at(g, t + 1))
                    k3 = by_head(qk[:, INNER:2 * INNER])
                    pl.tensor_tensor(k3, k3, rn[:, t, LH:2 * LH].unsqueeze(2).broadcast_to([P, LH, LD]), ALU.mult)\
                        .then_inc(self.k_normed.sem, 1)

                def divide(g, k):
                    pl.wait_ge(self.rsum.sem, self.rsum.at(g, k + 1))
                    p_ = probs[:, k % 8, :, H:2 * P]
                    pl.tensor_tensor(p_, p_, rs[:, k, :].unsqueeze(2).broadcast_to([P, 2, BAND]), ALU.mult)\
                        .then_inc(self.divided.sem, 1)

                def body(g, par, there):
                    for s in range(UNITS):
                        for d, _ in in_slot(s, STATS):
                            if d in there and layer == 0:
                                n.pool(pl, g + d, W["minus_half"])
                        for d, t in in_slot(s, NORM_K, NB):
                            if d in there:
                                norm_k(g + d, t)
                        for d, t in in_slot(s, TURN_Q, NB):
                            if d in there:
                                turn_q(g + d, t)
                        for d, t in in_slot(s, RN, NB):
                            if d in there:
                                norms(g + d, t)
                        for d, k in in_slot(s, INVERSE, UNITS, 1):
                            if d in there:
                                divide(g + d, k)

                modulo_pipeline(pl, first, body)

            @block.vector
            def _(v):
                if run == 0:
                    for s in (*n.of_vector, self.xs_ready, self.y_made, self.ss_ready, self.terms, self.k_turned,
                              self.top,
                              self.bias,
                              self.rsum, self.pT_ready[0], self.moved):
                        v.sem_inc(s.sem, s.credit())
                v.memset(hT[H:P, :, 0:1], 0.0).then_inc(self.cleared, 1)
                v.memset(probs[:, :, :, 0:H], 0.0).then_inc(self.cleared, 1)

                def stats(g):
                    v.wait_ge(n.out_ready.sem, n.out_ready.at(g, 0))
                    v.tensor_scalar(xs[:, :, :], slot(X, g, first), 1.0, None, ALU.mult)\
                        .then_inc(self.xs_ready.sem, 1)
                    v.wait_ge(self.xs_ready.sem, self.xs_ready.at(g - n.behind, 1))
                    n.vector_stats(v, g, xs)

                def tokens(g, par):
                    if layer == 0:
                        n.vector_apply(v, g, par, xs, lambda: v.wait_ge(self.yT_ps.sem, self.yT_ps.at(g, -1)))
                        v.wait_ge(n.out_ready.sem, n.out_ready.at(g, NB))
                        v.tensor_scalar(slot(Y, g, first), n.out[:, par, :, :], 1.0, None, ALU.mult)\
                            .then_inc(self.y_made.sem, 1)
                    else:
                        v.wait_ge(self.yT_ps.sem, self.yT_ps.at(g, -1))
                        for b in range(NB):
                            v.tensor_scalar(n.out[:, par, b:b + 1, :], slot(Y, g, first, b, 1), 1.0, None, ALU.mult)\
                                .then_inc(n.out_ready.sem, 1)

                def squares(g, t):
                    v.wait_ge(self.squares.sem, self.squares.at(g, t + 1))
                    v.wait_ge(self.rn_ready.sem, self.rn_ready.at(g, t))
                    v.tensor_reduce(ss[:, :], by_head(sq[:, :]), AX.X, ALU.add).then_inc(self.ss_ready.sem, 1)
                    v.wait_ge(self.ss_ready.sem, self.ss_ready.at(g, 2 * t + 1))
                    v.tensor_scalar(ss[:, :], ss[:, :], 1e-24, None, ALU.max).then_inc(self.ss_ready.sem, 1)

                q4 = qk_bank[:, :].rearrange("p (j h d) -> p j h d", j=2, d=LD)

                def cos_terms(g, t):
                    v.wait_ge(self.squares.sem, self.squares.at(g, t + 1))
                    v.wait_ge(self.q_turned.sem, self.q_turned.at(g, t))
                    v.wait_ge(self.k_turned.sem, self.k_turned.at(g, t))
                    cos = turn_cos[:, t, :, :].unsqueeze(2).broadcast_to([P, 2, LH, LD])
                    v.tensor_tensor(t1[:, :].rearrange("p (j h d) -> p j h d", j=2, d=LD), q4, cos, ALU.mult)\
                        .then_inc(self.terms.sem, 1)

                def sin_terms(g, t):
                    for j in range(2):
                        halves = lambda ap: ap.rearrange("p h (s d) -> p h s d", s=2)
                        sin = turn_sin[:, t, j, :].unsqueeze(1).broadcast_to([P, LH, LD])
                        v.tensor_tensor(halves(by_head(t2[:, j * INNER:(j + 1) * INNER])),
                                        halves(q4[:, j, :, :])[:, :, ::-1, :], halves(sin), ALU.mult)\
                            .then_inc(self.terms.sem, 1)

                def turn_k(g, t):
                    v.wait_ge(self.terms.sem, self.terms.at(g, 3 * t + 3))
                    v.wait_ge(self.kT_ps.sem, self.kT_ps.at(g, t))
                    k_ = slice(INNER, 2 * INNER)
                    v.tensor_tensor(qk[:, k_], t1[:, k_], t2[:, k_], ALU.add).then_inc(self.k_turned.sem, 1)

                def top_of(g, k):
                    v.wait_ge(self.scores.sem, self.scores.at(g, k + 1))
                    s3 = s_bank[k % 2][:, 0:2 * BAND].rearrange("p (j c) -> p j c", j=2)
                    v.tensor_reduce(top[:, k, :], s3, AX.X, ALU.max, negate=True).then_inc(self.top.sem, 1)

                def bias_of(g, k):
                    v.wait_ge(self.top.sem, self.top.at(g, k + 1))
                    v.wait_ge(self.rn_ready.sem, self.rn_ready.at(g, k // PAIRS + 1))
                    h = unit_heads(k)
                    v.tensor_tensor(bias[:, k, :], top[:, k, :], rn[:, k // PAIRS, h[0]:h[1] + 1:2], ALU.mult)\
                        .then_inc(self.bias.sem, 1)

                def inverse(g, k):
                    v.wait_ge(self.probs.sem, self.probs.at(g, 2 * k + 2))
                    v.reciprocal(rs[:, k, :], sums[:, k, :]).then_inc(self.rsum.sem, 1)

                def move_pT(g, k):
                    v.wait_ge(self.pT_ps.sem, self.pT_ps.at(g, k + 1))
                    v.wait_ge(self.pv.sem, self.pv.at(g, k // 2 - 1))
                    c = BAND if k >= PAIRS else P
                    src = p_bank[:, 0:2 * BAND].rearrange("p (j c) -> p j c", j=2)[:, :, 0:c]
                    v.tensor_copy(pT[:, k % 4, :, 0:c], src).then_inc(self.pT_ready[0].sem, 1)

                def add(g, t):
                    v.wait_ge(self.wo.sem, self.wo.at(g, t + 1))
                    if layer == 0:
                        v.wait_ge(self.y_made.sem, self.y_made.at(g - n.behind, 1))
                    y = slot(Y, g, first, t, 1)
                    v.tensor_tensor(y, t_bank[:, 0:DIM].unsqueeze(1), y, ALU.add).then_inc(self.moved.sem, 1)

                def body(g, par, there):
                    for s in range(UNITS):
                        if 0 in there:
                            top_of(g, s)
                        for d, k in in_slot(s, INVERSE, UNITS, 1):
                            if d in there:
                                inverse(g + d, k)
                        if 0 in there:
                            bias_of(g, s)
                        for d, t in in_slot(s, ADD, NB):
                            if d in there:
                                add(g + d, t)
                        for d, t in in_slot(s, SQUARES, NB):
                            if d in there:
                                squares(g + d, t)
                        for d, t in in_slot(s, COS, NB):
                            if d in there:
                                cos_terms(g + d, t)
                        for d, t in in_slot(s, SIN, NB):
                            if d in there:
                                sin_terms(g + d, t)
                        for d, t in in_slot(s, TURN_K, NB):
                            if d in there:
                                turn_k(g + d, t)
                        for d, _ in in_slot(s, STATS):
                            if d in there and layer == 0:
                                stats(g + d)
                        for d, _ in in_slot(s, APPLY):
                            if d in there:
                                tokens(g + d, par if d == 0 else 1 - par)
                        for d, k in in_slot(s, P_T, UNITS, 1):
                            if d in there and k % 2 == 0:
                                move_pT(g + d, k)

                modulo_pipeline(v, first, body)

            @block.scalar
            def _(act):
                if run == 0:
                    for s in (self.hT_ready, self.squares, self.v_ready, self.qT_ready, self.kT_ready, self.probs,
                              self.pT_ready[1], self.oT_ready):
                        act.sem_inc(s.sem, s.credit())
                act.wait_ge(self.cleared, 2 * run + 2)
                copy = lambda o, i: act.activation(o, i, ACT.Copy)

                def move_hT(g, par):
                    act.wait_ge(self.yT_ps.sem, self.yT_ps.at(g, 1))
                    act.wait_ge(self.v_ps.sem, self.v_ps.at(g, -NB))
                    copy(hT[0:H, par, :], t_bank[0:H, :]).then_inc(self.hT_ready.sem, 1)
                    copy(hT[H:P, par, 1:SEQ], t_bank[H:P, 0:SEQ - 1]).then_inc(self.hT_ready.sem, 1)

                def square_qk(g, t):
                    act.wait_ge(self.qkv.sem, self.qkv.at(g, t + 1))
                    act.wait_ge(self.ss_ready.sem, self.ss_ready.at(g, 2 * t))
                    act.activation(sq[:, :], qk_bank[:, :], ACT.Square).then_inc(self.squares.sem, 1)

                def take_v(g, par, t):
                    act.wait_ge(self.v_ps.sem, self.v_ps.at(g, t + 1))
                    act.wait_ge(self.pv.sem, self.pv.at(g, PAIRS * min(t + 2, NB) // 2 - UNITS))
                    copy(vs[:, par, t, :], v_bank[:, :]).then_inc(self.v_ready.sem, 1)

                def take_qT(g, t):
                    act.wait_ge(self.qT_ps.sem, self.qT_ps.at(g, t + 1))
                    act.wait_ge(self.scores.sem, self.scores.at(g, PAIRS * (t - 1)))
                    copy(qT[:, t % 2, :, :], t_bank[:, :].rearrange("p (a c) -> p a c", c=P))\
                        .then_inc(self.qT_ready.sem, 1)

                def take_kT(g, t):
                    act.wait_ge(self.kT_ps.sem, self.kT_ps.at(g, t + 1))
                    act.wait_ge(self.scores.sem, self.scores.at(g, PAIRS * min(t + 2, NB) - UNITS))
                    copy(kT[:, :, t * P:(t + 1) * P], t_bank[:, :].rearrange("p (a c) -> p a c", c=P))\
                        .then_inc(self.kT_ready.sem, 1)

                def exp(g, k):
                    act.wait_ge(self.bias.sem, self.bias.at(g, k + 1))
                    act.wait_ge(self.pT_ps.sem, self.pT_ps.at(g, k - 7))
                    act.wait_ge(self.rsum.sem, self.rsum.at(g, k + 1 - UNITS))
                    for j, h in enumerate(unit_heads(k)):
                        act.activation(
                            probs[:, k % 8, j, H:2 * P], s_bank[k % 2][:, j * BAND:(j + 1) * BAND], ACT.Exp,
                            bias=bias[:, k, j:j + 1], scale=rn[:, k // PAIRS, h:h + 1],
                            accum_out=sums[:, k, j:j + 1]).then_inc(self.probs.sem, 1)

                def move_pT(g, k):
                    act.wait_ge(self.pT_ps.sem, self.pT_ps.at(g, k + 1))
                    act.wait_ge(self.pv.sem, self.pv.at(g, k // 2 - 1))
                    c = BAND if k >= PAIRS else P
                    src = p_bank[:, 0:2 * BAND].rearrange("p (j c) -> p j c", j=2)[:, :, 0:c]
                    copy(pT[:, k % 4, :, 0:c], src).then_inc(self.pT_ready[1].sem, 1)

                def move_oT(g, t):
                    act.wait_ge(self.pv.sem, self.pv.at(g, PAIRS // 2 * (t + 1)))
                    act.wait_ge(self.wo.sem, self.wo.at(g, t))
                    copy(oT[:, :, :], o_bank[:, :].rearrange("p (a c) -> p a c", c=P)).then_inc(self.oT_ready.sem, 1)

                def body(g, par, there):
                    for s in range(UNITS):
                        if 0 in there:
                            exp(g, s)
                        for d, t in in_slot(s, O_T, NB):
                            if d in there:
                                move_oT(g + d, t)
                        for d, t in in_slot(s, Q_T, NB):
                            if d in there:
                                take_qT(g + d, t)
                        for d, t in in_slot(s, K_T, NB):
                            if d in there:
                                take_kT(g + d, t)
                        for d, t in in_slot(s, MOVE_V, NB):
                            if d in there:
                                take_v(g + d, par if d == 0 else 1 - par, t)
                        for d, t in in_slot(s, SQUARE, NB):
                            if d in there:
                                square_qk(g + d, t)
                        for d, k in in_slot(s, P_T, UNITS, 1):
                            if d in there and k % 2 == 1:
                                move_pT(g + d, k)
                        for d, _ in in_slot(s, Y_T):
                            if d in there:
                                move_hT(g + d, par if d == 0 else 1 - par)

                modulo_pipeline(act, first, body)

            @block.tensor
            def _(pe):
                if run == 0:
                    for s in (self.yT_ps, self.qkv, self.v_ps, self.qT_ps, self.kT_ps, self.scores, self.pT_ps, self.pv,
                              self.wo):
                        pe.sem_inc(s.sem, s.credit())
                pe.wait_ge(self.cleared, 2 * run + 2)


                def transpose_y(g, par):
                    pe.wait_ge(self.kT_ready.sem, self.kT_ready.at(g, 2 - NB))
                    pe.wait_ge(self.moved.sem, self.moved.at(g, 3 - 2 * NB))
                    for b in range(NB):
                        pe.wait_ge(n.out_ready.sem, n.out_ready.at(g, b + 1))
                        ins = pe.transpose(t_bank[:, b * P:(b + 1) * P], n.out[:, par, b, :], W["ident"])
                    ins.then_inc(self.yT_ps.sem, 1)

                def make_qk(g, par, t):
                    pe.wait_ge(self.hT_ready.sem, self.hT_ready.at(g, 2))
                    pe.wait_ge(self.squares.sem, self.squares.at(g, t))
                    pe.wait_ge(self.terms.sem, self.terms.at(g, 3 * t))
                    for j in range(2):
                        part = slice(j * INNER, (j + 1) * INNER)
                        ins = pe.matmul(qk_bank[:, part], hT[:, par, t * P:(t + 1) * P], wqkv[:, part],
                                        start=True, stop=True)
                    ins.then_inc(self.qkv.sem, 1)

                def make_v(g, par, t):
                    pe.wait_ge(self.v_ready.sem, self.v_ready.at(g, t))
                    pe.matmul(v_bank[:, :], hT[:, par, t * P:(t + 1) * P], wqkv[:, 2 * INNER:3 * INNER],
                              start=True, stop=True).then_inc(self.v_ps.sem, 1)

                def transpose_q(g, t, more):
                    pe.wait_ge(self.q_turned.sem, self.q_turned.at(g, t + 1))
                    pe.wait_ge(self.kT_ready.sem, self.kT_ready.at(g, t))
                    if t == NB - 2 and more:
                        pe.wait_ge(self.hT_ready.sem, self.hT_ready.at(g + 1, 2))
                    else:
                        pe.wait_ge(self.moved.sem, self.moved.at(g, t + 1 - NB))
                    for a in range(PAIRS):
                        ins = pe.transpose(t_bank[:, a * P:(a + 1) * P], qk[:, a * P:(a + 1) * P], W["ident"])
                    ins.then_inc(self.qT_ps.sem, 1)

                def transpose_k(g, t):
                    pe.wait_ge(self.k_normed.sem, self.k_normed.at(g, t + 1))
                    pe.wait_ge(self.qT_ready.sem, self.qT_ready.at(g, t + 1))
                    for a in range(PAIRS):
                        ins = pe.transpose(t_bank[:, a * P:(a + 1) * P], qk[:, INNER + a * P:INNER + (a + 1) * P],
                                           W["ident"])
                    ins.then_inc(self.kT_ps.sem, 1)

                def score(g, k):
                    t = k // PAIRS
                    pe.wait_ge(self.qT_ready.sem, self.qT_ready.at(g, t + 1))
                    pe.wait_ge(self.kT_ready.sem, self.kT_ready.at(g, t + 1))
                    pe.wait_ge(self.probs.sem, self.probs.at(g, 2 * (k - 1)))
                    skip = WINDOW if t == 0 else 0
                    bank = s_bank[k % 2]
                    pe.matmul(bank[:, 0:2 * BAND], W["ident16"], W["band"][:, min(t, 1), :], start=True, stop=False)
                    for j, h in enumerate(unit_heads(k)):
                        rows = slice(LD * (h % 2), LD * (h % 2) + LD)
                        ins = pe.matmul(bank[:, j * BAND + skip:(j + 1) * BAND], qT[rows, t % 2, h // 2, :],
                                        kT[rows, h // 2, t * P - WINDOW + skip:(t + 1) * P], start=False, stop=(j == 1))
                    ins.then_inc(self.scores.sem, 1)

                def transpose_p(g, k):
                    pe.wait_ge(self.divided.sem, self.divided.at(g, k + 1))
                    copied = self.pT_ready[(k - 1) % 2]
                    pe.wait_ge(copied.sem, copied.at(g, (k + 1) // 2 if k % 2 else k // 2))
                    for j in range(2):
                        o = p_bank[:, j * BAND:(j + 1) * BAND]
                        ins = pe.transpose(o[:, 0:P], probs[:, k % 8, j, P:2 * P], W["ident"])
                        if k >= PAIRS:
                            ins = pe.transpose(o[:, P:BAND], probs[0:WINDOW, k % 8, j, 0:P],
                                               W["ident"][0:WINDOW, 0:WINDOW])
                    ins.then_inc(self.pT_ps.sem, 1)

                def times_v(g, par, k):
                    t = k // PAIRS
                    pe.wait_ge(self.pT_ready[0].sem, self.pT_ready[0].at(g, k // 2 + 1))
                    pe.wait_ge(self.pT_ready[1].sem, self.pT_ready[1].at(g, k // 2 + 1))
                    if k % PAIRS == 0:
                        pe.wait_ge(self.oT_ready.sem, self.oT_ready.at(g, t))
                    for j in range(2):
                        for own in (True, False)[0:2 if t else 1]:
                            for u in (k, k + 1):
                                h = unit_heads(u)[j]
                                o = o_bank[LD * (h % 2):LD * (h % 2) + LD, h // 2 * P:(h // 2 + 1) * P]
                                v_ = vs[:, par, t if own else t - 1, h * LD:(h + 1) * LD]
                                if own:
                                    ins = pe.matmul(o, v_, pT[:, u % 4, j, 0:P], start=True, stop=(t == 0))
                                else:
                                    ins = pe.matmul(o[:, 0:WINDOW], v_, pT[:, u % 4, j, P:BAND],
                                                    start=False, stop=True)
                    ins.then_inc(self.pv.sem, 1)

                def project(g, t, more):
                    pe.wait_ge(self.oT_ready.sem, self.oT_ready.at(g, t + 1))
                    pe.wait_ge(self.kT_ready.sem, self.kT_ready.at(g, t + 4 if more else NB))
                    pe.wait_ge(self.moved.sem, self.moved.at(g, t))
                    for a in range(PAIRS):
                        ins = pe.matmul(t_bank[:, 0:DIM], oT[:, a, :], wo[:, a, :], start=(a == 0),
                                        stop=(a == PAIRS - 1))
                    ins.then_inc(self.wo.sem, 1)

                def body(g, par, there):
                    for s in range(UNITS):
                        for d, t in in_slot(s, QK, NB):
                            if d in there:
                                make_qk(g + d, par if d == 0 else 1 - par, t)
                        for d, k in in_slot(s, SCORE, UNITS, 1):
                            if d in there:
                                score(g + d, k)
                        for d, k in in_slot(s, P_T, UNITS, 1):
                            if d in there:
                                transpose_p(g + d, k)
                        for d, t in in_slot(s, PROJECT, NB):
                            if d in there:
                                project(g + d, t, d + 1 in there)
                        for d, t in in_slot(s, Q_T, NB):
                            if d in there:
                                transpose_q(g + d, t, d + 1 in there)
                        for d, t in in_slot(s, K_T, NB):
                            if d in there:
                                transpose_k(g + d, t)
                        for d, _ in in_slot(s, Y_T):
                            if d in there:
                                transpose_y(g + d, par if d == 0 else 1 - par)
                        for d, k in in_slot(s, TIMES_V, UNITS, 1):
                            if d in there and k % 2 == 0:
                                times_v(g + d, par if d == 0 else 1 - par, k)
                        for d, t in in_slot(s, V, NB):
                            if d in there:
                                make_v(g + d, par if d == 0 else 1 - par, t)

                modulo_pipeline(pe, first, body)


SPLIT = 3
PAIR_ROWS = SPLIT * SPLIT * HD
ROWS = PAIR_ROWS + SPLIT
GROUPS = HEADS // 4
PANE = 32
STEPS = 8
SLOTS = GROUPS * STEPS
ATOPS = NB * 4


class GlobalAttention:

    def __init__(self, ctx, nc, kind):
        sig = lambda n, per, unit=1: Signal(ctx, nc, f"{kind}_{n}", per, unit)
        self.kind, self.causal = kind, kind == "causal"
        self.norm = Norm(ctx, nc, kind + "_norm")
        self.xs_ready = sig("xs_ready", 1)
        self.hT_ps = sig("hT_in_psum", 1)
        self.hT_ready = sig("hT_ready", 1)
        self.made = sig("qkv_in_psum", 3 if self.causal else 5)
        self.qk_ready = sig("qk_ready", 2)
        self.v_ready = sig("v_ready", 1)
        self.part = sig("part_ready", 6)
        self.rest = sig("rest_ready", 4)
        self.spread_q = sig("spread_q", 9, 16)
        self.spread_k = sig("spread_k", 9, 16)
        self.a_scores = sig("a_scores", GROUPS * ATOPS)
        self.top = sig("top", GROUPS * ATOPS)
        self.top_step = sig("top_step", GROUPS * 5)
        self.mT_ps = sig("mT_in_psum", GROUPS)
        self.mT_ready = sig("mT_ready", GROUPS)
        self.m_spread = sig("m_spread", GROUPS, 16)
        self.b_scores = sig("b_scores", 2 * SLOTS)
        self.probs = sig("probs", 2 * SLOTS)
        self.pv = sig("pv", 4 * GROUPS)
        self.oT_ready = sig("oT_ready", GROUPS)
        self.o_ps = sig("o_in_psum", NB)
        self.out_step = sig("out_step", NB * 11 - 2 if self.causal else NB)
        self.on_ready = sig("on_ready", NB)
        self.onT_ps = sig("onT_in_psum", 1)
        self.onT_ready = sig("onT_ready", 1)
        self.proj = sig("proj_ready", 1)
        self.moved = sig("result_stored", 1)
        self.setup = ctx.enter_context(nc.semaphore(kind + "_setup"))
        if self.causal:
            self.tops_clipped = sig("tops_clipped", GROUPS)
            self.floor_ps = sig("floor_in_psum", HEADS)
            self.floor = sig("floor_ready", HEADS)
            self.clipped = sig("clipped", 2 * SLOTS)
            self.o_moved = sig("o_moved", NB)
            self.vsum_ps = sig("vsum_in_psum", 1)
            self.vsum_ready = sig("vsum_ready", 1)
            self.vsum_step = sig("vsum_step", 3)
            self.away_ready = sig("away_ready", 1)
            self.tables_made = ctx.enter_context(nc.semaphore(kind + "_tables_made"))
        else:
            self.turn = sig("turn_step", 4)
            self.biased = sig("biased", 1)

    def emit(self, nc, run, X, W):
        assert run == 0
        n, first, causal, kind = self.norm, 0, self.causal, self.kind
        wq, wproj = W[kind + "_wqkv"], W[kind + "_wproj"]
        with ExitStack() as ctx:
            pb = lambda name, banks=1: ctx.enter_context(nc.psum_tensor(f"{kind}_{name}", [P, banks * SEQ], F32))
            sb = lambda name, s, dt=F32: ctx.enter_context(nc.sbuf_tensor(f"{kind}_{name}", s, dt))
            n.buffers(ctx, nc, run)
            a_bank = [pb(f"a{j}") for j in range(3)]
            b_bank = [pb(f"b{j}") for j in range(3)]
            o_bank = pb("o")
            m_bank = pb("m")
            m16 = m_bank[:, :].bitcast(BF16)
            xs = sb("xs", [P, NB, DIM])
            hT = sb("hTs", [P, SEQ])
            full = sb("full", [P, 2, SEQ])
            rest = sb("rest", [P, SEQ])
            parts = sb("parts", [P, 2, SPLIT, SEQ], BF16)
            rep = {x: sb(x + "_rows", [ROWS + 1, 2, HEADS, SEQ], BF16) for x in "qk"}
            vs = sb("vs", [P, 2, NB, HEADS, PANE])
            tops = sb("tops", [P, 2, NB, HEADS])
            toprest = sb("toprest", [P, NB, 4])
            topp = sb("topp", [P, NB, SPLIT, 4], BF16)
            mT = sb("mT", [SPLIT * 4, SEQ], BF16)
            pT = sb("pT", [P, 2, 4, 2, SEQ])
            oT = sb("oT", [P, 2, GROUPS, SEQ])
            den = sb("den", [P, 3, HEADS])
            on = sb("on", [P, NB, HEADS, HD])
            onT = sb("onT", [P, SEQ])
            if not causal:
                t1 = sb("t1", [P, SEQ])
                t2 = sb("t2", [P, SEQ])
                total = sb("total", [P, NB, DIM])
            else:
                floor = sb("floor", [P, 4, SEQ])
                away = sb("away", [P, NB, HEADS])
                vsum = sb("vsum", [P, NB, HEADS, HD])
                ot = sb("ot", [P, 2, HEADS, HD])
                o_rows = sb("o_rows", [P, 2, SEQ])
                ones_rows = sb("ones_rows", [ROWS + 1, P], BF16)
                diag = sb("diag", [P, 2, P], BF16)
            number = lambda name: W["numbers"][:, NUMBERS.index(name), :]
            o_read = self.o_moved if causal else self.on_ready
            result_read = self.moved if causal else self.biased
            block = ctx.enter_context(nc.Block())

            def width(kb):
                return P * kb if causal else 0

            if causal:
                STATS, APPLY, H_T, Q, K, V = -32, -31, -29, -28, -27, -21
                QS = KS = None
                PARTS = -27, -24
                O, ON_T, PROJECT = (44, 45, 51, 52), 59, 60
            else:
                STATS, APPLY, H_T, Q, QS, K, KS, V = -32, -31, -29, -28, -27, -26, -25, -24
                PARTS = -26, -23
                O, ON_T, PROJECT = (43, 44, 45, 46), 47, 48
            A, TOP_PARTS, TOP_T, MOVE_TOP = -15, -7, -6, -6 if causal else -5
            B, TIMES_V, MOVE_O = -1, 5, 11
            FLOOR, V_SUM, AWAY = -1, 29, 33
            in_slot = lambda s, offset, count=1, every=1: due(s, SLOTS, offset, count, every)
            later = lambda d, par: par if d == 0 else 1 - par

            @block.sync
            def _(sp):
                for s in (self.spread_q, self.spread_k):
                    sp.sem_inc(s.sem, s.credit())
                sp.wait_ge(self.setup, 1)

                def spread(g, par, x):
                    name, spread_x = (("q", self.spread_q), ("k", self.spread_k))[x]
                    sp.wait_ge(self.part.sem, self.part.at(g, 3 * x + 3))
                    for i in range(SPLIT):
                        for j in range(SPLIT):
                            r = (SPLIT * i + j) * HD
                            sp.dma_start(rep[name][r:r + HD, par, :, :], parts[:, x, (i, j)[x], :])\
                                .then_inc(spread_x.sem, 16)

                def body(g, par, there):
                    for s in range(SLOTS):
                        for x in range(2):
                            for d, _ in in_slot(s, PARTS[x] + 2):
                                if d in there:
                                    spread(g + d, later(d, par), x)

                modulo_pipeline(sp, first, body)

            @block.gpsimd
            def _(pl):
                for s in (n.rstd_ready, self.rest, self.top_step):
                    pl.sem_inc(s.sem, s.credit())
                if causal:
                    pl.sem_inc(self.vsum_step.sem, self.vsum_step.credit())
                    pl.sem_inc(self.out_step.sem, self.out_step.credit())
                    pl.sem_inc(self.on_ready.sem, self.on_ready.credit())
                else:
                    pl.sem_inc(self.qk_ready.sem, self.qk_ready.credit())
                    pl.sem_inc(self.moved.sem, self.moved.credit())
                pl.memset(rep["k"][64:ROWS + 1, :, :, :], 1.0).then_inc(self.setup, 1)
                pl.wait_ge(self.setup, 1)
                pl.memset(rep["q"][64:ROWS + 1, :, :, :], 0.0).then_inc(self.setup, 1)
                pl.wait_ge(self.setup, 2)
                pl.memset(vs[:, :, :, :, :], 0.0).then_inc(self.setup, 1)
                pl.wait_ge(self.setup, 3)
                pl.memset(vs[:, :, :, :, HD:HD + 1], 1.0).then_inc(self.setup, 1)

                def subtract_part(g, x, i):
                    pl.wait_ge(self.part.sem, self.part.at(g, 3 * x + i + 1))
                    src = full[:, x, :] if i == 0 else rest[:, :]
                    pl.tensor_tensor(rest[:, :], src, parts[:, x, i, :], ALU.subtract).then_inc(self.rest.sem, 1)

                def sum_turned(g, x):
                    pl.wait_ge(self.turn.sem, self.turn.at(g, 2 * x + 2))
                    pl.wait_ge(self.rest.sem, self.rest.at(g, 2 * x + 1 - 4))
                    pl.wait_ge(self.part.sem, self.part.at(g, 3 * x + 1 - 6))
                    pl.tensor_tensor(full[:, x, :], t1[:, :], t2[:, :], ALU.add).then_inc(self.qk_ready.sem, 1)

                def add_result(g):
                    pl.wait_ge(self.biased.sem, self.biased.at(g, 1))
                    x = slot(X, g, first)
                    pl.tensor_tensor(x, total[:, :, :], x, ALU.add).then_inc(self.moved.sem, 1)

                def top_parts(g, par, gr):
                    n0 = gr * (self.top_step.per // GROUPS)
                    pl.wait_ge(self.top.sem, self.top.at(g, ATOPS * (gr + 1)))
                    m = tops[:, par, :, 4 * gr:4 * gr + 4]
                    by_block = lambda name: number(name).rearrange("p (b h) -> p b h", b=NB)
                    if causal:
                        pl.wait_ge(self.tops_clipped.sem, self.tops_clipped.at(g, gr + 1))
                    pl.wait_ge(self.mT_ps.sem, self.mT_ps.at(g, gr))
                    for i in range(SPLIT):
                        src = m if i == 0 else toprest[:, :, :]
                        pl.tensor_tensor(topp[:, :, i, :], src, by_block("1"), ALU.mult)\
                            .then_inc(self.top_step.sem, 1)
                        pl.wait_ge(self.top_step.sem, self.top_step.at(g, n0 + 2 * i + 1))
                        if i < SPLIT - 1:
                            pl.tensor_tensor(toprest[:, :, :], src, topp[:, :, i, :], ALU.subtract)\
                                .then_inc(self.top_step.sem, 1)
                            pl.wait_ge(self.top_step.sem, self.top_step.at(g, n0 + 2 * i + 2))

                def v_sums(g):
                    pl.wait_ge(self.vsum_ready.sem, self.vsum_ready.at(g, 1))
                    for i, b in enumerate((2, 1, 0)):
                        pl.tensor_tensor(vsum[:, b, :, :], vsum[:, b, :, :], vsum[:, b + 1, :, :], ALU.add)\
                            .then_inc(self.vsum_step.sem, 1)
                        pl.wait_ge(self.vsum_step.sem, self.vsum_step.at(g, i + 1))

                def output(g, b):
                    o3 = o_rows[:, b % 2, :].rearrange("p (h c) -> p h c", c=PANE)
                    o, sums = o3[:, :, 0:HD], o3[:, :, HD]
                    bc = lambda t: t.unsqueeze(2).broadcast_to([P, HEADS, HD])
                    n0 = 11 * b
                    d0, d1, d2 = (den[:, i, :] for i in range(3))
                    u, w = ot[:, 0, :, :], ot[:, 1, :, :]
                    pl.wait_ge(self.o_moved.sem, self.o_moved.at(g, b + 1))
                    pl.wait_ge(self.away_ready.sem, self.away_ready.at(g, 1))
                    pl.wait_ge(self.vsum_step.sem, self.vsum_step.at(g, 3))
                    pl.wait_ge(self.onT_ps.sem, self.onT_ps.at(g, 0))
                    pl.wait_ge(self.on_ready.sem, self.on_ready.at(g, b))
                    pl.tensor_tensor(d0, away[:, b, :], number(f"masked_{b}"), ALU.mult)\
                        .then_inc(self.out_step.sem, 1)
                    pl.wait_ge(self.out_step.sem, self.out_step.at(g, n0 + 1))
                    pl.tensor_tensor(d0, d0, sums, ALU.add).then_inc(self.out_step.sem, 1)
                    pl.wait_ge(self.out_step.sem, self.out_step.at(g, n0 + 2))
                    pl.tensor_tensor(d1, d0, number("1e-6"), ALU.add).then_inc(self.out_step.sem, 1)
                    pl.wait_ge(self.out_step.sem, self.out_step.at(g, n0 + 3))
                    pl.tensor_tensor(d1, d1, number("1e-8"), ALU.mult).then_inc(self.out_step.sem, 1)
                    pl.wait_ge(self.out_step.sem, self.out_step.at(g, n0 + 4))
                    pl.tensor_tensor(d2, d1, number("keys"), ALU.mult).then_inc(self.out_step.sem, 1)
                    pl.wait_ge(self.out_step.sem, self.out_step.at(g, n0 + 5))
                    pl.tensor_tensor(d2, d2, d0, ALU.add).then_inc(self.out_step.sem, 1)
                    pl.wait_ge(self.out_step.sem, self.out_step.at(g, n0 + 6))
                    pl.tensor_tensor(d2, d2, number("minus_1"), ALU.pow).then_inc(self.out_step.sem, 1)
                    pl.tensor_tensor(u, vsum[:, 0, :, :], bc(d1), ALU.mult).then_inc(self.out_step.sem, 1)
                    pl.wait_ge(self.out_step.sem, self.out_step.at(g, n0 + 8))
                    if b < NB - 1:
                        pl.tensor_tensor(w, vsum[:, b + 1, :, :], bc(away[:, b, :]), ALU.mult)\
                            .then_inc(self.out_step.sem, 1)
                        pl.wait_ge(self.out_step.sem, self.out_step.at(g, n0 + 9))
                        pl.tensor_tensor(u, u, w, ALU.add).then_inc(self.out_step.sem, 1)
                        pl.wait_ge(self.out_step.sem, self.out_step.at(g, n0 + 10))
                        n0 += 2
                    pl.tensor_tensor(w, o, u, ALU.add).then_inc(self.out_step.sem, 1)
                    pl.wait_ge(self.out_step.sem, self.out_step.at(g, n0 + 9))
                    pl.tensor_tensor(on[:, b, :, :], w, bc(d2), ALU.mult).then_inc(self.on_ready.sem, 1)

                def body(g, par, there):
                    for s in range(SLOTS):
                        for d, _ in in_slot(s, STATS):
                            if d in there:
                                n.pool(pl, g + d, W["minus_half"])
                        for d, gr in in_slot(s, TOP_PARTS, GROUPS, STEPS):
                            if d in there:
                                top_parts(g + d, later(d, par), gr)
                        for x in range(2):
                            for i in range(SPLIT - 1):
                                for d, _ in in_slot(s, PARTS[x] + i):
                                    if d in there:
                                        subtract_part(g + d, x, i)
                        for d, _ in in_slot(s, V_SUM + 1):
                            if d in there and causal:
                                v_sums(g + d)
                        if not causal:
                            for x, swapped in enumerate((QS, KS)):
                                for d, _ in in_slot(s, swapped):
                                    if d in there:
                                        sum_turned(g + d, x)
                            for d, _ in in_slot(s, PROJECT + 1):
                                if d in there:
                                    add_result(g + d)
                        for b in range(NB):
                            for d, _ in in_slot(s, O[b]):
                                if d in there and causal:
                                    output(g + d, b)

                modulo_pipeline(pl, first, body)

            @block.vector
            def _(v):
                for s in (*n.of_vector, self.xs_ready, self.top, *((self.tops_clipped, self.clipped) if causal else
                                                                   (self.turn, self.biased))):
                    v.sem_inc(s.sem, s.credit())
                if causal:
                    v.sem_inc(self.moved.sem, self.moved.credit())
                else:
                    v.sem_inc(self.out_step.sem, self.out_step.credit())
                    v.sem_inc(self.on_ready.sem, self.on_ready.credit())
                if causal:
                    v.tensor_copy(ones_rows[0:ROWS, :], W["ones_rows"]).then_inc(self.tables_made, 1)
                    v.tensor_copy(diag[:, :, :], W["diag"]).then_inc(self.tables_made, 1)

                def stats(g):
                    v.wait_ge(n.out_ready.sem, n.out_ready.at(g, 0))
                    v.tensor_scalar(xs[:, :, :], slot(X, g, first), 1.0, None, ALU.mult)\
                        .then_inc(self.xs_ready.sem, 1)
                    v.wait_ge(self.xs_ready.sem, self.xs_ready.at(g, 1))
                    n.vector_stats(v, g, xs)

                def turn(g, x, swapped):
                    if not swapped:
                        v.wait_ge(self.made.sem, self.made.at(g, 2 * x + 1))
                        v.wait_ge(self.qk_ready.sem, self.qk_ready.at(g, x))
                        v.tensor_tensor(t1[:, :], m_bank[:, :], W["rope"][:, x, 0, :], ALU.mult)\
                            .then_inc(self.turn.sem, 1)
                    else:
                        v.wait_ge(self.made.sem, self.made.at(g, 2 * x + 2))
                        v.tensor_tensor(t2[:, :], m_bank[:, :], W["rope"][:, x, 1, :], ALU.mult)\
                            .then_inc(self.turn.sem, 1)

                def top(g, par, a):
                    gr, b, j = a // ATOPS, a % ATOPS // 4, a % 4
                    v.wait_ge(self.a_scores.sem, self.a_scores.at(g, a + 1))
                    if a % ATOPS == 0:
                        per = self.top_step.per
                        v.wait_ge(self.top_step.sem, self.top_step.at(g, (gr + 1) * per // GROUPS - 2 * per))
                        if causal:
                            v.wait_ge(self.away_ready.sem, self.away_ready.at(g, -1))
                    keys = P * (b + 1) if causal else SEQ
                    h = 4 * gr + j
                    v.tensor_reduce(tops[:, par, b, h:h + 1], a_bank[a % 3][:, 0:keys], AX.X, ALU.max,
                                                       negate=True).then_inc(self.top.sem, 1)

                def clip_tops(g, par, gr):
                    v.wait_ge(self.top.sem, self.top.at(g, ATOPS * (gr + 1)))
                    m = tops[:, par, :, 4 * gr:4 * gr + 4]
                    v.tensor_scalar(m, m, -100.0, 100.0, ALU.max, ALU.min).then_inc(self.tops_clipped.sem, 1)

                def clip(g, s):
                    gr, c, j = s // STEPS, s % STEPS // 4, s % 4
                    v.wait_ge(self.floor.sem, self.floor.at(g, 4 * gr + j + 1))
                    v.wait_ge(self.pv.sem, self.pv.at(g, 4 * gr + 2 * c - 2))
                    for i in range(2):
                        q0 = width(2 * c + i)
                        v.wait_ge(self.b_scores.sem, self.b_scores.at(g, 2 * s + i + 1))
                        v.scalar_tensor_tensor(
                            out=pT[:, c, j, i, q0:SEQ], in0=b_bank[(2 * s + i) % 3][:, q0:SEQ], scalar=0.0,
                            in1=floor[:, j, q0:SEQ], op0=ALU.min, op1=ALU.max).then_inc(self.clipped.sem, 1)

                def output(g, b):
                    o3 = m_bank[:, :].rearrange("p (h c) -> p h c", c=PANE)
                    v.wait_ge(self.o_ps.sem, self.o_ps.at(g, b + 1))
                    v.wait_ge(self.onT_ps.sem, self.onT_ps.at(g, 0))
                    v.wait_ge(self.on_ready.sem, self.on_ready.at(g, b))
                    v.reciprocal(den[:, 0, :], o3[:, :, HD]).then_inc(self.out_step.sem, 1)
                    v.wait_ge(self.out_step.sem, self.out_step.at(g, b + 1))
                    v.tensor_tensor(on[:, b, :, :], o3[:, :, 0:HD],
                                    den[:, 0, :].unsqueeze(2).broadcast_to([P, HEADS, HD]), ALU.mult)\
                        .then_inc(self.on_ready.sem, 1)

                def result(g):
                    v.wait_ge(self.proj.sem, self.proj.at(g, 1))
                    out3 = m_bank[:, :].rearrange("p (b d) -> p b d", b=NB)
                    v.wait_ge(self.moved.sem, self.moved.at(g, 0))
                    x = slot(X, g, first)
                    if causal:
                        v.tensor_tensor(x, out3, x, ALU.add).then_inc(self.moved.sem, 1)
                    else:
                        v.tensor_tensor(
                            total[:, :, :], out3, W["b_proj"].unsqueeze(1).broadcast_to([P, NB, DIM]), ALU.add)\
                            .then_inc(self.biased.sem, 1)

                def body(g, par, there):
                    for s in range(SLOTS):
                        if causal and 0 in there:
                            clip(g, s)
                        for d, m in in_slot(s, A, GROUPS * ATOPS // 2):
                            if d in there:
                                top(g + d, later(d, par), 2 * m)
                                top(g + d, later(d, par), 2 * m + 1)
                        for b in range(NB):
                            for d, _ in in_slot(s, O[b]):
                                if d in there and not causal:
                                    output(g + d, b)
                        for d, _ in in_slot(s, PROJECT):
                            if d in there:
                                result(g + d)
                        if not causal:
                            for x, (plain, swapped) in enumerate(((Q, QS), (K, KS))):
                                for d, _ in in_slot(s, plain):
                                    if d in there:
                                        turn(g + d, x, False)
                                for d, _ in in_slot(s, swapped):
                                    if d in there:
                                        turn(g + d, x, True)
                        for d, _ in in_slot(s, STATS):
                            if d in there:
                                stats(g + d)
                        for d, _ in in_slot(s, APPLY):
                            if d in there:
                                i = g + d
                                n.vector_apply(v, i, later(d, par), xs,
                                               lambda: v.wait_ge(self.hT_ps.sem, self.hT_ps.at(i, -1)))
                        for d, gr in in_slot(s, A + 7, GROUPS, STEPS):
                            if d in there and causal:
                                clip_tops(g + d, later(d, par), gr)

                modulo_pipeline(v, first, body)

            @block.scalar
            def _(act):
                for s in (self.m_spread, self.hT_ready, self.v_ready, self.part, self.mT_ready, self.probs,
                          self.oT_ready, self.onT_ready,
                          *((self.o_moved, self.floor, self.vsum_ready, self.away_ready) if causal else ())):
                    act.sem_inc(s.sem, s.credit())
                if causal:
                    act.sem_inc(self.qk_ready.sem, self.qk_ready.credit())
                act.wait_ge(self.setup, 4)
                copy = lambda o, i: act.activation(o, i, ACT.Copy)

                def move_part(g, x, i):
                    if i == 0:
                        act.wait_ge(self.qk_ready.sem, self.qk_ready.at(g, x + 1))
                        spread_x = (self.spread_q, self.spread_k)[x]
                        act.wait_ge(spread_x.sem, spread_x.at(g, 0))
                    else:
                        act.wait_ge(self.rest.sem, self.rest.at(g, 2 * x + i))
                    copy(parts[:, x, i, :], full[:, x, :] if i == 0 else rest[:, :]).then_inc(self.part.sem, 1)

                def move_hT(g):
                    act.wait_ge(self.hT_ps.sem, self.hT_ps.at(g, 1))
                    act.wait_ge(self.made.sem, self.made.at(g, 0))
                    copy(hT[:, :], m_bank[:, :]).then_inc(self.hT_ready.sem, 1)

                def move_qk(g, x):
                    act.wait_ge(self.made.sem, self.made.at(g, x + 1))
                    act.wait_ge(self.rest.sem, self.rest.at(g, 2 * x + 1 - 4))
                    act.wait_ge(self.part.sem, self.part.at(g, 3 * x + 1 - 6))
                    act.activation(full[:, x, :], m_bank[:, :], ACT.Copy, scale=1.0 if x else float(HD) ** -0.5)\
                        .then_inc(self.qk_ready.sem, 1)

                def move_v(g, par):
                    act.wait_ge(self.made.sem, self.made.at(g, self.made.per))
                    act.wait_ge(self.pv.sem, self.pv.at(g, -4 * GROUPS))
                    if causal:
                        act.wait_ge(self.vsum_ps.sem, self.vsum_ps.at(g, -1))
                    copy(vs[:, par, :, :, 0:HD], m_bank[:, :].rearrange("p (b h d) -> p b h d", b=NB, d=HD))\
                        .then_inc(self.v_ready.sem, 1)

                def take_mT(g, gr):
                    act.wait_ge(self.mT_ps.sem, self.mT_ps.at(g, gr + 1))
                    act.wait_ge(self.m_spread.sem, self.m_spread.at(g, gr))
                    copy(mT[:, :], m16[0:SPLIT * 4, 0:SEQ]).then_inc(self.mT_ready.sem, 1)

                def spread_top(g, par, gr):
                    act.wait_ge(self.mT_ready.sem, self.mT_ready.at(g, gr + 1))
                    act.dma_start(rep["q"][PAIR_ROWS:ROWS, par, 4 * gr:4 * gr + 4, :], mT[:, :])\
                        .then_inc(self.m_spread.sem, 16)

                def take_floor(g, h):
                    act.wait_ge(self.floor_ps.sem, self.floor_ps.at(g, h + 1))
                    act.wait_ge(self.clipped.sem, self.clipped.at(g, 2 * STEPS * (h // 4)))
                    act.activation(floor[:, h % 4, :], m_bank[:, :], ACT.Identity,
                                                        bias=W["minus_100"]).then_inc(self.floor.sem, 1)

                def exp(g, s):
                    gr, c, j = s // STEPS, s % STEPS // 4, s % 4
                    for i in range(2):
                        q0 = width(2 * c + i)
                        p_ = pT[:, c, j, i, q0:SEQ]
                        if causal:
                            act.wait_ge(self.clipped.sem, self.clipped.at(g, 2 * s + i + 1))
                            act.activation(p_, p_, ACT.Exp).then_inc(self.probs.sem, 1)
                        else:
                            act.wait_ge(self.b_scores.sem, self.b_scores.at(g, 2 * s + i + 1))
                            act.wait_ge(self.pv.sem, self.pv.at(g, 4 * gr + 2 * c - 2))
                            act.activation(p_, b_bank[(2 * s + i) % 3][:, :], ACT.Exp).then_inc(self.probs.sem, 1)

                def take_o(g, par, gr):
                    act.wait_ge(self.pv.sem, self.pv.at(g, 4 * gr + 4))
                    act.wait_ge(self.o_ps.sem, self.o_ps.at(g, -NB))
                    copy(oT[:, par, gr, :], o_bank[:, :]).then_inc(self.oT_ready.sem, 1)

                def move_v_sums(g):
                    act.wait_ge(self.vsum_ps.sem, self.vsum_ps.at(g, 1))
                    act.wait_ge(self.on_ready.sem, self.on_ready.at(g, 0))
                    copy(vsum[:, :, :, :], m_bank[:, :].rearrange("p (b h d) -> p b h d", b=NB, d=HD))\
                        .then_inc(self.vsum_ready.sem, 1)

                def take_away(g, par):
                    act.wait_ge(self.top_step.sem, self.top_step.at(g, self.top_step.per))
                    act.wait_ge(self.on_ready.sem, self.on_ready.at(g, 0))
                    act.activation(away[:, :, :], tops[:, par, :, :], ACT.Exp, bias=W["minus_100"])\
                        .then_inc(self.away_ready.sem, 1)

                def move_o_rows(g, b):
                    act.wait_ge(self.o_ps.sem, self.o_ps.at(g, b + 1))
                    act.wait_ge(self.on_ready.sem, self.on_ready.at(g, b - 1))
                    copy(o_rows[:, b % 2, :], m_bank[:, :]).then_inc(self.o_moved.sem, 1)

                def move_onT(g):
                    act.wait_ge(self.onT_ps.sem, self.onT_ps.at(g, 1))
                    act.wait_ge(self.proj.sem, self.proj.at(g, 0))
                    copy(onT[:, :], m_bank[:, :]).then_inc(self.onT_ready.sem, 1)

                def body(g, par, there):
                    for s in range(SLOTS):
                        for b in range(NB):
                            for d, _ in in_slot(s, O[b]):
                                if d in there and causal:
                                    move_o_rows(g + d, b)
                        for j in range(4):
                            for d, gr in in_slot(s, FLOOR + j, GROUPS, STEPS):
                                if d in there and causal:
                                    take_floor(g + d, 4 * gr + j)
                        if 0 in there:
                            exp(g, s)
                        for d, gr in in_slot(s, MOVE_TOP, GROUPS, STEPS):
                            if d in there:
                                take_mT(g + d, gr)
                                spread_top(g + d, later(d, par), gr)
                        for d, gr in in_slot(s, MOVE_O, GROUPS, STEPS):
                            if d in there:
                                take_o(g + d, later(d, par), gr)
                        for d, _ in in_slot(s, H_T):
                            if d in there:
                                move_hT(g + d)
                        for d, _ in in_slot(s, V):
                            if d in there:
                                move_v(g + d, later(d, par))
                        for d, _ in in_slot(s, V_SUM):
                            if d in there and causal:
                                move_v_sums(g + d)
                        for d, _ in in_slot(s, AWAY):
                            if d in there and causal:
                                take_away(g + d, later(d, par))
                        for d, _ in in_slot(s, ON_T):
                            if d in there:
                                move_onT(g + d)
                        for x in range(2):
                            for i in reversed(range(SPLIT)):
                                for d, _ in in_slot(s, PARTS[x] + i):
                                    if d in there:
                                        move_part(g + d, x, i)
                            for d, _ in in_slot(s, (Q, K)[x]):
                                if d in there and causal:
                                    move_qk(g + d, x)

                modulo_pipeline(act, first, body)

            @block.tensor
            def _(pe):
                for s in (self.hT_ps, self.made, self.a_scores, self.mT_ps, self.b_scores, self.pv, self.o_ps,
                          self.onT_ps, self.proj,
                          *((self.floor_ps, self.vsum_ps) if causal else ())):
                    pe.sem_inc(s.sem, s.credit())
                pe.wait_ge(self.setup, 4)
                if causal:
                    pe.wait_ge(self.tables_made, 2)


                def before(x, count):
                    if x >= 3:
                        return x - 2
                    return max(y for y in range(count - 3, count) if y % 3 == x) + 1 - count

                mul = lambda o, l, r: pe.matmul(o, l, r, start=True, stop=True)
                col = lambda i: slice(i * P, (i + 1) * P)

                def transpose_h(g, par):
                    pe.wait_ge(self.mT_ready.sem, self.mT_ready.at(g, 2 - GROUPS))
                    for b in range(NB):
                        pe.wait_ge(n.out_ready.sem, n.out_ready.at(g, b + 1))
                        ins = pe.transpose(m_bank[:, col(b)], n.out[:, par, b, :], W["ident"])
                    ins.then_inc(self.hT_ps.sem, 1)

                def make(g, i):
                    pe.wait_ge(self.hT_ready.sem, self.hT_ready.at(g, 1))
                    if causal and i:
                        pe.wait_ge(self.qk_ready.sem, self.qk_ready.at(g, 1))
                    elif i:
                        pe.wait_ge(self.turn.sem, self.turn.at(g, i))
                    mul(m_bank[:, :], wq[:, col(i if causal else (0, 2, 1, 3)[i])], hT[:, :])\
                        .then_inc(self.made.sem, 1)

                def make_v(g):
                    if causal:
                        pe.wait_ge(self.qk_ready.sem, self.qk_ready.at(g, 2))
                        pe.wait_ge(self.mT_ready.sem, self.mT_ready.at(g, 3 - GROUPS))
                    else:
                        pe.wait_ge(self.turn.sem, self.turn.at(g, 4))
                    for b in range(NB):
                        ins = mul(m_bank[:, col(b)], hT[:, col(b)], wq[:, col(2 if causal else 4)])
                    ins.then_inc(self.made.sem, 1)

                def a_scores(g, par, a):
                    gr, b, j = a // ATOPS, a % ATOPS // 4, a % 4
                    h = 4 * gr + j
                    if a == 0:
                        pe.wait_ge(self.spread_q.sem, self.spread_q.at(g, 9))
                        pe.wait_ge(self.spread_k.sem, self.spread_k.at(g, 9))
                    bank = a_bank[a % 3]
                    pe.wait_ge(self.top.sem, self.top.at(g, before(a, GROUPS * ATOPS)))
                    keys = P * (b + 1) if causal else SEQ
                    ins = pe.matmul(bank[:, 0:keys], rep["q"][0:PAIR_ROWS, par, h, b * P:(b + 1) * P],
                                    rep["k"][0:PAIR_ROWS, par, h, 0:keys], start=True, stop=not causal)
                    if causal:
                        ins = pe.matmul(bank[:, keys - P:keys], W["ident16"], diag[:, 0, :], start=False, stop=True)
                    ins.then_inc(self.a_scores.sem, 1)

                def transpose_tops(g, gr):
                    pe.wait_ge(self.top_step.sem, self.top_step.at(g, (gr + 1) * self.top_step.per // GROUPS))
                    for b in range(NB):
                        ins = pe.transpose(m16[0:SPLIT * 4, b * P:(b + 1) * P],
                                           topp[:, b, :, :].rearrange("p i j -> p (i j)"), W["ident16"])
                    ins.then_inc(self.mT_ps.sem, 1)

                def floors(g, par, h):
                    pe.wait_ge(self.floor.sem, self.floor.at(g, h))
                    pe.wait_ge(self.m_spread.sem, self.m_spread.at(g, h // 4 + 1))
                    mul(m_bank[:, :], ones_rows[0:ROWS, :], rep["q"][0:ROWS, par, h, :])\
                        .then_inc(self.floor_ps.sem, 1)

                def b_scores(g, par, s, i):
                    gr, c, j = s // STEPS, s % STEPS // 4, s % 4
                    h, x = 4 * gr + j, 2 * s + i
                    pe.wait_ge(self.m_spread.sem, self.m_spread.at(g, gr + 1))
                    if causal:
                        pe.wait_ge(self.clipped.sem, self.clipped.at(g, before(x, 2 * SLOTS)))
                    else:
                        pe.wait_ge(self.probs.sem, self.probs.at(g, before(x, 2 * SLOTS)))
                    kb = 2 * c + i
                    q0 = width(kb)
                    ins = pe.matmul(b_bank[x % 3][:, q0:SEQ], rep["k"][0:ROWS, par, h, kb * P:(kb + 1) * P],
                                    rep["q"][0:ROWS, par, h, q0:SEQ], start=True, stop=not causal)
                    if causal:
                        ins = pe.matmul(b_bank[x % 3][:, q0:q0 + P], W["ident16"], diag[:, 1, :], start=False,
                                        stop=True)
                    ins.then_inc(self.b_scores.sem, 1)

                def times_v(g, par, e, i):
                    gr, c = e // 2, e % 2
                    pe.wait_ge(self.probs.sem, self.probs.at(g, 8 * e + 7 + i))
                    if e == 0:
                        pe.wait_ge(self.v_ready.sem, self.v_ready.at(g, 1))
                    if c == 0:
                        pe.wait_ge(self.oT_ready.sem, self.oT_ready.at(g, gr))
                    kb = 2 * c + i
                    q0 = width(kb)
                    for j in range(4):
                        ins = pe.matmul(o_bank[PANE * j:PANE * (j + 1), q0:SEQ], vs[:, par, kb, 4 * gr + j, :],
                                        pT[:, c, j, i, q0:SEQ], start=(kb == 0), stop=(kb == NB - 1))
                    ins.then_inc(self.pv.sem, 1)

                def sum_v(g, par):
                    for b in range(NB):
                        ins = mul(m_bank[:, col(b)], W["ones"], vs[:, par, b, :, 0:HD])
                    ins.then_inc(self.vsum_ps.sem, 1)

                def transpose_o(g, par, b):
                    pe.wait_ge(self.oT_ready.sem, self.oT_ready.at(g, GROUPS))
                    pe.wait_ge(o_read.sem, o_read.at(g, b))
                    for gr in range(GROUPS):
                        ins = pe.transpose(m_bank[:, col(gr)], oT[:, par, gr, col(b)], W["ident"])
                    ins.then_inc(self.o_ps.sem, 1)

                def transpose_on(g):
                    pe.wait_ge(self.on_ready.sem, self.on_ready.at(g, NB))
                    for b in range(NB):
                        ins = pe.transpose(m_bank[:, col(b)], on[:, b, :, :].rearrange("p h d -> p (h d)"), W["ident"])
                    ins.then_inc(self.onT_ps.sem, 1)

                def project(g):
                    pe.wait_ge(self.onT_ready.sem, self.onT_ready.at(g, 1))
                    for b in range(NB):
                        ins = mul(m_bank[:, col(b)], onT[:, col(b)], wproj)
                    ins.then_inc(self.proj.sem, 1)

                def body(g, par, there):
                    for s in range(SLOTS):
                        for j in range(4):
                            for d, gr in in_slot(s, FLOOR + j, GROUPS, STEPS):
                                if d in there and causal:
                                    i = g + d
                                    if j == 0 and gr == 0:
                                        pe.wait_ge(self.moved.sem, self.moved.at(i, -1))
                                        pe.wait_ge(self.vsum_ready.sem, self.vsum_ready.at(i, 0))
                                        pe.wait_ge(self.mT_ready.sem, self.mT_ready.at(i, 1))
                                    elif j == 0 and gr == 1:
                                        pe.wait_ge(self.mT_ready.sem, self.mT_ready.at(i, 2))
                                        if 1 in there:
                                            pe.wait_ge(self.qk_ready.sem, self.qk_ready.at(i + 1, 2))
                                    elif j == 0 and gr == 2:
                                        pe.wait_ge(self.mT_ready.sem, self.mT_ready.at(i, 3))
                                        if 1 in there:
                                            pe.wait_ge(self.v_ready.sem, self.v_ready.at(i + 1, 1))
                                        pe.wait_ge(o_read.sem, o_read.at(i, 2 - NB))
                                    elif j == 0:
                                        pe.wait_ge(self.mT_ready.sem, self.mT_ready.at(i, 4))
                                        pe.wait_ge(o_read.sem, o_read.at(i, 0))
                                    floors(i, later(d, par), 4 * gr + j)
                        for i in range(2):
                            for d, m in in_slot(s, A, GROUPS * ATOPS // 2):
                                if d in there:
                                    a_scores(g + d, later(d, par), 2 * m + i)
                            for d, k in in_slot(s, B, SLOTS):
                                if d in there:
                                    b_scores(g + d, later(d, par), k, i)
                        for d, gr in in_slot(s, TOP_T, GROUPS, STEPS):
                            if d in there:
                                i = g + d
                                pe.wait_ge(self.mT_ready.sem, self.mT_ready.at(i, gr))
                                if causal and gr:
                                    pe.wait_ge(self.floor.sem, self.floor.at(i, 4 * gr))
                                elif gr == 0:
                                    pe.wait_ge(self.v_ready.sem, self.v_ready.at(i, 1))
                                    if causal:
                                        pe.wait_ge(self.floor.sem, self.floor.at(i, 0))
                                elif gr == 2 and 1 in there:
                                    pe.wait_ge(self.v_ready.sem, self.v_ready.at(i + 1, 1))
                                elif gr == 3:
                                    pe.wait_ge(result_read.sem, result_read.at(i, 0))
                                transpose_tops(i, gr)
                        for d, _ in in_slot(s, H_T):
                            if d in there:
                                transpose_h(g + d, later(d, par))
                        for i, at in enumerate((Q, K) if causal else (Q, QS, K, KS)):
                            for d, _ in in_slot(s, at):
                                if d in there:
                                    make(g + d, i)
                        for d, _ in in_slot(s, V):
                            if d in there:
                                make_v(g + d)
                        for d, _ in in_slot(s, V_SUM):
                            if d in there and causal:
                                pe.wait_ge(result_read.sem, result_read.at(g + d, 0))
                                pe.wait_ge(self.floor.sem, self.floor.at(g + d, HEADS))
                                if 1 in there:
                                    pe.wait_ge(self.mT_ready.sem, self.mT_ready.at(g + 1, 1))
                                sum_v(g + d, later(d, par))
                        for d, _ in in_slot(s, ON_T):
                            if d in there:
                                if causal and 0 in there:
                                    pe.wait_ge(self.floor.sem, self.floor.at(g, HEADS))
                                    if 1 in there:
                                        pe.wait_ge(self.mT_ready.sem, self.mT_ready.at(g + 1, 1))
                                transpose_on(g + d)
                        for d, _ in in_slot(s, PROJECT):
                            if d in there:
                                project(g + d)
                        for i in range(2):
                            for d, e in in_slot(s, TIMES_V + i, 2 * GROUPS, 4):
                                if d in there:
                                    times_v(g + d, later(d, par), e, i)
                        for b in range(NB):
                            for d, _ in in_slot(s, O[b]):
                                if d in there:
                                    i = g + d
                                    if causal and b == 2:
                                        pe.wait_ge(self.mT_ready.sem,
                                                   self.mT_ready.at(i, GROUPS + (4 if 0 in there else 0)))
                                    elif causal and b == 0:
                                        pe.wait_ge(self.mT_ready.sem,
                                                   self.mT_ready.at(i, GROUPS + (3 if 0 in there else 0)))
                                        if 1 in there:
                                            pe.wait_ge(self.v_ready.sem, self.v_ready.at(i + 2, 1))
                                        pe.wait_ge(self.vsum_ready.sem, self.vsum_ready.at(i, 1))
                                    elif b == 0:
                                        pe.wait_ge(self.mT_ready.sem,
                                                   self.mT_ready.at(i, GROUPS + (3 if 0 in there else 0)))
                                    transpose_o(i, later(d, par), b)

                modulo_pipeline(pe, first, body)


NUMBERS = ["1", "minus_1", "1e-6", "1e-8", "keys"] + [f"masked_{b}" for b in range(NB)]
NUMBER_VALUES = [1, -1, 1e-6, 1e-8, SEQ] + [SEQ - P * (b + 1) for b in range(NB)]
MOE_ARRAYS = {"lower": [P, NB * EXPERTS, EXPERTS], "wg": [P, EXPERTS], "wup": [P, MOE_UP_COLS],
              "wdm": [P, 1 + EXPERTS, DIM], "wdt": [P, MOE_PASSES, DIM]}
CAUSAL_ARRAYS = {"causal_wqkv": [P, 3 * P], "causal_wproj": [P, DIM], "diag": [P, 2, P], "ones": [P, P],
                 "ones_rows": [ROWS, P], "minus_100": [P, 1], "numbers": [P, len(NUMBERS), HEADS]}
ROTARY_ARRAYS = {"rotary_wqkv": [P, 5 * P], "rotary_wproj": [P, DIM], "b_proj": [P, DIM], "rope": [P, 2, 2, SEQ],
                 "numbers": [P, len(NUMBERS), HEADS]}
LOCAL_ARRAYS = {"wqkv": [P, DEPTH, 3 * INNER], "wo": [P, DEPTH, PAIRS, DIM], "qk_scale": [P, DEPTH, 2, LD],
                "qk_scale_swapped": [P, DEPTH, 2, LD], "turn_cos": [P, NB, 2, LD], "turn_sin": [P, NB, 2, LD],
                "band": [P, 2, 2 * BAND], "w1": [P, DEPTH, 2 * HID], "w2": [P, DEPTH, 3, DIM], "b1": [P, DEPTH, 6],
                "b2": [P, DEPTH, DIM], "ln_g": [P, DEPTH], "ln_b": [P, DEPTH]}
STAGES = ["moe", "causal", "moe", "local", "rotary", "local"]


class Loader:

    def __init__(self, ctx, nc, ins):
        self.nc, self.ins, self.count = nc, ins, 0
        self.sem = ctx.enter_context(nc.semaphore("loaded"))

    def load(self, ctx, name, arrays, sp):
        W = {}
        for n, s in arrays.items():
            W[n] = ctx.enter_context(self.nc.sbuf_tensor(f"{name}_{n}", s, F32))[tuple(slice(None) for _ in s)]
            sp.dma_start(W[n], self.ins[n]).then_inc(self.sem, 16)
            self.count += 16
        return W


def program(nc, ins, out, stages):
    with ExitStack() as ctx:
        sb = lambda n, s, dt=F32: ctx.enter_context(nc.sbuf_tensor(n, s, dt))
        X = sb("X", [P, NSEQ * NB, DIM])
        common = {"ident16": sb("ident16", [P, P], BF16)[:, :]}
        loader = Loader(ctx, nc, ins)
        stored = ctx.enter_context(nc.semaphore("stored"))
        made = ctx.enter_context(nc.semaphore("made"))
        with nc.Block() as block:
            @block.sync
            def _(sp):
                common.update(loader.load(ctx, "common", {"ident": [P, P], "minus_half": [P, 64]}, sp))
                x = ins["x"].rearrange("(n p) d -> p n d", p=P)
                for s in range(0, NSEQ, 4):
                    sp.dma_start(X[:, s * NB:(s + 4) * NB, :], x[:, s * NB:(s + 4) * NB, :]).then_inc(loader.sem, 16)
                    loader.count += 16
                sp.wait_ge(loader.sem, loader.count)
        with nc.Block() as block:
            @block.vector
            def _(v):
                v.tensor_copy(common["ident16"], common["ident"]).then_inc(made, 1)
                v.wait_ge(made, 1)
        kinds = {"moe": Moe(ctx, nc), "ffn": Geglu(ctx, nc), "attention": LocalAttention(ctx, nc),
                 "causal": GlobalAttention(ctx, nc, "causal"), "rotary": GlobalAttention(ctx, nc, "rotary")}
        arrays = {"moe": MOE_ARRAYS, "causal": CAUSAL_ARRAYS, "rotary": ROTARY_ARRAYS, "local": LOCAL_ARRAYS}
        runs = {}
        for number, kind in enumerate(stages):
            with ExitStack() as own:
                W = dict(common)
                with nc.Block() as block:
                    @block.sync
                    def _(sp):
                        W.update(loader.load(own, f"stage{number}", arrays[kind], sp))
                        sp.wait_ge(loader.sem, loader.count)
                run = runs.setdefault(kind, 0)
                runs[kind] += 1
                if kind in ("causal", "rotary"):
                    kinds[kind].emit(nc, 0, X, W)
                elif kind == "moe":
                    kinds["moe"].emit(nc, run, X, W)
                else:
                    local_tables(nc, own, W, made, 1 + run * (1 + 2 * DEPTH), number)
                    Y = own.enter_context(nc.sbuf_tensor(f"stage{number}_Y", [P, NSEQ * NB, DIM], F32))
                    for layer in range(DEPTH):
                        kinds["attention"].emit(nc, DEPTH * run + layer, X, Y, W, layer)
                        kinds["ffn"].emit(nc, DEPTH * run + layer, X, Y, W, layer, layer == DEPTH - 1)
        with nc.Block() as block:
            @block.sync
            def _(sp):
                y = out.rearrange("(n p) d -> p n d", p=P)
                for s in range(0, NSEQ, 4):
                    sp.dma_start(y[:, s * NB:(s + 4) * NB, :], X[:, s * NB:(s + 4) * NB, :]).then_inc(stored, 16)
                sp.wait_ge(stored, 16 * (NSEQ // 4))


def local_tables(nc, ctx, W, made, count, number):
    sb = lambda n, s, dt=F32: ctx.enter_context(nc.sbuf_tensor(f"stage{number}_{n}", s, dt))
    band16 = sb("band16", [P, 2, 2 * BAND], BF16)
    turn = {n: sb(n + "_scaled", [P, DEPTH, NB, 2, LD]) for n in ("turn_cos", "turn_sin")}
    with nc.Block() as block:
        @block.vector
        def _(v):
            v.tensor_copy(band16[:, :, :], W["band"]).then_inc(made, 1)
            for name, scale in (("turn_cos", "qk_scale"), ("turn_sin", "qk_scale_swapped")):
                for l in range(DEPTH):
                    v.tensor_tensor(turn[name][:, l, :, :, :], W[name],
                                    W[scale][:, l, :, :].unsqueeze(1).broadcast_to([P, NB, 2, LD]), ALU.mult)\
                        .then_inc(made, 1)
            v.wait_ge(made, count + 1 + 2 * DEPTH)
    W["band"] = band16[:, :, :]
    for name, t in turn.items():
        W[name] = t[:, :, :, :, :]


def constants():
    e = np.arange(EXPERTS)
    lower = (e[None, :] < e[:, None]).astype(np.float32)
    half = np.arange(0, LD, 2, dtype=np.float32)
    pos = np.arange(SEQ, dtype=np.float32)
    freqs = pos[:, None] * (1.0 / 10000.0 ** (half / LD)).astype(np.float32)[None, :]
    power = (pos - SEQ // 2) / float(WINDOW // 2)
    scale = ((half + 0.4 * LD) / (1.4 * LD))[None, :] ** power[:, None]
    two = lambda t: np.concatenate([t, t], 1)
    cos, scale = two(np.cos(freqs)), two(scale)
    sin = np.concatenate([-np.sin(freqs), np.sin(freqs)], 1)
    blocks = lambda q, k: np.ascontiguousarray(
        np.stack([8.0 * q, k], 1).reshape(NB, P, 2, LD).transpose(1, 0, 2, 3), dtype=np.float32)
    lag = np.arange(P)[:, None] + WINDOW - np.arange(BAND)[None, :]
    seen = (lag >= 0) & (lag <= WINDOW)
    band = np.stack([np.where(seen & (np.arange(BAND) >= WINDOW), 0, -1e30), np.where(seen, 0, -1e30)], 1)
    theta = (1.0 / 10000.0 ** (np.arange(0, HD, 2, dtype=np.float32) / HD) * 3.0).astype(np.float32)
    ang = pos[:, None] * theta[None, :]
    by_d = lambda t: np.repeat(t.T, HEADS, 0)
    rc = by_d(np.repeat(np.cos(ang), 2, 1))
    rs = by_d(np.stack([-np.sin(ang), np.sin(ang)], 2).reshape(SEQ, HD))
    f = np.float32(HD ** -0.5)
    later = np.where(np.arange(P)[None, :] > np.arange(P)[:, None], -1e30, 0)
    ones_rows = np.zeros((ROWS, P), np.float32)
    ones_rows[PAIR_ROWS:] = 1
    return {
        "rope": np.ascontiguousarray(np.stack([np.stack([rc * f, rs * f], 1), np.stack([rc, rs], 1)], 1), np.float32),
        "diag": np.ascontiguousarray(np.stack([later, later.T], 1), np.float32),
        "ones": np.ones((P, P), np.float32),
        "ones_rows": ones_rows,
        "minus_100": np.full((P, 1), -100.0, np.float32),
        "numbers": np.ascontiguousarray(np.broadcast_to(np.float32(NUMBER_VALUES)[None, :, None],
                                                        (P, len(NUMBERS), HEADS))),
        "turn_cos": blocks(cos * scale, cos / scale),
        "turn_sin": blocks(sin * scale, sin / scale),
        "band": np.ascontiguousarray(np.concatenate([band, band], 2), dtype=np.float32),
        "ident": np.eye(P, dtype=np.float32),
        "lower": np.ascontiguousarray(np.broadcast_to(np.tile(lower, (NB, 1)), (P, NB * EXPERTS, EXPERTS))),
        "minus_half": np.full((P, 64), -0.5, np.float32),
    }


def layouts(a):
    up = np.concatenate([np.asarray(a["L0_ffn_w_up"]),
                         np.concatenate([a["L0_ffn_sg_gate"], a["L0_ffn_sg_up"]], 0)[None]], 0)
    down = np.concatenate([np.asarray(a["L0_ffn_w_down"]), np.asarray(a["L0_ffn_sg_down"])[None]], 0)
    S = EXPERTS
    rows = [up[S, 0:P], up[S, HALF:HALF + P], up[S, P:HALF], up[S, HALF + P:]]
    for p in range(EXPERTS // 2):
        for e in (2 * p, 2 * p + 1):
            rows += [up[e, 0:P], up[e, HALF:HALF + P]]
        rows += [up[e, o + P:o + HALF] for o in (0, HALF) for e in (2 * p, 2 * p + 1)]
    order = [S, *range(EXPERTS)]
    tail = np.zeros((MOE_PASSES, P, DIM), np.float32)
    tail[0, 0:TAIL] = down[S, :, P:].T
    for p in range(EXPERTS // 2):
        tail[1 + p] = np.concatenate([down[2 * p, :, P:].T, down[2 * p + 1, :, P:].T], 0)
    c = np.ascontiguousarray
    f32 = lambda n: np.asarray(a["L1_ffn_" + n])

    def blocks(rows):
        out = np.zeros((P, DEPTH, 3, rows.shape[-1]), np.float32)
        for j, (r, m) in enumerate(HID_BLOCKS):
            out[0:m, :, j] = rows[:, r:r + m].transpose(1, 0, 2)
        return out

    def global_qkv(w, swapped):
        q, k = (w[:, i * DIM:(i + 1) * DIM].reshape(DIM, HEADS, HD).transpose(0, 2, 1) for i in range(2))
        pairs = [x.reshape(DIM, HD // 2, 2, HEADS)[:, :, ::-1] for x in (q, k)] if swapped else []
        return c(np.concatenate([x.reshape(DIM, DIM) for x in (q, k, *pairs)] + [w[:, 2 * DIM:]], 1))

    scales = np.stack([f32("q_scale"), f32("k_scale")], 1)
    b1 = f32("b1")[:, :, None]
    spread = lambda t: c(np.broadcast_to(t, (P, *t.shape)))
    return {
        "causal_wqkv": global_qkv(np.asarray(a["L0_attn_w_qkv"]).T, False),
        "causal_wproj": c(np.asarray(a["L0_attn_w_proj"]).T),
        "rotary_wqkv": global_qkv(np.asarray(a["L1_attn_w_qkv"]), True),
        "rotary_wproj": c(np.asarray(a["L1_attn_w_proj"])),
        "b_proj": spread(np.asarray(a["L1_attn_b_proj"])),
        "wqkv": c(f32("wqkv").transpose(1, 0, 2)),
        "wo": c(f32("wo").reshape(DEPTH, PAIRS, P, DIM).transpose(2, 0, 1, 3)),
        "qk_scale": spread(scales),
        "qk_scale_swapped": spread(np.concatenate([scales[..., LD // 2:], scales[..., :LD // 2]], -1)),
        "w1": c(f32("w1").transpose(1, 0, 2)),
        "w2": blocks(f32("w2")),
        "b1": c(np.concatenate([blocks(b1[:, :HID]), blocks(b1[:, HID:])], 2)[..., 0]),
        "b2": spread(f32("b2")),
        "ln_g": c(f32("ln_g").T),
        "ln_b": c(f32("ln_b").T),
        "x": c(np.asarray(a["L0_attn_x"]).reshape(NSEQ * SEQ, DIM)),
        "wg": c(np.asarray(a["L0_ffn_gate_w"]).T),
        "wup": c(np.concatenate(rows, 0).T),
        "wdm": c(down[order, :, 0:P].transpose(2, 0, 1)),
        "wdt": c(tail.transpose(1, 0, 2)),
    }


def kernel(**inputs):
    import concourse.bacc as bacc
    from concourse.bass_utils import run_bass_kernel_spmd

    nc = bacc.Bacc("TRN2", target_bir_lowering=False, num_devices=1)
    arrays = {**layouts(inputs), **constants()}
    ins = {n: nc.dram_tensor(n + "_in", a.shape, mybir.dt.from_np(a.dtype), kind="ExternalInput").ap()
           for n, a in arrays.items()}
    out = nc.dram_tensor("out", (NSEQ * SEQ, DIM), F32, kind="ExternalOutput").ap()
    program(nc, ins, out, STAGES)
    r = run_bass_kernel_spmd(nc, [{n + "_in": a for n, a in arrays.items()}], core_ids=[0])
    return r.results[0]["out"].reshape(NSEQ, SEQ, DIM)
```
